# Optimizing a Trainium2 kernel written in Bass

```python
import numpy as np
import jax
import jax.numpy as jnp

def _softmax(x, axis=-1):
    return jax.nn.softmax(x, axis=axis)

def _gelu(x):
    return jax.nn.gelu(x, approximate=True)

def _silu(x):
    return jax.nn.silu(x)

def _sigmoid(x):
    return jax.nn.sigmoid(x)

def _layernorm(x, axis=-1, eps=1e-05):
    m = jnp.mean(x, axis=axis, keepdims=True)
    v = jnp.var(x, axis=axis, keepdims=True)
    return (x - m) / jnp.sqrt(v + eps)

def _scatter_add(tgt, idx, src, axis=0):
    return tgt.at[idx].add(src)

def _segment_sum(src, seg, n):
    return jax.ops.segment_sum(src, seg, n)
kernel_name = 'mk_decoder_postln_d2_seqx_r4_792e1f'

def setup_inputs(seed: int=0):
    np.random.seed(seed)
    _w = jnp.asarray

    def _rec_inputs():
        import jax
        import jax.numpy as jnp
        _rk = jax.random.key(seed)
        x = -0.0003929 + 0.9999 * jax.random.normal(jax.random.fold_in(_rk, 1), (8, 256, 256), jnp.float32)
        _lenS = 256 - jax.random.randint(jax.random.fold_in(_rk, 7), (8,), 0, max(1, 256 // 4) + 1, jnp.int32)
        _lenS2 = 256 - jax.random.randint(jax.random.fold_in(_rk, 8), (8,), 0, max(1, 256 // 4) + 1, jnp.int32)
        _ctx_768P = jax.random.normal(jax.random.fold_in(_rk, 11), (8, 16, 192), jnp.float32)
        _ctx_768c = jax.random.dirichlet(jax.random.fold_in(_rk, 511), 0.3 * jnp.ones((16,), jnp.float32), (8, 256))
        _ctx_768t = jnp.einsum('bsk,bkd->bsd', _ctx_768c, _ctx_768P)
        _ctx_768t = _ctx_768t * jax.lax.rsqrt(jnp.mean(jnp.square(_ctx_768t)) + 1e-12) * 0.953939
        ctx_768 = -7.36909e-05 + 0.999899 * (_ctx_768t + 0.3 * jax.random.normal(jax.random.fold_in(_rk, 611), (8, 256, 192), jnp.float32))
        return (x, ctx_768)
    x, ctx_768 = _rec_inputs()

    def _L0_attn_setup():
        import jax, jax.numpy as jnp
        import numpy as np
        B, S, D = (8, 512, 256)

        def _forward(x, W_qkv, b_qkv, W_vconv):
            b, s, d = x.shape
            qkv = x @ W_qkv + b_qkv
            q, k, v = jnp.split(qkv, 3, axis=-1)
            scores = jnp.einsum('bid,bjd->bij', q, k) * (1.0 / np.sqrt(d))
            mask = jnp.tril(jnp.ones((s, s), bool))
            scores = jnp.where(mask, scores, -jnp.inf)
            A = jax.nn.softmax(scores, axis=-1)
            w0, w1, w2 = (W_vconv[:, 0], W_vconv[:, 1], W_vconv[:, 2])
            v_prev = jnp.pad(v, ((0, 0), (1, 0), (0, 0)))[:, :s]
            v_next = jnp.pad(v, ((0, 0), (0, 1), (0, 0)))[:, 1:]
            C = w0 * v_prev + w1 * v + w2 * v_next
            out = jnp.einsum('bij,bjc->bic', A, C)
            diagA = jnp.diagonal(A, axis1=1, axis2=2)
            out = out - diagA[:, :, None] * (w2 * v_next)
            return out
        key = jax.random.key(seed)
        k0, k1, k2, k3 = jax.random.split(key, 4)
        x = jax.random.normal(k0, (B, S, D), jnp.float32)
        W_qkv = jax.random.normal(k1, (D, 3 * D), jnp.float32) * (1.0 / np.sqrt(D))
        b_qkv = jax.random.normal(k2, (3 * D,), jnp.float32) * 0.02
        W_vconv = jax.random.normal(k3, (D, 3), jnp.float32) * 0.02
        return {'x': x, 'W_qkv': W_qkv, 'b_qkv': b_qkv, 'W_vconv': W_vconv}
    _L0_attn_all = _L0_attn_setup()
    _L0_attn_in = {k: v for k, v in _L0_attn_all.items() if k in ('W_qkv', 'b_qkv', 'W_vconv')}
    del _L0_attn_all

    def _L0_xattn_setup():
        import jax, jax.numpy as jnp
        import numpy as np
        EPS = 1e-08
        key = jax.random.key(seed)
        kv, kt, k1, k2, k3, k4 = jax.random.split(key, 6)
        B, S = (16, 256)
        VD, TD, H = (256, 192, 128)
        visual_features = jax.random.normal(kv, (B, S, VD), dtype=jnp.float32)
        text_features = jax.random.normal(kt, (B, S, TD), dtype=jnp.float32)
        Wv = jax.random.normal(k1, (H, VD), dtype=jnp.float32) * (1.0 / np.sqrt(VD))
        bv = jax.random.normal(k2, (H,), dtype=jnp.float32) * 0.01
        Wt = jax.random.normal(k3, (H, TD), dtype=jnp.float32) * (1.0 / np.sqrt(TD))
        bt = jax.random.normal(k4, (H,), dtype=jnp.float32) * 0.01
        return {'visual_features': visual_features, 'text_features': text_features, 'Wv': Wv, 'bv': bv, 'Wt': Wt, 'bt': bt}
    _L0_xattn_all = _L0_xattn_setup()
    _L0_xattn_in = {k: v for k, v in _L0_xattn_all.items() if k in ('Wv', 'bv', 'Wt', 'bt')}
    del _L0_xattn_all

    def _L0_ffn_setup():
        import jax, jax.numpy as jnp
        import numpy as np
        D_IN, D_HID = (256, 1024)

        def _ternary(key, shape):
            return jax.random.randint(key, shape, -1, 2).astype(jnp.float32)

        def _tlin(x, w, s):
            return jnp.einsum('bsi,oi->bso', x, w) * s
        key = jax.random.key(seed)
        ks = jax.random.split(key, 12)
        inv = lambda fan: 1.0 / np.sqrt(fan).astype(np.float32)
        return {'x': jax.random.normal(ks[0], (4, 512, D_IN), dtype=jnp.float32), 'w1_w': _ternary(ks[1], (D_HID, D_IN)), 'w1_s': jax.random.uniform(ks[2], (D_HID,), dtype=jnp.float32) * inv(D_IN), 'w2_w': _ternary(ks[3], (D_HID, D_IN)), 'w2_s': jax.random.uniform(ks[4], (D_HID,), dtype=jnp.float32) * inv(D_IN), 'h1_w': _ternary(ks[5], (D_HID, D_HID)), 'h1_s': jax.random.uniform(ks[6], (D_HID,), dtype=jnp.float32) * inv(D_HID), 'h2_w': _ternary(ks[7], (D_HID, D_HID)), 'h2_s': jax.random.uniform(ks[8], (D_HID,), dtype=jnp.float32) * inv(D_HID), 'w3_w': _ternary(ks[9], (D_IN, D_HID)), 'w3_s': jax.random.uniform(ks[10], (D_IN,), dtype=jnp.float32) * inv(D_HID)}
    _L0_ffn_all = _L0_ffn_setup()
    _L0_ffn_in = {k: v for k, v in _L0_ffn_all.items() if k in ('w1_w', 'w1_s', 'w2_w', 'w2_s', 'h1_w', 'h1_s', 'h2_w', 'h2_s', 'w3_w', 'w3_s')}
    del _L0_ffn_all

    def _L1_attn_setup():
        import jax, jax.numpy as jnp
        import numpy as np
        B, T, C = (2, 1024, 256)
        H, M, CHUNK = (16, 64, 128)
        D = C // H
        DELTA = 1e-06
        key = jax.random.key(seed)
        ks = jax.random.split(key, 4)
        x = jax.random.normal(ks[0], (B, T, C), dtype=jnp.float32)
        Wqkv = jax.random.normal(ks[1], (3 * C, C), dtype=jnp.float32) * 0.02
        bqkv = jnp.zeros((3 * C,), dtype=jnp.float32)
        Wout = jax.random.normal(ks[2], (C, C), dtype=jnp.float32) * 0.02
        bout = jnp.zeros((C,), dtype=jnp.float32)
        proj = jax.random.normal(ks[3], (H, D, M), dtype=jnp.float32) / np.sqrt(D)
        return {'x': x, 'Wqkv': Wqkv, 'bqkv': bqkv, 'Wout': Wout, 'bout': bout, 'proj': proj}
    _L1_attn_all = _L1_attn_setup()
    _L1_attn_in = {k: v for k, v in _L1_attn_all.items() if k in ('Wqkv', 'bqkv', 'Wout', 'bout', 'proj')}
    del _L1_attn_all

    def _L1_xattn_setup():
        import jax, jax.numpy as jnp
        import numpy as np
        NUM_HEADS = 16
        CLAMP = 10000.0
        key = jax.random.key(seed)
        ks = jax.random.split(key, 8)
        B, Nq, Nkv, Cq, Ckv = (4, 512, 512, 256, 192)
        s_q = 1.0 / np.sqrt(Cq)
        s_kv = 1.0 / np.sqrt(Ckv)
        return {'query': jax.random.normal(ks[0], (B, Nq, Cq), jnp.float32), 'key_value': jax.random.normal(ks[1], (B, Nkv, Ckv), jnp.float32), 'Wq': jax.random.normal(ks[2], (Cq, Cq), jnp.float32) * s_q, 'bq': jnp.zeros((Cq,), jnp.float32), 'Wk': jax.random.normal(ks[3], (Ckv, Cq), jnp.float32) * s_kv, 'bk': jnp.zeros((Cq,), jnp.float32), 'Wv': jax.random.normal(ks[4], (Ckv, Cq), jnp.float32) * s_kv, 'bv': jnp.zeros((Cq,), jnp.float32), 'Wo': jax.random.normal(ks[5], (Cq, Cq), jnp.float32) * s_q, 'bo': jnp.zeros((Cq,), jnp.float32)}
    _L1_xattn_all = _L1_xattn_setup()
    _L1_xattn_in = {k: v for k, v in _L1_xattn_all.items() if k in ('Wq', 'bq', 'Wk', 'bk', 'Wv', 'bv', 'Wo', 'bo')}
    del _L1_xattn_all

    def _L1_ffn_setup():
        import jax, jax.numpy as jnp
        import numpy as np
        TOP_K = 2
        key = jax.random.key(seed)
        ks = jax.random.split(key, 6)
        B, S, D, F, E = (2, 512, 256, 1024, 8)
        sd = 1.0 / np.sqrt(D)
        sf = 1.0 / np.sqrt(F)
        return {'x': jax.random.normal(ks[0], (B, S, D), jnp.float32), 'gate_w': jax.random.normal(ks[1], (D, E), jnp.float32) * sd, 'w1': jax.random.normal(ks[2], (E, D, F), jnp.float32) * sd, 'b1': jax.random.normal(ks[3], (E, F), jnp.float32) * 0.01, 'w2': jax.random.normal(ks[4], (E, F, D), jnp.float32) * sf, 'b2': jax.random.normal(ks[5], (E, D), jnp.float32) * 0.01}
    _L1_ffn_all = _L1_ffn_setup()
    _L1_ffn_in = {k: v for k, v in _L1_ffn_all.items() if k in ('gate_w', 'w1', 'b1', 'w2', 'b2')}
    del _L1_ffn_all
    return {'x': x, 'ctx_768': ctx_768, 'L0_attn_W_qkv': _L0_attn_in['W_qkv'], 'L0_attn_b_qkv': _L0_attn_in['b_qkv'], 'L0_attn_W_vconv': _L0_attn_in['W_vconv'], 'L0_xattn_Wv': _L0_xattn_in['Wv'], 'L0_xattn_bv': _L0_xattn_in['bv'], 'L0_xattn_Wt': _L0_xattn_in['Wt'], 'L0_xattn_bt': _L0_xattn_in['bt'], 'L0_ffn_w1_w': _L0_ffn_in['w1_w'], 'L0_ffn_w1_s': _L0_ffn_in['w1_s'], 'L0_ffn_w2_w': _L0_ffn_in['w2_w'], 'L0_ffn_w2_s': _L0_ffn_in['w2_s'], 'L0_ffn_h1_w': _L0_ffn_in['h1_w'], 'L0_ffn_h1_s': _L0_ffn_in['h1_s'], 'L0_ffn_h2_w': _L0_ffn_in['h2_w'], 'L0_ffn_h2_s': _L0_ffn_in['h2_s'], 'L0_ffn_w3_w': _L0_ffn_in['w3_w'], 'L0_ffn_w3_s': _L0_ffn_in['w3_s'], 'L1_attn_Wqkv': _L1_attn_in['Wqkv'], 'L1_attn_bqkv': _L1_attn_in['bqkv'], 'L1_attn_Wout': _L1_attn_in['Wout'], 'L1_attn_bout': _L1_attn_in['bout'], 'L1_attn_proj': _L1_attn_in['proj'], 'L1_xattn_Wq': _L1_xattn_in['Wq'], 'L1_xattn_bq': _L1_xattn_in['bq'], 'L1_xattn_Wk': _L1_xattn_in['Wk'], 'L1_xattn_bk': _L1_xattn_in['bk'], 'L1_xattn_Wv': _L1_xattn_in['Wv'], 'L1_xattn_bv': _L1_xattn_in['bv'], 'L1_xattn_Wo': _L1_xattn_in['Wo'], 'L1_xattn_bo': _L1_xattn_in['bo'], 'L1_ffn_gate_w': _L1_ffn_in['gate_w'], 'L1_ffn_w1': _L1_ffn_in['w1'], 'L1_ffn_b1': _L1_ffn_in['b1'], 'L1_ffn_w2': _L1_ffn_in['w2'], 'L1_ffn_b2': _L1_ffn_in['b2']}

def reference(x, ctx_768, L0_attn_W_qkv, L0_attn_b_qkv, L0_attn_W_vconv, L0_xattn_Wv, L0_xattn_bv, L0_xattn_Wt, L0_xattn_bt, L0_ffn_w1_w, L0_ffn_w1_s, L0_ffn_w2_w, L0_ffn_w2_s, L0_ffn_h1_w, L0_ffn_h1_s, L0_ffn_h2_w, L0_ffn_h2_s, L0_ffn_w3_w, L0_ffn_w3_s, L1_attn_Wqkv, L1_attn_bqkv, L1_attn_Wout, L1_attn_bout, L1_attn_proj, L1_xattn_Wq, L1_xattn_bq, L1_xattn_Wk, L1_xattn_bk, L1_xattn_Wv, L1_xattn_bv, L1_xattn_Wo, L1_xattn_bo, L1_ffn_gate_w, L1_ffn_w1, L1_ffn_b1, L1_ffn_w2, L1_ffn_b2):
    import jax
    import jax.numpy as jnp

    def _L0_attn_ref(x, W_qkv, b_qkv, W_vconv):
        import jax, jax.numpy as jnp
        import numpy as np
        B, S, D = (8, 512, 256)

        def _forward(x, W_qkv, b_qkv, W_vconv):
            b, s, d = x.shape
            qkv = x @ W_qkv + b_qkv
            q, k, v = jnp.split(qkv, 3, axis=-1)
            scores = jnp.einsum('bid,bjd->bij', q, k) * (1.0 / np.sqrt(d))
            mask = jnp.tril(jnp.ones((s, s), bool))
            scores = jnp.where(mask, scores, -jnp.inf)
            A = jax.nn.softmax(scores, axis=-1)
            w0, w1, w2 = (W_vconv[:, 0], W_vconv[:, 1], W_vconv[:, 2])
            v_prev = jnp.pad(v, ((0, 0), (1, 0), (0, 0)))[:, :s]
            v_next = jnp.pad(v, ((0, 0), (0, 1), (0, 0)))[:, 1:]
            C = w0 * v_prev + w1 * v + w2 * v_next
            out = jnp.einsum('bij,bjc->bic', A, C)
            diagA = jnp.diagonal(A, axis1=1, axis2=2)
            out = out - diagA[:, :, None] * (w2 * v_next)
            return out
        return _forward(x, W_qkv, b_qkv, W_vconv)

    def _L0_xattn_ref(visual_features, text_features, Wv, bv, Wt, bt):
        import jax, jax.numpy as jnp
        import numpy as np
        EPS = 1e-08
        v = jnp.einsum('bsd,hd->bsh', visual_features, Wv) + bv
        t = jnp.einsum('bsd,hd->bsh', text_features, Wt) + bt
        dots = jnp.einsum('bih,bjh->bij', v, t)
        vn = jnp.linalg.norm(v, axis=-1)
        tn = jnp.linalg.norm(t, axis=-1)
        denom = jnp.maximum(vn[:, :, None] * tn[:, None, :], EPS)
        return dots / denom

    def _L0_ffn_ref(x, w1_w, w1_s, w2_w, w2_s, h1_w, h1_s, h2_w, h2_s, w3_w, w3_s):
        import jax, jax.numpy as jnp
        import numpy as np
        D_IN, D_HID = (256, 1024)

        def _ternary(key, shape):
            return jax.random.randint(key, shape, -1, 2).astype(jnp.float32)

        def _tlin(x, w, s):
            return jnp.einsum('bsi,oi->bso', x, w) * s
        h = jax.nn.silu(_tlin(x, w1_w, w1_s)) * _tlin(x, w2_w, w2_s)
        h = jax.nn.gelu(_tlin(h, h1_w, h1_s), approximate=False)
        h = jax.nn.gelu(_tlin(h, h2_w, h2_s), approximate=False)
        return _tlin(h, w3_w, w3_s)

    def _L1_attn_ref(x, Wqkv, bqkv, Wout, bout, proj):
        import jax, jax.numpy as jnp
        import numpy as np
        B, T, C = (2, 1024, 256)
        H, M, CHUNK = (16, 64, 128)
        D = C // H
        DELTA = 1e-06
        b, t, c = x.shape
        qkv = x @ Wqkv.T + bqkv
        q, k, v = jnp.split(qkv, 3, axis=-1)

        def to_heads(z):
            return z.reshape(b, t, H, D).transpose(0, 2, 1, 3).astype(jnp.float32)
        q, k, v = (to_heads(q), to_heads(k), to_heads(v))
        nch = t // CHUNK

        def to_chunks(z):
            return z.reshape(b, H, nch, CHUNK, D).transpose(2, 0, 1, 3, 4)
        qc, kc, vc = (to_chunks(q), to_chunks(k), to_chunks(v))
        mask = jnp.tril(jnp.ones((CHUNK, CHUNK), dtype=jnp.float32))

        def step(carry, inp):
            kv_state, k_state = carry
            q_ch, k_ch, v_ch = inp
            qp = jax.nn.relu(jnp.einsum('bhtd,hdm->bhtm', q_ch, proj))
            kp = jax.nn.relu(jnp.einsum('bhtd,hdm->bhtm', k_ch, proj))
            ctx_hist = jnp.einsum('bhtm,bhmd->bhtd', qp, kv_state)
            norm_hist = jnp.einsum('bhtm,bhm->bht', qp, k_state)
            aw = jnp.einsum('bhtm,bhsm->bhts', qp, kp) * mask
            ctx_intra = jnp.einsum('bhts,bhsd->bhtd', aw, v_ch)
            norm_intra = aw.sum(-1)
            out = (ctx_hist + ctx_intra) / (norm_hist + norm_intra + DELTA)[..., None]
            new_kv = kv_state + jnp.einsum('bhtm,bhtd->bhmd', kp, v_ch)
            new_k = k_state + kp.sum(2)
            return ((new_kv, new_k), out)
        carry0 = (jnp.zeros((b, H, M, D), jnp.float32), jnp.zeros((b, H, M), jnp.float32))
        _, outs = jax.lax.scan(step, carry0, (qc, kc, vc))
        out = outs.transpose(1, 2, 0, 3, 4).reshape(b, H, t, D)
        out = out.transpose(0, 2, 1, 3).reshape(b, t, c)
        return out @ Wout.T + bout

    def _L1_xattn_ref(query, key_value, Wq, bq, Wk, bk, Wv, bv, Wo, bo):
        import jax, jax.numpy as jnp
        import numpy as np
        NUM_HEADS = 16
        CLAMP = 10000.0
        B, Nq, Cq = query.shape
        Nkv = key_value.shape[1]
        H = NUM_HEADS
        D = Cq // H
        scale = D ** (-0.5)
        q = (query @ Wq + bq).reshape(B, Nq, H, D).transpose(0, 2, 1, 3)
        k = (key_value @ Wk + bk).reshape(B, Nkv, H, D).transpose(0, 2, 1, 3)
        v = (key_value @ Wv + bv).reshape(B, Nkv, H, D).transpose(0, 2, 1, 3)
        attn = jnp.einsum('bhqd,bhkd->bhqk', q, k) * scale
        attn = jnp.clip(attn, -CLAMP, CLAMP)
        attn = jax.nn.softmax(attn, axis=-1)
        attn = jnp.where(jnp.any(jnp.isnan(attn)), jnp.asarray(1.0 / Nkv, attn.dtype), attn)
        x = jnp.einsum('bhqk,bhkd->bqhd', attn, v).reshape(B, Nq, Cq)
        return x @ Wo + bo

    def _L1_ffn_ref(x, gate_w, w1, b1, w2, b2):
        import jax, jax.numpy as jnp
        import numpy as np
        TOP_K = 2
        B, S, D = x.shape
        T = B * S
        xf = x.reshape(T, D)
        gate_scores = jax.nn.softmax(xf @ gate_w, axis=-1)
        topk_scores, topk_idx = jax.lax.top_k(gate_scores, TOP_K)
        topk_scores = topk_scores / jnp.sum(topk_scores, axis=-1, keepdims=True)
        h = jax.nn.gelu(jnp.einsum('td,edf->etf', xf, w1) + b1[:, None, :], approximate=False)
        y = jnp.einsum('etf,efd->etd', h, w2) + b2[:, None, :]
        tok = jnp.arange(T)
        y_sel = y[topk_idx.T, tok[None, :]]
        out = jnp.einsum('kt,ktd->td', topk_scores.T, y_sel)
        return out.reshape(B, S, D)
    x = _layernorm(x + _L0_attn_ref(x, L0_attn_W_qkv, L0_attn_b_qkv, L0_attn_W_vconv), axis=-1)
    x = _layernorm(x + _L0_xattn_ref(x, ctx_768, L0_xattn_Wv, L0_xattn_bv, L0_xattn_Wt, L0_xattn_bt), axis=-1)
    x = _layernorm(x + _L0_ffn_ref(x, L0_ffn_w1_w, L0_ffn_w1_s, L0_ffn_w2_w, L0_ffn_w2_s, L0_ffn_h1_w, L0_ffn_h1_s, L0_ffn_h2_w, L0_ffn_h2_s, L0_ffn_w3_w, L0_ffn_w3_s), axis=-1)
    x = _layernorm(x + _L1_attn_ref(x, L1_attn_Wqkv, L1_attn_bqkv, L1_attn_Wout, L1_attn_bout, L1_attn_proj), axis=-1)
    x = _layernorm(x + _L1_xattn_ref(x, ctx_768, L1_xattn_Wq, L1_xattn_bq, L1_xattn_Wk, L1_xattn_bk, L1_xattn_Wv, L1_xattn_bv, L1_xattn_Wo, L1_xattn_bo), axis=-1)
    x = _layernorm(x + _L1_ffn_ref(x, L1_ffn_gate_w, L1_ffn_w1, L1_ffn_b1, L1_ffn_w2, L1_ffn_b2), axis=-1)
    return x

_drawn_inputs = setup_inputs


def setup_inputs(seed=0):
    import zlib

    import numpy as np

    out = dict(_drawn_inputs(seed))
    spreads = {'L1_attn_bqkv': (0.0, 0.1),
     'L1_attn_bout': (0.0, 0.1),
     'L1_xattn_bq': (0.0, 0.1),
     'L1_xattn_bk': (0.0, 2.0),
     'L1_xattn_bv': (0.0, 0.1),
     'L1_xattn_bo': (0.0, 0.1)}
    factors = {'L0_attn_W_qkv': 2.903,
     'L0_attn_b_qkv': 7.923,
     'L0_attn_W_vconv': 2.915,
     'L0_xattn_bv': 6.342,
     'L0_xattn_bt': 46.764,
     'L0_ffn_w1_w': 4.355,
     'L0_ffn_w1_s': 4.209,
     'L0_ffn_w2_w': 3.453,
     'L0_ffn_w2_s': 6.112,
     'L0_ffn_h1_w': 4.599,
     'L0_ffn_h1_s': 6.384,
     'L0_ffn_h2_w': 3.629,
     'L0_ffn_h2_s': 8.0,
     'L0_ffn_w3_w': 3.607,
     'L0_ffn_w3_s': 5.764,
     'L1_attn_proj': 13.853,
     'L1_ffn_b1': 8.0,
     'L1_ffn_b2': 8.0}
    for name, (base, spread) in spreads.items():
        noise = np.random.default_rng([zlib.crc32(name.encode()), seed]).standard_normal(out[name].shape)
        drawn = base * np.exp(spread * noise) if base else spread * noise
        out[name] = jnp.asarray(drawn.astype(out[name].dtype))
    for name, factor in factors.items():
        out[name] = (out[name] * factor).astype(out[name].dtype)
    return out
```

```python
from contextlib import ExitStack

import numpy as np

import concourse.bass as bass
from concourse import mybir

F32 = mybir.dt.float32
F32R = mybir.dt.float32r
U32 = mybir.dt.uint32
ALU = mybir.AluOpType
ACT = mybir.ActivationFunctionType
AX = mybir.AxisListType

P = 128
B, S, D = 8, 256, 256
DC = 192
TT = S // P
NT = B * TT
KC = D // P
CK = DC // 2
HID = 1024
FC = HID // P
NH, DH, M = 16, 16, 64
NE = 8
SB = 512
NSB = B * S // SB
BPS = SB // S
EPS_LN = 1e-5
DELTA = 1e-6
CLAMP = 10000.0
MASKED = -3.0e38
VW = 34
VH = 3
NVT = -(-NH // VH)
CW = 1024


class Engine:

    def __init__(self, sem):
        self.sem, self.count, self.queue = sem, 0, []

    def do(self, instruction, after=(), signal=None):
        if signal is None:
            self.count += 1
            signal = (self.sem, 1, self.count)
        self.queue.append((list(after), instruction, signal))
        return (signal[0], signal[2])

    def quiet(self, instruction, after=()):
        self.queue.append((list(after), instruction, None))

    def last(self):
        return (self.sem, self.count)

    def play(self, eng):
        seen = {}
        for after, instruction, signal in self.queue:
            for sem, value in after:
                if value > seen.get(id(sem), 0):
                    eng.wait_ge(sem, value)
                    seen[id(sem)] = value
            made = instruction(eng)
            if signal is not None:
                made.then_inc(signal[0], signal[1])


class Turns:

    def __init__(self, buffers, after=()):
        self.free = [(b, list(after)) for b in buffers]

    def take(self):
        return self.free.pop(0)

    def give(self, buffer, readers):
        self.free.append((buffer, list(readers)))


def build(nc, a, out):
    ctx = ExitStack()
    early = ExitStack()
    late = ExitStack()
    with ctx:
        def sem(name):
            return ctx.enter_context(nc.semaphore(name))

        def sb(name, shape, dt=F32, scope=ctx, side="left"):
            return scope.enter_context(nc.sbuf_tensor(name, shape, dt, side=side))

        pe, act, dve, pool = (Engine(sem(f"s_{n}")) for n in ("pe", "act", "dve", "pool"))
        sp = Engine(None)
        out_sem = sem("s_out")
        banks = Turns([ctx.enter_context(nc.psum_tensor(f"bank{i}", [P, 512], F32)) for i in range(8)])

        loads = {}

        def load(name, dst, src, after=()):
            if name not in loads:
                loads[name] = [sem(f"l_{name}"), 0]
            loads[name][1] += 16
            return sp.do(lambda e: e.dma_start(dst, src), after, (loads[name][0], 16, loads[name][1]))

        def matmuls(terms, after=()):
            n = len(terms)
            for i, (o, st, mv) in enumerate(terms):
                def mm(e, o=o, st=st, mv=mv, i=i):
                    return e.matmul(o, st, mv, start=(i == 0), stop=(i == n - 1))
                if i < n - 1:
                    pe.quiet(mm, after if i == 0 else ())
                else:
                    tok = pe.do(mm, after if i == 0 else ())
            return tok

        def product(o, pairs, after=()):
            terms = []
            for (sh, sl), (mh, ml) in pairs:
                terms += [(o, sl, mh), (o, sh, ml), (o, sh, mh)]
            return matmuls(terms, after)

        def transposes(bank, parts, after=()):
            for i, (dst, src) in enumerate(parts):
                n = src.shape[0]
                fn = lambda e, dst=dst, src=src, n=n: e.transpose(dst, src, ident[0:n, 0:n])
                if i < len(parts) - 1:
                    pe.quiet(fn, after if i == 0 else ())
                else:
                    tok = pe.do(fn, after if i == 0 else ())
            return tok

        def act_do(o, i, func, after=(), **kw):
            return act.do(lambda e: e.activation(o, i, func, **kw), after)

        def tt(eng, o, x, y, op, after=()):
            return eng.do(lambda e: e.tensor_tensor(o, x, y, op), after)

        def ts(eng, o, x, s1, s2, op0, op1=None, after=()):
            if op1 is None:
                return eng.do(lambda e: e.tensor_scalar(o, x, s1, s2, op0), after)
            return eng.do(lambda e: e.tensor_scalar(o, x, s1, s2, op0, op1), after)

        def stt(o, x, s, y, op0, op1, after=(), **kw):
            return dve.do(lambda e: e.scalar_tensor_tensor(out=o, in0=x, scalar=s, in1=y, op0=op0, op1=op1, **kw),
                          after)

        def copy(eng, o, i, after=()):
            return eng.do(lambda e: e.tensor_copy(o, i), after)

        def f(ap):
            return ap.bitcast(F32)

        def split_bank(hi, lo, bank_ap, after):
            t_hi = act_do(hi, bank_ap, ACT.Identity, after)
            t_lo = tt(dve, lo, bank_ap, f(hi), ALU.subtract, [*after, t_hi])
            return [t_hi, t_lo]

        def split_biased(parts, after):
            for hi, lo, ps, bias in parts:
                t_hi = act_do(hi, ps, ACT.Identity, after, bias=bias)
            for hi, lo, ps, bias in parts:
                t_lo = stt(lo, ps, bias, f(hi), ALU.add, ALU.subtract, [*after, t_hi])
            return [t_hi, t_lo]

        def split_dve(hi, lo, x, after):
            t_hi = copy(dve, hi, x, after)
            t_lo = tt(dve, lo, x, f(hi), ALU.subtract, [t_hi])
            return [t_hi, t_lo]

        def split_pool(hi, lo, x, after):
            t_hi = ts(pool, hi, x, 1.0, 0.0, ALU.mult, ALU.add, after=after)
            t_lo = tt(pool, lo, x, f(hi), ALU.subtract, [t_hi])
            return [t_hi, t_lo]

        def fence():
            return [x.last() for x in (pe, act, dve, pool)]

        x_tok = sb("x_tok", [P, NT, D])
        xt_hi = sb("xt_hi", [P, KC, B * S], F32R)
        xt_lo = sb("xt_lo", [P, KC, B * S], F32R)
        ident = sb("ident", [P, P])
        ln_stats = sb("ln_stats", [P, 2, TT, 6])
        ln_mv = sb("ln_mv", [P, 2, TT, 2])
        ln_rstd = sb("ln_rstd", [P, 2, TT])
        minus_half = sb("minus_half", [P, 4])
        r_bufs = Turns([sb(f"resid{i}", [P, TT, D]) for i in range(3)])
        mask_a = sb("mask_a", [P, 3 * P])
        ones = sb("ones", [P, P])
        ctx_raw = Turns([(i, sb(f"ctx_raw{i}", [CK, 2, S])) for i in range(2)])
        ctx_t = Turns([[sb(f"ctx_{n}{i}", [CK, 2, S], F32R) for n in ("hi", "lo")] for i in range(2)])
        gw_raw = sb("gw_raw", [P, KC, NE])
        gates = sb("gates", [P, NT, NE])
        b2_sb = sb("b2", [NE, D])
        iota8 = sb("iota8", [P, NE])

        def xt(buf, b, c):
            return buf[:, c, b * S:(b + 1) * S]

        def xt_tile(b, t):
            c0 = b * S + t * P
            return [(xt_hi[:, c, c0:c0 + P], xt_lo[:, c, c0:c0 + P]) for c in range(KC)]

        x_ready = [None] * B
        xt_ready = [None] * B
        ln_turn = [0]

        def layernorm(b, r, r_ready, xt_readers, last=False):
            i = ln_turn[0] % 2
            ln_turn[0] += 1
            for t in range(TT):
                t_st = dve.do(lambda e, t=t: e.bn_stats(ln_stats[:, i, t, :], r[:, t, :]), r_ready if t == 0 else ())
            for t in range(TT):
                t_mv = dve.do(lambda e, t=t: e.bn_aggr(ln_mv[:, i, t, :], ln_stats[:, i, t, :]), [t_st])
            t_ve = ts(dve, ln_rstd[:, i, :], ln_mv[:, i, :, 1], EPS_LN, None, ALU.add, after=[t_mv])
            t_rs = tt(pool, ln_rstd[:, i, :], ln_rstd[:, i, :], minus_half[:, 0:TT], ALU.pow, [t_ve, t_const])
            yield
            for t in range(TT):
                t_x = ts(dve, x_tok[:, b * TT + t, :], r[:, t, :], ln_mv[:, i, t, 0:1], ln_rstd[:, i, t:t + 1],
                         ALU.subtract, ALU.mult, after=[t_rs])
            x_ready[b] = [t_x]
            if last:
                return
            r_bufs.give(r, [t_x])
            yield
            bank, free = banks.take()
            t_tr = transposes(bank, [(bank[:, c * S + t * P:c * S + (t + 1) * P],
                                      x_tok[:, b * TT + t, c * P:(c + 1) * P])
                                     for c in range(KC) for t in range(TT)], [t_x, t_const, *free])
            hi = xt_hi[:, :, b * S:(b + 1) * S]
            lo = xt_lo[:, :, b * S:(b + 1) * S]
            done = split_bank(hi, lo, bank[:, :].rearrange("p (c t) -> p c t", c=KC), [t_tr, *xt_readers])
            xt_ready[b] = done
            banks.give(bank, done)

        staging_t = Turns([(i, sb(f"staging{i}", [P, KC * 3 * D])) for i in range(2)])

        def weights(split, hi, lo, source, after=()):
            (i, raw), free = staging_t.take()
            n = int(np.prod(source.shape[1:]))
            raw_view = raw[0:source.shape[0], 0:n].rearrange("p (a b) -> p a b", a=source.shape[1])
            t_l = load(f"staging{i}", raw_view, source, free)
            toks = split(hi, lo, raw_view, [t_l, *after])
            staging_t.give((i, raw), toks)
            return toks

        plan = []

        def at(round_, gen):
            plan.append((round_, len(plan), gen))

        t_ident = load("ident", ident[:, :], a["ident"])
        t_mask_a = load("mask_a", mask_a[:, :], a["mask_a"])
        t_const = pool.do(lambda e: e.memset(minus_half[:, :], -0.5))
        t_const_ident = t_ident

        xraw = Turns([sb(f"xraw{i}", [P, KC, S], F32, early) for i in range(2)])
        wqkv = [sb(f"wqkv_{n}", [P, KC, 3 * D], F32R, early) for n in ("hi", "lo")]
        bqkv = sb("bqkv", [P, 6], F32, early)
        wconv = sb("wconv", [P, KC, 3], F32, early)
        t_bc = [load("a_bias", bqkv[:, :], a["A_b"]), load("a_conv", wconv[:, :, :], a["A_wconv"])]

        def load_x(b):
            buf, free = xraw.take()
            t_l = load(f"xT{b % 2}", buf[:, :, :], a["xT"][:, :, b * S:(b + 1) * S], free)
            t_x = load(f"x{b % 2}", x_tok[:, b * TT:(b + 1) * TT, :], a["x"][:, b * TT:(b + 1) * TT, :])
            x_ready[b] = [t_x]
            hi = xt_hi[:, :, b * S:(b + 1) * S]
            lo = xt_lo[:, :, b * S:(b + 1) * S]
            xt_ready[b] = (split_dve if b < 2 else split_pool)(hi, lo, buf[:, :, :], [t_l])
            xraw.give(buf, xt_ready[b])
            return
            yield

        at(0, load_x(0))
        t_wq = []

        def split_wqkv():
            t_wq.extend(weights(split_dve, wqkv[0][:, :, :], wqkv[1][:, :, :], a["A_wqkv"]))
            return
            yield
        at(0, split_wqkv())
        for b in range(1, B):
            at(max(0, b - 2), load_x(b))

        qa = [[sb(f"qa_{n}{i}", [P, KC, S], F32R, early) for n in ("hi", "lo")] for i in range(2)]
        ka = [[sb(f"ka_{n}{i}", [P, KC, S], F32R, early) for n in ("hi", "lo")] for i in range(2)]
        qa_t, ka_t = Turns(qa), Turns(ka)
        vpad_t = Turns([sb(f"vpad{i}", [P, KC, S + 2], F32, early) for i in range(2)])
        ucv_t = Turns([(sb(f"uT{i}", [P, KC, S], F32, early), sb(f"cT{i}", [P, KC, S], F32, early)) for i in range(2)])
        utok_t = Turns([sb(f"utok{i}", [P, TT, D], F32, early) for i in range(2)])
        ctok_t = Turns([[sb(f"ctok_{n}{i}", [P, TT, D], F32R, early) for n in ("hi", "lo")] for i in range(2)])
        sm_t = Turns([sb(f"scoreA{i}", [P, 3 * P], F32, early) for i in range(2)])
        pa_t = Turns([sb(f"probA{i}", [P, 3 * P], F32, early) for i in range(2)])
        pta_t = Turns([[sb(f"probTA_{n}{i}", [P, 3 * P], F32R, early) for n in ("hi", "lo")] for i in range(2)])
        sma_t = Turns([sb(f"smallA{i}", [P, 16], F32, early) for i in range(3)])
        junk_a = sb("junkA", [P, P], F32, early)
        t_vz = [pool.do(lambda e, v=v: e.memset(v[:, :, :], 0.0)) for v, _ in vpad_t.free]
        scale_a = float(D) ** -0.5

        def attention_a(b):
            (qh, ql), q_free = qa_t.take()
            (kh, kl), k_free = ka_t.take()
            vp, v_free = vpad_t.take()
            (uT, cT), uc_free = ucv_t.take()
            need = [*xt_ready[b], *t_wq, *t_bc]
            done = []
            for which in range(3):
                bank, free = banks.take()
                for c in range(KC):
                    col = (which * KC + c) * P
                    t_mm = product(bank[:, c * S:(c + 1) * S],
                                   [((wqkv[0][:, k, col:col + P], wqkv[1][:, k, col:col + P]),
                                     (xt(xt_hi, b, k), xt(xt_lo, b, k))) for k in range(KC)],
                                   [*need, *free])
                halves = [(bank[:, c * S:(c + 1) * S], bqkv[:, which * KC + c:which * KC + c + 1]) for c in range(KC)]
                if which < 2:
                    hi, lo = ((qh, ql), (kh, kl))[which]
                    reads = split_biased([(hi[:, c, :], lo[:, c, :], *halves[c]) for c in range(KC)],
                                         [t_mm, *t_bc, *(q_free, k_free)[which]])
                else:
                    reads = [act_do(vp[:, c, 1:S + 1], ps, ACT.Identity, [t_mm, *t_vz, *v_free], bias=bias)
                             for c, (ps, bias) in enumerate(halves)]
                banks.give(bank, reads)
                done.append(reads)
            t_v = done[2]
            t_proj = t_mm
            t_c = []
            for c in range(KC):
                w = [wconv[:, c, j:j + 1] for j in range(3)]
                t_u = ts(pool, uT[:, c, :], vp[:, c, 2:S + 2], w[2], 1.0, ALU.mult, ALU.mult, after=[*t_v, *uc_free])
                t_1 = stt(cT[:, c, :], vp[:, c, 0:S], w[0], uT[:, c, :], ALU.mult, ALU.add, [t_u])
                t_c.append(stt(cT[:, c, :], vp[:, c, 1:S + 1], w[1], cT[:, c, :], ALU.mult, ALU.add, [t_1]))
            vpad_t.give(vp, t_c)
            yield
            bank, free = banks.take()
            t_s = product(bank[:, 0:P], [((qh[:, k, 0:P], ql[:, k, 0:P]), (kh[:, k, 0:P], kl[:, k, 0:P]))
                                         for k in range(KC)], [*done[0], *done[1], *free])
            t_s = product(bank[:, P:3 * P], [((qh[:, k, P:S], ql[:, k, P:S]), (kh[:, k, :], kl[:, k, :]))
                                             for k in range(KC)])
            qa_t.give((qh, ql), [t_s])
            ka_t.give((kh, kl), [t_s])
            bank_c, free_c = banks.take()
            t_ct = transposes(bank_c, [(bank_c[:, t * D + c * P:t * D + (c + 1) * P], cT[:, c, t * P:(t + 1) * P])
                                       for t in range(TT) for c in range(KC)], [*t_c, t_const_ident, *free_c])
            bank_u, free_u = banks.take()
            t_ut = transposes(bank_u, [(bank_u[:, t * D + c * P:t * D + (c + 1) * P], uT[:, c, t * P:(t + 1) * P])
                                       for t in range(TT) for c in range(KC)], free_u)
            ucv_t.give((uT, cT), [t_ut])
            sm, sm_free = sm_t.take()
            pr, pr_free = pa_t.take()
            small, small_free = sma_t.take()
            t_m = tt(dve, sm[:, :], bank[:, 0:3 * P], mask_a[:, :], ALU.add, [t_s, t_mask_a, *sm_free])
            banks.give(bank, [t_m])
            mx, nmx, den, dia, rin, ndg = (small[:, 2 * j:2 * j + 2] for j in range(6))
            dve.do(lambda e: e.tensor_reduce(mx[:, 0:1], sm[:, 0:P], AX.X, ALU.max), [t_m, *small_free])
            t_mx = dve.do(lambda e: e.tensor_reduce(mx[:, 1:2], sm[:, P:3 * P], AX.X, ALU.max))
            t_nm = ts(dve, nmx, mx, -scale_a, None, ALU.mult, after=[t_mx])
            act_do(pr[:, 0:P], sm[:, 0:P], ACT.Exp, [t_nm, *pr_free], scale=scale_a, bias=nmx[:, 0:1],
                   accum_out=den[:, 0:1])
            t_p = act_do(pr[:, P:3 * P], sm[:, P:3 * P], ACT.Exp, scale=scale_a, bias=nmx[:, 1:2],
                         accum_out=den[:, 1:2])
            sm_t.give(sm, [t_p])
            (ch, cl), c_free = ctok_t.take()
            t_cs = split_bank(ch[:, :, :], cl[:, :, :], bank_c[:, :].rearrange("p (t d) -> p t d", t=TT),
                              [t_ct, *c_free])
            banks.give(bank_c, t_cs)
            utok, u_free = utok_t.take()
            t_uc = act_do(utok[:, :, :], bank_u[:, :].rearrange("p (t d) -> p t d", t=TT), ACT.Identity,
                          [t_ut, *u_free])
            banks.give(bank_u, [t_uc])
            diag_cols = (slice(0, P), slice(2 * P, 3 * P))
            t_j = None
            for t in range(TT):
                t_j = stt(junk_a[:, :], pr[:, diag_cols[t]], 1.0, ident[:, :], ALU.mult, ALU.mult,
                          [t_p, t_const_ident] if t_j is None else [t_j], accum_out=dia[:, t:t + 1])
            t_ri = dve.do(lambda e: e.reciprocal(rin, den), [t_p])
            t_nd = stt(ndg, dia, -1.0, rin, ALU.mult, ALU.mult, [t_ri, t_j])
            yield
            bank, free = banks.take()
            t_t = transposes(bank, [(bank[:, j * P:(j + 1) * P], pr[:, j * P:(j + 1) * P]) for j in range(3)],
                             [t_p, *free])
            pa_t.give(pr, [t_t, t_j])
            (ph, pl), p_free = pta_t.take()
            t_ps = split_bank(ph[:, :], pl[:, :], bank[:, 0:3 * P], [t_t, *p_free])
            banks.give(bank, t_ps)
            yield
            bank, free = banks.take()
            t_o = product(bank[:, 0:D], [((ph[:, 0:P], pl[:, 0:P]), (ch[:, 0, :], cl[:, 0, :]))],
                          [*t_ps, *t_cs, *free])
            t_o = product(bank[:, D:2 * D], [((ph[:, (1 + j) * P:(2 + j) * P], pl[:, (1 + j) * P:(2 + j) * P]),
                                              (ch[:, j, :], cl[:, j, :])) for j in range(TT)])
            pta_t.give((ph, pl), [t_o])
            ctok_t.give((ch, cl), [t_o])
            r, r_free = r_bufs.take()
            for t in range(TT):
                t_r = stt(r[:, t, :], bank[:, t * D:(t + 1) * D], rin[:, t:t + 1], x_tok[:, b * TT + t, :],
                          ALU.mult, ALU.add, [t_o, t_ri, *x_ready[b], *r_free])
                t_r2 = stt(r[:, t, :], utok[:, t, :], ndg[:, t:t + 1], r[:, t, :], ALU.mult, ALU.add,
                           [t_r, t_nd, t_uc])
            banks.give(bank, [t_r])
            utok_t.give(utok, [t_r2])
            sma_t.give(small, [t_r2])
            yield from layernorm(b, r, [t_r2], [t_proj])

        for b in range(B):
            at(1 + b, attention_a(b))

        wv_b = [sb(f"bwv_{n}", [P, KC, P], F32R, early) for n in ("hi", "lo")]
        wt_b = [sb(f"bwt_{n}", [CK, 2, P], F32R, early) for n in ("hi", "lo")]
        b_bias = sb("b_bias", [P, 2], F32, early)
        t_ones = pool.do(lambda e: e.memset(ones[:, :], 1.0))
        t_bb = load("b_bias", b_bias[:, :], a["B_b"])
        t_bw = []

        def weights_b():
            t_bw.extend(weights(split_pool, wv_b[0][:, :, :], wv_b[1][:, :, :], a["B_wv"]))
            t_bw.extend(weights(split_pool, wt_b[0][:, :, :], wt_b[1][:, :, :], a["B_wt"]))
            return
            yield
        at(2, weights_b())

        def load_context(b):
            (i, raw), free = ctx_raw.take()
            t_l = load(f"ctx{i}", raw[:, :, :], a["ctxT"][:, :, b * S:(b + 1) * S], free)
            (hi, lo), c_free = ctx_t.take()
            toks = split_pool(hi[:, :, :], lo[:, :, :], raw[:, :, :], [t_l, *c_free])
            ctx_raw.give((i, raw), toks)
            return (hi, lo), toks

        vt_t = Turns([[sb(f"vt_{n}{i}", [P, 2, S], F32R, early) for n in ("hi", "lo")] for i in range(4)])
        sq_t = Turns([sb(f"sq{i}", [P, 2, S], F32, early) for i in range(2)])
        rn_t = Turns([sb(f"rn{i}", [P, 4], F32, early) for i in range(4)])
        dg_t = Turns([sb(f"dgt{i}", [P, TT, P], F32, early) for i in range(2)])
        rec_t = Turns([sb(f"recB{i}", [P, TT, S], F32, early) for i in range(2)])

        def cosine_b(b):
            (cxh, cxl), t_cx = load_context(b)
            yield
            bank, free = banks.take()
            t_v = product(bank[:, 0:S], [((wv_b[0][:, k, :], wv_b[1][:, k, :]), (xt(xt_hi, b, k), xt(xt_lo, b, k)))
                                         for k in range(KC)], [*xt_ready[b], *t_bw, *free])
            t_t = product(bank[:, S:2 * S], [((wt_b[0][:, k, :], wt_b[1][:, k, :]), (cxh[:, k, :], cxl[:, k, :]))
                                             for k in range(2)], t_cx)
            ctx_t.give((cxh, cxl), [t_t])
            (vh, vl), vt_free = vt_t.take()
            sq, sq_free = sq_t.take()
            halves = [(bank[:, i * S:(i + 1) * S], b_bias[:, i:i + 1]) for i in range(2)]
            for i, (ps, bias) in enumerate(halves):
                t_q = act_do(sq[:, i, :], ps, ACT.Square, [t_t, t_bb, *sq_free], bias=bias)
            toks = [t_q, *split_biased([(vh[:, i, :], vl[:, i, :], *halves[i]) for i in range(2)], [t_t, *vt_free])]
            banks.give(bank, toks)
            yield
            bank, free = banks.take()
            for i in range(2):
                for t in range(TT):
                    j = i * TT + t
                    t_n = matmuls([(bank[:, j:j + 1], sq[:, i, t * P:(t + 1) * P], ones[:, 0:1])],
                                  [*toks, t_ones, *free])
            sq_t.give(sq, [t_n])
            rn, rn_free = rn_t.take()
            t_rn = copy(dve, rn[:, :], bank[:, 0:4], [t_n, *rn_free])
            banks.give(bank, [t_rn])
            t_rn = tt(pool, rn[:, :], rn[:, :], minus_half[:, :], ALU.pow, [t_rn, t_const])
            yield
            dgt, dg_free = dg_t.take()
            for t in range(TT):
                t_d = ts(dve, dgt[:, t, :], ident[:, :], rn[:, TT + t:TT + t + 1], None, ALU.mult,
                         after=[t_rn, t_const_ident, *dg_free])
            yield
            bank_r, free = banks.take()
            for t in range(TT):
                t_r = matmuls([(bank_r[:, t * P:(t + 1) * P], ones[:, :], dgt[:, t, :])], [t_d, *free])
            dg_t.give(dgt, [t_r])
            bank, free = banks.take()
            for t in range(TT):
                t_dot = product(bank[:, t * S:(t + 1) * S],
                                [((vh[:, 0, t * P:(t + 1) * P], vl[:, 0, t * P:(t + 1) * P]), (vh[:, 1, :], vl[:, 1, :]))],
                                free)
            vt_t.give((vh, vl), [t_dot])
            rec, rec_free = rec_t.take()
            r, r_free = r_bufs.take()
            for t in range(TT):
                t_rec = ts(dve, rec[:, t, :], bank_r[:, 0:S], rn[:, t:t + 1], 1e8, ALU.mult, ALU.min,
                           after=[t_r, *rec_free])
            banks.give(bank_r, [t_rec])
            rn_t.give(rn, [t_rec])
            t_m = tt(dve, rec[:, :, :], bank[:, :].rearrange("p (t s) -> p t s", t=TT), rec[:, :, :], ALU.mult,
                     [t_dot, t_rec])
            banks.give(bank, [t_m])
            t_add = tt(dve, r[:, :, :], rec[:, :, :], x_tok[:, b * TT:(b + 1) * TT, :], ALU.add,
                       [t_m, *x_ready[b], *r_free])
            rec_t.give(rec, [t_add])
            yield from layernorm(b, r, [t_add], [t_v])

        first_b = 6
        for b in range(B):
            at(first_b + b, cosine_b(b))

        def run():
            todo = sorted(plan)
            plan.clear()
            live, r = [], 0
            while todo or live:
                while todo and todo[0][0] <= r:
                    live.append(todo.pop(0)[2])
                live = [g for g in live if next(g, "end") != "end"]
                r += 1

        run()
        early.close()
        t_early = fence()
        NPIECE = 4 + 8 + 8 + 2
        wraw_t = Turns([(i, sb(f"wraw{i}", [P, CW], F32, late, "right")) for i in range(3)], t_early)
        wpiece_t = Turns([[sb(f"wpiece_{n}{i}", [P, CW], F32R, late, "right") for n in ("hi", "lo")] for i in range(3)], t_early)
        hid = [[sb(f"hid{i}_{n}", [P, FC, SB], F32R, late, "right") for n in ("hi", "lo")] for i in range(2)]
        hf_t = Turns([sb(f"hf{i}", [P, SB], F32, late, "right") for i in range(2)], t_early)
        sg_t = Turns([sb(f"sg{i}", [P, SB], F32, late, "right") for i in range(2)], t_early)
        scl = sb("ffn_scales", [P, 4, FC], F32, late, "right")
        s3b = sb("ffn_s3", [P, D], F32, late, "right")
        t_scl = [load("ffn_s", scl[:, :, :], a["C_s"], t_early), load("ffn_s3", s3b[:, :], a["C_s3"], t_early)]

        pieces = {}

        def piece(sbk, n):
            (i, raw), free = wraw_t.take()
            t_l = load(f"piece{i}", raw[:, :], a["C_w"][n], free)
            (hi, lo), w_free = wpiece_t.take()
            toks = split_pool(hi[:, :], lo[:, :], raw[:, :], [t_l, *w_free])
            wraw_t.give((i, raw), toks)
            pieces[(sbk, n)] = ((hi, lo), toks)

        def ffn():
            order = [(s, n) for s in range(NSB) for n in range(NPIECE)]
            ahead = [0]

            def want():
                if ahead[0] < len(order) and len(wpiece_t.free) and len(wraw_t.free):
                    piece(*order[ahead[0]])
                    ahead[0] += 1

            want(), want()
            hid_readers = [t_early, t_early]
            for s in range(NSB):
                cols = slice(s * SB, (s + 1) * SB)
                seqs = range(s * BPS, (s + 1) * BPS)
                x_in = [(xt_hi[:, k, cols], xt_lo[:, k, cols]) for k in range(KC)]
                need = [t for b in seqs for t in xt_ready[b]]
                chunk_ready = []
                for n in range(4):
                    want()
                    (wh, wl), t_w = pieces.pop((s, n))
                    for oo in range(2):
                        o = 2 * n + oo
                        pair = []
                        for mat in range(2):
                            bank, free = banks.take()
                            terms = []
                            for k in range(KC):
                                c0 = ((mat * 2 + oo) * KC + k) * P
                                terms.append(((wh[:, c0:c0 + P], wl[:, c0:c0 + P]), x_in[k]))
                            t_mm = product(bank[:, :], terms, [*need, *t_w, *free])
                            pair.append((bank, t_mm))
                        sg, sg_free = sg_t.take()
                        hf, hf_free = hf_t.take()
                        t_sg = act_do(sg[:, :], pair[0][0][:, :], ACT.Silu, [pair[0][1], *t_scl, *sg_free],
                                      scale=scl[:, 0, o:o + 1])
                        banks.give(pair[0][0], [t_sg])
                        t_h = stt(hf[:, :], pair[1][0][:, :], scl[:, 1, o:o + 1], sg[:, :], ALU.mult, ALU.mult,
                                  [pair[1][1], t_sg, *t_scl, *hf_free])
                        banks.give(pair[1][0], [t_h])
                        sg_t.give(sg, [t_h])
                        toks = split_dve(hid[0][0][:, o, :], hid[0][1][:, o, :], hf[:, :], [t_h, *hid_readers[0]])
                        hf_t.give(hf, toks)
                        chunk_ready.append(toks)
                    wpiece_t.give((wh, wl), [t_mm])
                for layer in range(2):
                    src, dst = hid[layer % 2], hid[(layer + 1) % 2]
                    new_ready = []
                    for o in range(FC):
                        want()
                        (wh, wl), t_w = pieces.pop((s, 4 + layer * FC + o))
                        bank, free = banks.take()
                        for k in range(FC):
                            for i3, (ww, hh) in enumerate(((wl, src[0]), (wh, src[1]), (wh, src[0]))):
                                first, final = k == 0 and i3 == 0, k == FC - 1 and i3 == 2
                                mm = lambda e, ww=ww, hh=hh, k=k, first=first, final=final, bank=bank: e.matmul(
                                    bank[:, :], ww[:, k * P:(k + 1) * P], hh[:, k, :], start=first, stop=final)
                                after = (*chunk_ready[k], *t_w, *free) if i3 == 0 else ()
                                if final:
                                    t_mm = pe.do(mm, after)
                                else:
                                    pe.quiet(mm, after)
                        wpiece_t.give((wh, wl), [t_mm])
                        hf, hf_free = hf_t.take()
                        t_g = act_do(hf[:, :], bank[:, :], ACT.Gelu, [t_mm, *t_scl, *hf_free],
                                     scale=scl[:, 2 + layer, o:o + 1])
                        banks.give(bank, [t_g])
                        toks = split_dve(dst[0][:, o, :], dst[1][:, o, :], hf[:, :],
                                         [t_g, *hid_readers[(layer + 1) % 2]])
                        hf_t.give(hf, toks)
                        new_ready.append(toks)
                    hid_readers[layer % 2] = [t_mm]
                    chunk_ready = new_ready
                src = hid[0]
                want(), want()
                halves = [pieces.pop((s, NPIECE - 2 + j)) for j in range(2)]
                for bi, b in enumerate(seqs):
                    bank, free = banks.take()
                    for t in range(TT):
                        c0 = bi * S + t * P
                        terms = []
                        need3 = [*free]
                        for k in range(FC):
                            (wh, wl), t_w = halves[k // 4]
                            w0 = (k % 4) * D
                            terms.append(((src[0][:, k, c0:c0 + P], src[1][:, k, c0:c0 + P]),
                                          (wh[:, w0:w0 + D], wl[:, w0:w0 + D])))
                            need3 += [*t_w, *chunk_ready[k]]
                        t_mm = product(bank[:, t * D:(t + 1) * D], terms, need3)
                    r, r_free = r_bufs.take()
                    for t in range(TT):
                        t_y = tt(dve, r[:, t, :], bank[:, t * D:(t + 1) * D], s3b[:, :], ALU.mult,
                                 [t_mm, *t_scl, *r_free])
                    banks.give(bank, [t_y])
                    t_r = tt(dve, r[:, :, :], r[:, :, :], x_tok[:, b * TT:(b + 1) * TT, :], ALU.add,
                             [t_y, *x_ready[b]])
                    yield from layernorm(b, r, [t_r], [t_mm])
                for (wh, wl), _ in halves:
                    wpiece_t.give((wh, wl), [t_mm])
                hid_readers[0] = [t_mm]

        at(0, ffn())
        run()
        late.close()

        t_late = fence()
        part = ExitStack()
        sbp = lambda name, shape, dt=F32, scope=part, side="left": sb(name, shape, dt, scope, side)
        vpad2_t = Turns([sbp(f"vheads{i}", [P, TT, NH, P], F32R) for i in range(1)])
        acc_sb_t = Turns([sbp(f"accT{i}", [P, NVT, S]) for i in range(1)])
        ctok2_t = Turns([sbp(f"ctxtok{i}", [P, TT, D]) for i in range(2)])
        sum_t = Turns([sbp(f"csum{i}", [P, NH, DH]) for i in range(2)])
        rin_t = Turns([sbp(f"crin{i}", [P, NH]) for i in range(2)])
        cT_t = Turns([[sbp(f"ctxT_{n}{i}", [P, KC, S], F32R) for n in ("hi", "lo")] for i in range(1)])
        vf_t = Turns([sbp(f"vf{i}", [P, TT, D]) for i in range(1)])
        xb_t = Turns([sbp(f"xb{i}", [P, TT, D]) for i in range(2)])
        t_vheads = []
        for v, _ in vpad2_t.free:
            t_z = pool.do(lambda e, v=v: e.memset(f(v[:, :, :, :]), 0.0), t_late)
            for g in range(VH):
                heads = v[:, :, g::VH, g * VW + 2 * DH:g * VW + 2 * DH + 1]
                t_z = pool.do(lambda e, heads=heads: e.memset(f(heads), 1.0), [t_z])
            t_vheads.append(t_z)

        def place_values(v, vf, after):
            toks = []
            for g in range(VH):
                nh = len(range(g, NH, VH))
                for t in range(TT):
                    src = vf[:, t, :].rearrange("p (h d) -> p h d", h=NH)[:, g::VH, :]
                    hi = v[:, t, g::VH, g * VW:g * VW + DH]
                    lo = v[:, t, g::VH, g * VW + DH:g * VW + 2 * DH]
                    t_hi = copy(dve, hi, src, after)
                    toks.append(tt(dve, lo, src, f(hi), ALU.subtract, [t_hi]))
            return toks

        def finish_heads(b, accs, t_acc, delta, wo, t_wo, xb, t_xb, xt_readers, then=None):
            acc_sb, s_free = acc_sb_t.take()
            toks = []
            for i, bank in enumerate(accs):
                t_e = act_do(acc_sb[:, 2 * i:2 * i + 2, :], bank[:, :].rearrange("p (j s) -> p j s", j=2),
                             ACT.Identity, [t_acc, *s_free])
                banks.give(bank, [t_e])
                toks.append(t_e)
            yield
            ctok, c_free = ctok2_t.take()
            for t in range(TT):
                csum, cs_free = sum_t.take()
                rin, ri_free = rin_t.take()
                h0 = 0
                for tiles in ((0, 1, 2), (3, 4, 5)):
                    nh = min(NH, (tiles[-1] + 1) * VH) - tiles[0] * VH
                    bank, free = banks.take()
                    parts = []
                    for j, tile in enumerate(tiles):
                        rows = VW * min(VH, NH - tile * VH)
                        parts.append((bank[:, j * VH * VW:j * VH * VW + rows], acc_sb[0:rows, tile, t * P:(t + 1) * P]))
                    t_tr = transposes(bank, parts, [*toks, *free])
                    view = bank[:, 0:nh * VW].rearrange("p (h w) -> p h w", w=VW)
                    hi_lo = view[:, :, 0:2 * DH].rearrange("p h (two d) -> p h d two", two=2)
                    t_sum = dve.do(lambda e, csum=csum, h0=h0, nh=nh, hi_lo=hi_lo: e.tensor_reduce(
                        csum[:, h0:h0 + nh, :], hi_lo, AX.X, ALU.add), [t_tr, *cs_free])
                    t_den = ts(dve, rin[:, h0:h0 + nh], view[:, :, 2 * DH], delta, None, ALU.add,
                               after=[t_tr, *ri_free])
                    banks.give(bank, [t_sum, t_den])
                    h0 += nh
                t_ri = dve.do(lambda e, rin=rin: e.reciprocal(rin[:, :], rin[:, :]), [t_den])
                t_ct = tt(dve, ctok[:, t, :].rearrange("p (h d) -> p h d", h=NH), csum[:, :, :],
                          rin[:, :, None].to_broadcast([P, NH, DH]), ALU.mult, [t_ri, t_sum, *c_free])
                sum_t.give(csum, [t_ct])
                rin_t.give(rin, [t_ct])
            acc_sb_t.give(acc_sb, [t_tr])
            yield
            bank, free = banks.take()
            t_tr = transposes(bank, [(bank[:, c * S + t * P:c * S + (t + 1) * P], ctok[:, t, c * P:(c + 1) * P])
                                     for c in range(KC) for t in range(TT)], [t_ct, *free])
            ctok2_t.give(ctok, [t_tr])
            (ch, cl), ct_free = cT_t.take()
            t_cs = split_bank(ch[:, :, :], cl[:, :, :], bank[:, :].rearrange("p (c s) -> p c s", c=KC),
                              [t_tr, *ct_free])
            banks.give(bank, t_cs)
            yield
            bank, free = banks.take()
            for t in range(TT):
                t_y = product(bank[:, t * D:(t + 1) * D],
                              [((ch[:, c, t * P:(t + 1) * P], cl[:, c, t * P:(t + 1) * P]), (wo[0][:, c, :], wo[1][:, c, :]))
                               for c in range(KC)], [*t_cs, *t_wo, *free])
            cT_t.give((ch, cl), [t_y])
            r, r_free = r_bufs.take()
            t_r = tt(dve, r[:, :, :], bank[:, :].rearrange("p (t d) -> p t d", t=TT), xb[:, :, :], ALU.add,
                     [t_y, t_xb, *r_free])
            banks.give(bank, [t_r])
            xb_t.give(xb, [t_r])
            yield from layernorm(b, r, [t_r], xt_readers)
            if then is not None:
                yield
                yield from then(b)

        def head_bank(h, accs):
            tile = h // VH
            return accs[tile // 2][:, (tile % 2) * S:(tile % 2 + 1) * S]

        dpart = ExitStack()
        sbd = lambda name, shape, dt=F32: sb(name, shape, dt, dpart, "right")
        dw = [sbd(f"dw_{n}", [P, KC, 3 * D], F32R) for n in ("hi", "lo")]
        dwo = [sbd(f"dwo_{n}", [P, KC, D], F32R) for n in ("hi", "lo")]
        proj = [sbd(f"proj_{n}", [P, NH // 2, P], F32R) for n in ("hi", "lo")]
        dbias = sbd("dbias", [P, 2 * KC])
        dbv = sbd("dbv", [P, D])
        dbo = sbd("dbo", [P, D])
        mask_d = sbd("mask_d", [P, 3 * P])
        t_db = [load("d_b", dbias[:, :], a["D_b"], t_late), load("d_bv", dbv[:, :], a["D_bv"], t_late),
                load("d_bo", dbo[:, :], a["D_bo"], t_late), load("d_mask", mask_d[:, :], a["mask_d"], t_late)]
        t_dw = weights(split_dve, dw[0][:, :, :], dw[1][:, :, :], a["D_w"], t_late)
        t_dp = weights(split_dve, proj[0][:, :, :], proj[1][:, :, :], a["D_proj"], t_late)
        t_dwo = weights(split_pool, dwo[0][:, :, :], dwo[1][:, :, :], a["D_wo"], t_late)
        qk_t = Turns([[[sbd(f"{w}d_{n}{i}", [P, KC, S], F32R) for n in ("hi", "lo")] for w in "qk"] for i in range(2)],
                     t_late)
        feat_t = Turns([[sbd(f"feat_{n}{i}", [P, 2, S], F32R) for n in ("hi", "lo")] for i in range(3)], t_late)
        awm_t = Turns([sbd(f"awm{i}", [P, 3 * P]) for i in range(4)], t_late)
        aw_t = Turns([[sbd(f"aw_{n}{i}", [P, 3 * P], F32R) for n in ("hi", "lo")] for i in range(6)], t_late)
        state_d = {}

        def prelude_d(b):
            ((qh, ql), (kh, kl)), qk_free = qk_t.take()
            need = [*xt_ready[b], *t_dw, *t_db]
            toks = []
            for which, (hi, lo) in enumerate(((qh, ql), (kh, kl))):
                bank, free = banks.take()
                for c in range(KC):
                    col = (which * KC + c) * P
                    t_mm = product(bank[:, c * S:(c + 1) * S],
                                   [((dw[0][:, k, col:col + P], dw[1][:, k, col:col + P]),
                                     (xt(xt_hi, b, k), xt(xt_lo, b, k))) for k in range(KC)], [*need, *free])
                reads = split_biased([(hi[:, c, :], lo[:, c, :], bank[:, c * S:(c + 1) * S],
                                       dbias[:, which * KC + c:which * KC + c + 1]) for c in range(KC)],
                                     [t_mm, *t_db, *qk_free])
                banks.give(bank, reads)
                toks += reads
            yield
            bank, free = banks.take()
            for t in range(TT):
                t_mm = product(bank[:, t * D:(t + 1) * D],
                               [(sh, (dw[0][:, k, 2 * D:3 * D], dw[1][:, k, 2 * D:3 * D]))
                                for k, sh in enumerate(xt_tile(b, t))], free)
            vf, vf_free = vf_t.take()
            for t in range(TT):
                t_vf = tt(dve, vf[:, t, :], bank[:, t * D:(t + 1) * D], dbv[:, :], ALU.add, [t_mm, *vf_free, *t_late])
            banks.give(bank, [t_vf])
            xb, xb_free = xb_t.take()
            for t in range(TT):
                t_xb = tt(pool, xb[:, t, :], x_tok[:, b * TT + t, :], dbo[:, :], ALU.add,
                          [*x_ready[b], *t_db, *xb_free, *t_late])
            state_d[b] = dict(q=(qh, ql), k=(kh, kl), qk_ready=toks, vf=vf, t_vf=t_vf, xb=xb, t_xb=t_xb, xt_last=t_mm)

        def place(state, b, zeroed):
            st = state[b]
            v, v_free = vpad2_t.take()
            st["v"] = v
            st["v_ready"] = place_values(v, st["vf"], [st["t_vf"], *v_free, *zeroed])
            vf_t.give(st["vf"], st["v_ready"])
            return
            yield

        def pair_d(b, j):
            st = state_d[b]
            c = 2 * j // (NH // KC)
            pair_bufs, f_free = feat_t.take()
            feat_hi, feat_lo = pair_bufs
            (qfh, kfh), (qfl, kfl) = ((x[:, 0, :], x[:, 1, :]) for x in pair_bufs)
            bank, free = banks.take()
            for w, (hi, lo) in enumerate((st["q"], st["k"])):
                t_f = product(bank[:, w * S:(w + 1) * S],
                              [((proj[0][:, j, :], proj[1][:, j, :]), (hi[:, c, :], lo[:, c, :]))],
                              [*st["qk_ready"], *t_dp, *free])
            if j == NH // 2 - 1:
                qk_t.give((st["q"], st["k"]), [t_f])
            both = bank[:, :].rearrange("p (w s) -> p w s", w=2)
            t_hi = act_do(feat_hi[:, :, :], both, ACT.Relu, [t_f, *f_free])
            t_lo = stt(feat_lo[:, :, :], both, 0.0, f(feat_hi[:, :, :]), ALU.max, ALU.subtract, [t_hi])
            f_ready = [t_hi, t_lo]
            banks.give(bank, f_ready)
            yield
            yield
            aws = []
            for g in range(2):
                rows = slice(g * M, (g + 1) * M)
                bank, free = banks.take()
                t_a = product(bank[:, 0:S], [((kfh[rows, 0:P], kfl[rows, 0:P]), (qfh[rows, :], qfl[rows, :]))],
                              [*f_ready, *free])
                t_a = product(bank[:, S:S + P], [((kfh[rows, P:S], kfl[rows, P:S]), (qfh[rows, P:S], qfl[rows, P:S]))])
                awm, m_free = awm_t.take()
                (ah, al), a_free = aw_t.take()
                t_m = tt(dve, awm[:, :], bank[:, 0:3 * P], mask_d[:, :], ALU.mult, [t_a, *t_db, *m_free])
                banks.give(bank, [t_m])
                t_h = act_do(ah[:, :], awm[:, :], ACT.Identity, [t_m, *a_free])
                aws.append([(ah, al), awm, t_h])
            feat_t.give(pair_bufs, [t_a])
            yield
            for g, ((ah, al), awm, t_h) in enumerate(aws):
                t_l = tt(dve, al[:, :], awm[:, :], f(ah[:, :]), ALU.subtract, [t_h])
                awm_t.give(awm, [t_h, t_l])
                aws[g] = ((ah, al), [t_h, t_l])
            yield
            if j == 0:
                st["accs"] = [banks.take() for _ in range(3)]
            for g in range(2):
                h = 2 * j + g
                (ah, al), ready = aws[g]
                weighted_values(st, h, [(0, ah[:, 0:S], al[:, 0:S], slice(0, S)),
                                        (1, ah[:, S:S + P], al[:, S:S + P], slice(P, S))], ready)
                aw_t.give((ah, al), [pe.last()])
            if j == NH // 2 - 1:
                vpad2_t.give(st["v"], [pe.last()])

        def weighted_values(st, h, parts, ready):
            bank, bank_free = st["accs"][h // VH // 2]
            base = (h // VH % 2) * S
            first_of_tile = h % VH == 0
            last_of_tile = h % VH == VH - 1 or h == NH - 1
            terms = [(t, w, cols) for t, hi, lo, cols in parts for w in (lo, hi)]
            for i, (t, w, cols) in enumerate(terms):
                o = bank[:, base + cols.start:base + cols.stop]
                mm = lambda e, o=o, t=t, w=w, i=i: e.matmul(
                    o, st["v"][:, t, h, :], w, start=(first_of_tile and i == 0),
                    stop=(last_of_tile and i == len(terms) - 1), skip_group_check=True)
                after = [*ready, *st["v_ready"], *bank_free] if i == 0 else ()
                if i == len(terms) - 1:
                    pe.do(mm, after)
                else:
                    pe.quiet(mm, after)

        def finish_d(b):
            st = state_d[b]
            yield from finish_heads(b, [x for x, _ in st["accs"]], pe.last(), DELTA, dwo, t_dwo,
                                    st["xb"], st["t_xb"], [st["xt_last"]])

        per_b = NH // 2
        for b in range(B):
            at(max(0, 2 + per_b * b - 3), prelude_d(b))
            for j in range(per_b):
                at(2 + per_b * b + j, pair_d(b, j))
            at(2 + per_b * b + 3, place(state_d, b, t_vheads))
            at(2 + per_b * b + per_b + 3, finish_d(b))
        run()
        dpart.close()
        t_d = fence()

        epart = ExitStack()
        sbe = lambda name, shape, dt=F32: sb(name, shape, dt, epart, "right")
        NS4 = 4
        eq = [sbe(f"eq_{n}", [P, KC, NS4 * P], F32R) for n in ("hi", "lo")]
        ek = [sbe(f"ek_{n}", [CK, 2, NS4 * P], F32R) for n in ("hi", "lo")]
        ev = [sbe(f"ev_{n}", [CK, 2, D], F32R) for n in ("hi", "lo")]
        eo = [sbe(f"eo_{n}", [P, KC, D], F32R) for n in ("hi", "lo")]
        ebias = sbe("ebias", [P, 3 * NS4])
        ebv, ebo = sbe("ebv", [P, D]), sbe("ebo", [P, D])
        low_rows = sbe("low_rows", [P, 1])
        t_eb = [load("e_b", ebias[:, 0:2 * NS4], a["E_b"], t_d), load("e_bv", ebv[:, :], a["E_bv"], t_d),
                load("e_bo", ebo[:, :], a["E_bo"], t_d), load("e_m", low_rows[:, :], a["low_rows"], t_d)]
        t_ew = [*weights(split_dve, eq[0][:, :, :], eq[1][:, :, :], a["E_wq"], t_d),
                *weights(split_dve, ek[0][:, :, :], ek[1][:, :, :], a["E_wk"], t_d),
                *weights(split_pool, ev[0][:, :, :], ev[1][:, :, :], a["E_wv"], t_d)]
        t_eo = weights(split_pool, eo[0][:, :, :], eo[1][:, :, :], a["E_wo"], t_d)
        t_eb.append(ts(dve, ebias[:, 2 * NS4:3 * NS4], ebias[:, 0:NS4], low_rows[:, 0:1], None, ALU.mult, after=t_eb))
        qs_t = Turns([sbe(f"qslots{i}", [P, NS4, S], F32R) for i in range(2)], t_d)
        qm_t = Turns([sbe(f"qmask{i}", [P, 2, S], F32R) for i in range(2)], t_d)
        ks_t = Turns([[sbe(f"kslots_{n}{i}", [P, NS4, S], F32R) for n in ("hi", "lo")] for i in range(2)], t_d)
        se_t = Turns([sbe(f"scoreE{i}", [P, TT, S]) for i in range(2)], t_d)
        pe_t = Turns([sbe(f"probE{i}", [P, TT, S]) for i in range(2)], t_d)
        pte_t = Turns([[sbe(f"probTE_{n}{i}", [P, TT, S], F32R) for n in ("hi", "lo")] for i in range(3)], t_d)
        sme_t = Turns([sbe(f"smallE{i}", [P, 2 * TT]) for i in range(3)], t_d)
        scale_e = float(DH) ** -0.5
        state_e = {}

        def prelude_e(b):
            (cxh, cxl), t_cx = load_context(b)
            qs, q_free = qs_t.take()
            (kh, kl), k_free = ks_t.take()
            ready = []
            yield
            for half in range(2):
                bank, free = banks.take()
                for j in range(2):
                    n = 2 * half + j
                    t_mm = product(bank[:, j * S:(j + 1) * S],
                                   [((eq[0][:, k, n * P:(n + 1) * P], eq[1][:, k, n * P:(n + 1) * P]),
                                     (xt(xt_hi, b, k), xt(xt_lo, b, k))) for k in range(KC)],
                                   [*xt_ready[b], *t_ew, *free])
                qm, m_free = qm_t.take()
                for j in range(2):
                    n = 2 * half + j
                    t_m = act_do(qm[:, j, :], bank[:, j * S:(j + 1) * S], ACT.Identity, [t_mm, *t_eb, *m_free],
                                 scale=low_rows[:, 0:1], bias=ebias[:, 2 * NS4 + n:2 * NS4 + n + 1])
                for j in range(2):
                    n = 2 * half + j
                    t_q = stt(qs[:, n, :], bank[:, j * S:(j + 1) * S], ebias[:, n:n + 1], f(qm[:, j, :]),
                              ALU.add, ALU.subtract, [t_m, *q_free])
                toks = [t_m, t_q]
                banks.give(bank, toks)
                qm_t.give(qm, toks)
                ready += toks
            t_xt = t_mm
            yield
            for half in range(2):
                bank, free = banks.take()
                for j in range(2):
                    n = 2 * half + j
                    t_mm = product(bank[:, j * S:(j + 1) * S],
                                   [((ek[0][:, k, n * P:(n + 1) * P], ek[1][:, k, n * P:(n + 1) * P]),
                                     (cxh[:, k, :], cxl[:, k, :])) for k in range(2)], [*t_cx, *free])
                toks = split_biased([(kh[:, n, :], kl[:, n, :], bank[:, (n % 2) * S:(n % 2 + 1) * S],
                                      ebias[:, NS4 + n:NS4 + n + 1]) for n in (2 * half, 2 * half + 1)],
                                    [t_mm, *t_eb, *k_free])
                banks.give(bank, toks)
                ready += toks
            yield
            bank, free = banks.take()
            for t in range(TT):
                t_mm = product(bank[:, t * D:(t + 1) * D],
                               [((cxh[:, k, t * P:(t + 1) * P], cxl[:, k, t * P:(t + 1) * P]),
                                 (ev[0][:, k, :], ev[1][:, k, :])) for k in range(2)], free)
            ctx_t.give((cxh, cxl), [t_mm])
            vf, vf_free = vf_t.take()
            for t in range(TT):
                t_vf = tt(dve, vf[:, t, :], bank[:, t * D:(t + 1) * D], ebv[:, :], ALU.add, [t_mm, *t_eb, *vf_free])
            banks.give(bank, [t_vf])
            xb, xb_free = xb_t.take()
            for t in range(TT):
                t_xb = tt(pool, xb[:, t, :], x_tok[:, b * TT + t, :], ebo[:, :], ALU.add,
                          [*x_ready[b], *t_eb, *xb_free])
            state_e[b] = dict(q=qs, k=(kh, kl), qk_ready=ready, vf=vf, t_vf=t_vf, xb=xb, t_xb=t_xb, xt_last=t_xt)

        def head_e(b, h):
            st = state_e[b]
            rows, n = slice(32 * (h % 4), 32 * (h % 4) + 32), h // 4
            qs, (kh, kl) = st["q"], st["k"]
            bank, free = banks.take()
            for t in range(TT):
                o = bank[:, t * S:(t + 1) * S]
                q = qs[rows, n, t * P:(t + 1) * P]
                t_s = matmuls([(o, q, kl[rows, n, :]), (o, q, kh[rows, n, :])], [*st["qk_ready"], *free])
            if h == NH - 1:
                qs_t.give(qs, [t_s])
                ks_t.give((kh, kl), [t_s])
            sc, sc_free = se_t.take()
            small, sm_free = sme_t.take()
            mx, nmx = small[:, 0:TT], small[:, TT:2 * TT]
            lim = CLAMP / scale_e
            yield
            t_c = ts(dve, sc[:, :, :], bank[:, :].rearrange("p (t s) -> p t s", t=TT), lim, -lim, ALU.min, ALU.max,
                     after=[t_s, *sc_free])
            banks.give(bank, [t_c])
            t_mx = dve.do(lambda e: e.tensor_reduce(mx, sc[:, :, :], AX.X, ALU.max), [t_c, *sm_free])
            t_nm = ts(dve, nmx, mx, -scale_e, None, ALU.mult, after=[t_mx])
            yield
            pr, p_free = pe_t.take()
            for t in range(TT):
                t_p = act_do(pr[:, t, :], sc[:, t, :], ACT.Exp, [t_nm, *p_free], scale=scale_e, bias=nmx[:, t:t + 1])
            se_t.give(sc, [t_p])
            sme_t.give(small, [t_p])
            yield
            bank, free = banks.take()
            t_t = transposes(bank, [(bank[:, kt * S + t * P:kt * S + (t + 1) * P], pr[:, t, kt * P:(kt + 1) * P])
                                    for kt in range(TT) for t in range(TT)], [t_p, *free])
            pe_t.give(pr, [t_t])
            (ph, pl), pt_free = pte_t.take()
            both = bank[:, :].rearrange("p (k s) -> p k s", k=TT)
            t_hi = act_do(ph[:, :, :], both, ACT.Identity, [t_t, *pt_free])
            yield
            ready = [t_hi, tt(dve, pl[:, :, :], both, f(ph[:, :, :]), ALU.subtract, [t_hi])]
            banks.give(bank, ready)
            yield
            if h == 0:
                st["accs"] = [banks.take() for _ in range(3)]
            weighted_values(st, h, [(kt, ph[:, kt, :], pl[:, kt, :], slice(0, S)) for kt in range(TT)], ready)
            pte_t.give((ph, pl), [pe.last()])
            if h == NH - 1:
                vpad2_t.give(st["v"], [pe.last()])

        t_gw = [load("gw", gw_raw[:, :, :], a["gate_w"], t_d), load("b2", b2_sb[:, :], a["F_b2"], t_d),
                load("iota8", iota8[:, :], a["iota8"], t_d)]
        xtf_t = Turns([sbe(f"xtf{i}", [P, KC, S]) for i in range(1)], t_d)
        rt_t = Turns([sbe(f"route{i}", [P, TT, 8, NE]) for i in range(2)], t_d)
        gT_t = Turns([sbe("gatesT", [NE, S])], t_d)
        ridx_t = Turns([sbe(f"ridx{i}", [P, TT, NE], U32) for i in range(2)], t_d)
        gates_ready = [None] * B

        def route(b):
            xtf, x_free = xtf_t.take()
            t_x = tt(pool, xtf[:, :, :], f(xt_hi[:, :, b * S:(b + 1) * S]), f(xt_lo[:, :, b * S:(b + 1) * S]), ALU.add,
                     [*xt_ready[b], *x_free])
            yield
            bank, free = banks.take()
            for t in range(TT):
                t_l = matmuls([(bank[:, t * NE:(t + 1) * NE], xtf[:, k, t * P:(t + 1) * P], gw_raw[:, k, :])
                               for k in range(KC)], [t_x, *t_gw, *free])
            xtf_t.give(xtf, [t_l])
            rt, rt_free = rt_t.take()
            ridx, ri_free = ridx_t.take()
            lg, ex, top, oh = rt[:, :, 0, :], rt[:, :, 1, :], rt[:, :, 2, :], rt[:, :, 3:5, :]
            small, idf = rt[:, :, 5, :], rt[:, :, 6, :]
            t_c = copy(dve, lg, bank[:, 0:TT * NE].rearrange("p (t e) -> p t e", t=TT), [t_l, *rt_free, *ri_free])
            banks.give(bank, [t_c])
            t_m = dve.do(lambda e: e.tensor_reduce(small[:, :, 0], lg, AX.X, ALU.max, negate=True), [t_c])
            for t in range(TT):
                t_e = act_do(ex[:, t, :], lg[:, t, :], ACT.Exp, [t_m], bias=small[:, t, 0:1],
                             accum_out=small[:, t, 1:2])
            yield
            t_r = dve.do(lambda e: e.reciprocal(small[:, :, 2], small[:, :, 1]), [t_e])
            for t in range(TT):
                t_g = ts(dve, ex[:, t, :], ex[:, t, :], small[:, t, 2:3], None, ALU.mult, after=[t_r])
            for t in range(TT):
                t_t = dve.do(lambda e, t=t: e.max(top[:, t, :], ex[:, t, :]), [t_g])
            for t in range(TT):
                t_i = dve.do(lambda e, t=t: e.max_index(ridx[:, t, :], top[:, t, :], ex[:, t, :]), [t_t])
            t_f = copy(dve, idf, ridx[:, :, :], [t_i])
            t_s = tt(dve, small[:, :, 3], top[:, :, 0], top[:, :, 1], ALU.add, [t_t])
            t_s = dve.do(lambda e: e.reciprocal(small[:, :, 3], small[:, :, 3]), [t_s])
            for j in range(2):
                t_s = tt(dve, small[:, :, 4 + j], top[:, :, j], small[:, :, 3], ALU.mult, [t_s])
            for t in range(TT):
                for j in range(2):
                    t_o = ts(dve, oh[:, t, j, :], iota8[:, :], idf[:, t, j:j + 1], small[:, t, 4 + j:5 + j],
                             ALU.is_equal, ALU.mult, after=[t_f, t_s, *t_gw])
            t_g = tt(dve, gates[:, b * TT:(b + 1) * TT, :], oh[:, :, 0, :], oh[:, :, 1, :], ALU.add, [t_o])
            rt_t.give(rt, [t_g])
            ridx_t.give(ridx, [t_g])
            gates_ready[b] = [t_g]
            yield
            bank, free = banks.take()
            t_t = transposes(bank, [(bank[0:NE, t * P:(t + 1) * P], gates[:, b * TT + t, :]) for t in range(TT)],
                             [t_g, *free])
            gT, gT_free = gT_t.take()
            t_c = copy(dve, gT[:, :], bank[0:NE, 0:S], [t_t, *gT_free])
            banks.give(bank, [t_c])
            yield
            bank, free = banks.take()
            for t in range(TT):
                t_b = matmuls([(bank[:, t * D:(t + 1) * D], gT[:, t * P:(t + 1) * P], b2_sb[:, :])],
                              [t_c, *t_gw, *free])
            gT_t.give(gT, [t_b])
            xs = x_tok[:, b * TT:(b + 1) * TT, :]
            t_a = tt(dve, xs, bank[:, :].rearrange("p (t d) -> p t d", t=TT), xs, ALU.add,
                     [t_b, *x_ready[b], *xt_ready[b]])
            banks.give(bank, [t_a])
            x_ready[b] = [t_a]

        def finish_e(b):
            st = state_e[b]
            yield from finish_heads(b, [x for x, _ in st["accs"]], pe.last(), 0.0, eo, t_eo,
                                    st["xb"], st["t_xb"], [st["xt_last"]], route)

        for b in range(B):
            at(max(0, 4 + NH * b - 5), prelude_e(b))
            for h in range(NH):
                at(4 + NH * b + h, head_e(b, h))
            at(4 + NH * b + 4, place(state_e, b, []))
            at(4 + NH * b + NH + 4, finish_e(b))
        run()
        epart.close()
        part.close()
        t_e = fence()

        fpart = ExitStack()
        sbf = lambda name, shape, dt=F32: sb(name, shape, dt, fpart, "right")
        w1r_t = Turns([(i, sbf(f"w1raw{i}", [P, KC, HID])) for i in range(1)], t_e)
        w2r_t = Turns([(i, sbf(f"w2raw{i}", [P, FC, D])) for i in range(1)], t_e)
        w1_t = Turns([[sbf(f"w1_{n}{i}", [P, KC, HID], F32R) for n in ("hi", "lo")] for i in range(2)], t_e)
        w2_t = Turns([[sbf(f"w2_{n}{i}", [P, FC, D], F32R) for n in ("hi", "lo")] for i in range(2)], t_e)
        b1_sb = sbf("b1", [P, NE, FC])
        t_b1 = load("b1", b1_sb[:, :, :], a["F_b1"], t_e)
        gf_t = Turns([sbf(f"gf{i}", [P, SB]) for i in range(2)], t_e)
        gh_t = Turns([[sbf(f"gh_{n}{i}", [P, SB], F32R) for n in ("hi", "lo")] for i in range(4)], t_e)
        acc_ready = [x_ready[n // TT][0] for n in range(NT)]

        experts = {}

        def expert(e_):
            (i, raw), free = w1r_t.take()
            t_l = load(f"w1r{i}", raw[:, :, :], a["F_w1"][e_], free)
            (h1, l1), w_free = w1_t.take()
            (j, raw2), free2 = w2r_t.take()
            t_l2 = load(f"w2r{j}", raw2[:, :, :], a["F_w2"][e_], free2)
            (h2, l2), w2_free = w2_t.take()
            split = split_dve if e_ == 0 else split_pool
            t1, t2 = [], []
            for q in range(4):
                cols = slice(q * HID // 4, (q + 1) * HID // 4)
                t1.append(split(h1[:, :, cols], l1[:, :, cols], raw[:, :, cols], [t_l, *w_free]))
                ks = slice(q * FC // 4, (q + 1) * FC // 4)
                t2.append(split(h2[:, ks, :], l2[:, ks, :], raw2[:, ks, :], [t_l2, *w2_free]))
            w1r_t.give((i, raw), t1[-1])
            w2r_t.give((j, raw2), t2[-1])
            experts[e_] = ((h1, l1), t1, (h2, l2), t2)

        ybanks = {}
        expert(0)

        def moe_chunk(e_, s, fc):
            if s == 1 and fc == 0 and e_ + 1 < NE:
                expert(e_ + 1)
            (h1, l1), t1, (h2, l2), t2 = experts[e_]
            cols = slice(s * SB, (s + 1) * SB)
            need = [t for b in range(s * BPS, (s + 1) * BPS) for t in xt_ready[b]]
            fcols = slice(fc * P, (fc + 1) * P)
            bank, free = banks.take()
            t_mm = product(bank[:, :], [((h1[:, k, fcols], l1[:, k, fcols]), (xt_hi[:, k, cols], xt_lo[:, k, cols]))
                                        for k in range(KC)], [*need, *t1[fc // 2], *free])
            gf, gf_free = gf_t.take()
            t_g = act_do(gf[:, :], bank[:, :], ACT.Gelu, [t_mm, t_b1, *gf_free], bias=b1_sb[:, e_, fc:fc + 1])
            banks.give(bank, [t_g])
            (gh, gl), g_free = gh_t.take()
            ready = split_dve(gh[:, :], gl[:, :], gf[:, :], [t_g, *g_free])
            gf_t.give(gf, ready)
            if s == NSB - 1 and fc == FC - 1:
                w1_t.give((h1, l1), [t_mm])
            yield
            yield
            if fc == 0:
                ybanks[(e_, s)] = [banks.take() for _ in range(2)]
            ys = ybanks[(e_, s)]
            for t in range(SB // P):
                bank, free = ys[t // 2]
                o = bank[:, (t % 2) * D:(t % 2 + 1) * D]
                st = slice(t * P, (t + 1) * P)
                for i, (hh, ww) in enumerate(((gl, h2), (gh, l2), (gh, h2))):
                    mm = lambda e, o=o, st=st, hh=hh, ww=ww, i=i, t=t: e.matmul(
                        o, hh[:, st], ww[:, fc, :], start=(fc == 0 and i == 0 and t % 2 == 0),
                        stop=(fc == FC - 1 and i == 2), skip_group_check=True)
                    after = [*ready, *t2[fc // 2], *free] if i == 0 else ()
                    if i == 2 and t == SB // P - 1:
                        t_y = pe.do(mm, after)
                    else:
                        pe.quiet(mm, after)
            gh_t.give((gh, gl), [t_y])
            if fc < FC - 1:
                return
            if s == NSB - 1:
                w2_t.give((h2, l2), [t_y])
            for t in range(SB // P):
                bank, _ = ys[t // 2]
                n = s * (SB // P) + t
                acc_ready[n] = stt(x_tok[:, n, :], bank[:, (t % 2) * D:(t % 2 + 1) * D], gates[:, n, e_:e_ + 1],
                                   x_tok[:, n, :], ALU.mult, ALU.add, [t_y, acc_ready[n], *gates_ready[n // TT]])
                if t % 2:
                    banks.give(bank, [acc_ready[n]])
            if e_ == NE - 1:
                for b in range(s * BPS, (s + 1) * BPS):
                    yield from last_norm(b)

        def last_norm(b):
            yield from layernorm(b, x_tok[:, b * TT:(b + 1) * TT, :], [acc_ready[b * TT + t] for t in range(TT)],
                                 [], last=True)
            for t in range(TT):
                n = b * TT + t
                stored[0] += 16
                sp.do(lambda e, n=n: e.dma_start(out[n], x_tok[:, n, :]), x_ready[b], (out_sem, 16, stored[0]))

        stored = [0]
        i = 0
        for e_ in range(NE):
            for s in range(NSB):
                for fc in range(FC):
                    at(i, moe_chunk(e_, s, fc))
                    i += 1
        run()

        block = ctx.enter_context(nc.Block())

        @block.tensor
        def _(e):
            pe.play(e)

        @block.scalar
        def _(e):
            act.play(e)

        @block.vector
        def _(e):
            dve.play(e)

        @block.gpsimd
        def _(e):
            pool.play(e)

        @block.sync
        def _(e):
            sp.play(e)
            e.wait_ge(out_sem, stored[0])
        fpart.close()


def kernel(**inputs):
    import concourse.bacc as _bacc
    from concourse.bass_utils import run_bass_kernel_spmd as _run

    g = {k: np.asarray(v) for k, v in inputs.items()}

    def rows(w, n=P):
        return w.reshape(w.shape[0] // n, n, *w.shape[1:]).swapaxes(0, 1)

    def cols(v):
        return v.reshape(-1, P).T

    def wide(v):
        return np.broadcast_to(v, (P, v.shape[0]))

    def slots(w):
        w = w.reshape(*w.shape[:-1], NH, 1, DH)
        return np.broadcast_to(w, (*w.shape[:-2], 2, DH)).reshape(*w.shape[:-3], NH * 2 * DH)

    tri = np.tril(np.ones((P, P), np.float32))
    L0, L1 = "L0_", "L1_"
    w12 = np.stack([g[L0 + "ffn_w1_w"].T.reshape(KC, P, 4, 2, P), g[L0 + "ffn_w2_w"].T.reshape(KC, P, 4, 2, P)])
    w12 = w12.transpose(3, 2, 0, 4, 1, 5).reshape(4, P, CW)
    square = [g[L0 + f"ffn_{n}_w"].T.reshape(FC, P, FC, P).transpose(2, 1, 0, 3).reshape(FC, P, CW) for n in ("h1", "h2")]
    w3 = g[L0 + "ffn_w3_w"].T.reshape(2, 4, P, D).transpose(0, 2, 1, 3).reshape(2, P, CW)
    proj = np.zeros((P, NH // 2, 2, M), np.float32)
    for h in range(NH):
        r = h % (P // DH) * DH
        proj[r:r + DH, h // 2, h % 2, :] = g[L1 + "attn_proj"][h]
    laid = {
        "ident": np.eye(P, dtype=np.float32),
        "mask_a": np.concatenate([np.where(tri > 0, 0, MASKED), np.zeros((P, P)), np.where(tri > 0, 0, MASKED)], 1)
        .astype(np.float32),
        "mask_d": np.concatenate([tri.T, np.ones((P, P), np.float32), tri.T], 1),
        "low_rows": (np.arange(P) % 32 >= 16).astype(np.float32)[:, None],
        "iota8": np.broadcast_to(np.arange(NE, dtype=np.float32), (P, NE)),
        "x": rows(g["x"].reshape(B * S, D)),
        "xT": rows(g["x"].reshape(B * S, D).T),
        "ctxT": rows(g["ctx_768"].reshape(B * S, DC).T, CK),
        "A_wqkv": rows(g[L0 + "attn_W_qkv"]),
        "A_b": cols(g[L0 + "attn_b_qkv"]),
        "A_wconv": rows(g[L0 + "attn_W_vconv"]),
        "B_wv": rows(g[L0 + "xattn_Wv"].T),
        "B_wt": rows(g[L0 + "xattn_Wt"].T, CK),
        "B_b": np.stack([g[L0 + "xattn_bv"], g[L0 + "xattn_bt"]], 1),
        "C_w": np.concatenate([w12, *square, w3]),
        "C_s": np.stack([cols(g[L0 + f"ffn_{n}_s"]) for n in ("w1", "w2", "h1", "h2")], 1),
        "C_s3": wide(g[L0 + "ffn_w3_s"]),
        "D_w": rows(g[L1 + "attn_Wqkv"].T),
        "D_b": cols(g[L1 + "attn_bqkv"][:2 * D]),
        "D_bv": wide(g[L1 + "attn_bqkv"][2 * D:]),
        "D_wo": rows(g[L1 + "attn_Wout"].T),
        "D_bo": wide(g[L1 + "attn_bout"]),
        "D_proj": proj.reshape(P, NH // 2, P),
        "E_wq": rows(slots(g[L1 + "xattn_Wq"])),
        "E_wk": rows(slots(g[L1 + "xattn_Wk"]), CK),
        "E_b": np.concatenate([cols(slots(g[L1 + "xattn_bq"])), cols(slots(g[L1 + "xattn_bk"]))], 1),
        "E_wv": rows(g[L1 + "xattn_Wv"], CK),
        "E_bv": wide(g[L1 + "xattn_bv"]),
        "E_wo": rows(g[L1 + "xattn_Wo"]),
        "E_bo": wide(g[L1 + "xattn_bo"]),
        "gate_w": rows(g[L1 + "ffn_gate_w"]),
        "F_w1": g[L1 + "ffn_w1"].reshape(NE, KC, P, HID).transpose(0, 2, 1, 3),
        "F_w2": g[L1 + "ffn_w2"].reshape(NE, FC, P, D).transpose(0, 2, 1, 3),
        "F_b1": g[L1 + "ffn_b1"].reshape(NE, FC, P).transpose(2, 0, 1),
        "F_b2": g[L1 + "ffn_b2"],
    }
    nc = _bacc.Bacc("TRN2", target_bir_lowering=False, num_devices=1)
    arrays = {f"in_{k}": np.ascontiguousarray(v) for k, v in laid.items()}
    aps = {k: nc.dram_tensor(f"in_{k}", arrays[f"in_{k}"].shape, F32, kind="ExternalInput").ap() for k in laid}
    out = nc.dram_tensor("out_x", (NT, P, D), F32, kind="ExternalOutput").ap()
    build(nc, aps, out)
    r = _run(nc, [arrays], core_ids=[0])
    return r.results[0]["out_x"].reshape(B, S, D)
```

```python
from contextlib import ExitStack

import numpy as np

import concourse.bass as bass
from concourse import mybir

F32 = mybir.dt.float32
F32R = mybir.dt.float32r
U32 = mybir.dt.uint32
ALU = mybir.AluOpType
ACT = mybir.ActivationFunctionType
AX = mybir.AxisListType

P = 128
B, S, D = 8, 256, 256
DC = 192
TT = S // P
NT = B * TT
KC = D // P
CK = DC // 2
HID = 1024
FC = HID // P
NH, DH, M = 16, 16, 64
NE = 8
SB = 512
NSB = B * S // SB
BPS = SB // S
EPS_LN = 1e-5
DELTA = 1e-6
CLAMP = 10000.0
MASKED = -3.0e38
VW = 34
VH = 3
NVT = -(-NH // VH)
HPB = 2 * VH
NAB = -(-NVT // 2)
CW = 1024
TOPK = 2
BT = 256
XPB = B * S // BT
NBK = (TOPK * B * S - NE) // BT + NE
NONE = 1 << 20


class Engine:

    def __init__(self, sem):
        self.sem, self.count, self.queue = sem, 0, []

    def do(self, instruction, after=(), signal=None):
        if signal is None:
            self.count += 1
            signal = (self.sem, 1, self.count)
        self.queue.append((list(after), instruction, signal))
        return (signal[0], signal[2])

    def quiet(self, instruction, after=()):
        self.queue.append((list(after), instruction, None))

    def last(self):
        return (self.sem, self.count)

    def play(self, eng):
        seen = {}
        for after, instruction, signal in self.queue:
            for sem, value in after:
                if value > seen.get(id(sem), 0):
                    eng.wait_ge(sem, value)
                    seen[id(sem)] = value
            made = instruction(eng)
            if signal is not None:
                made.then_inc(signal[0], signal[1])


class Turns:

    def __init__(self, buffers, after=()):
        self.free = [(b, list(after)) for b in buffers]

    def take(self):
        return self.free.pop(0)

    def give(self, buffer, readers):
        self.free.append((buffer, list(readers)))


def build(nc, a, out):
    ctx = ExitStack()
    mid = ExitStack()
    early = ExitStack()
    late = ExitStack()
    with ctx:
        def sem(name):
            return ctx.enter_context(nc.semaphore(name))

        def sb(name, shape, dt=F32, scope=ctx, side="left"):
            return scope.enter_context(nc.sbuf_tensor(name, shape, dt, side=side))

        pe, act, dve, pool = (Engine(sem(f"s_{n}")) for n in ("pe", "act", "dve", "pool"))
        sp = Engine(None)
        out_sem = sem("s_out")
        banks = Turns([ctx.enter_context(nc.psum_tensor(f"bank{i}", [P, 512], F32)) for i in range(8)])

        loads = {}

        def load(name, dst, src, after=()):
            if name not in loads:
                loads[name] = [sem(f"l_{name}"), 0]
            loads[name][1] += 16
            return sp.do(lambda e: e.dma_start(dst, src), after, (loads[name][0], 16, loads[name][1]))

        def matmuls(terms, after=()):
            n = len(terms)
            for i, (o, st, mv, *own) in enumerate(terms):
                def mm(e, o=o, st=st, mv=mv, i=i):
                    return e.matmul(o, st, mv, start=(i == 0), stop=(i == n - 1))
                need = [*(after if i == 0 else ()), *(own[0] if own else ())]
                if i < n - 1:
                    pe.quiet(mm, need)
                else:
                    tok = pe.do(mm, need)
            return tok

        def product(o, pairs, after=()):
            terms = []
            for (sh, sl), (mh, ml), *own in pairs:
                terms += [(o, sl, mh, *own), (o, sh, ml), (o, sh, mh)]
            return matmuls(terms, after)

        def transposes(bank, parts, after=()):
            for i, (dst, src) in enumerate(parts):
                n = src.shape[0]
                fn = lambda e, dst=dst, src=src, n=n: e.transpose(dst, src, ident[0:n, 0:n])
                if i < len(parts) - 1:
                    pe.quiet(fn, after if i == 0 else ())
                else:
                    tok = pe.do(fn, after if i == 0 else ())
            return tok

        def act_do(o, i, func, after=(), **kw):
            return act.do(lambda e: e.activation(o, i, func, **kw), after)

        def tt(eng, o, x, y, op, after=()):
            return eng.do(lambda e: e.tensor_tensor(o, x, y, op), after)

        def ts(eng, o, x, s1, s2, op0, op1=None, after=()):
            if op1 is None:
                return eng.do(lambda e: e.tensor_scalar(o, x, s1, s2, op0), after)
            return eng.do(lambda e: e.tensor_scalar(o, x, s1, s2, op0, op1), after)

        def stt(o, x, s, y, op0, op1, after=(), **kw):
            return dve.do(lambda e: e.scalar_tensor_tensor(out=o, in0=x, scalar=s, in1=y, op0=op0, op1=op1, **kw),
                          after)

        def copy(eng, o, i, after=()):
            return eng.do(lambda e: e.tensor_copy(o, i), after)

        def f(ap):
            return ap.bitcast(F32)

        def split_bank(hi, lo, bank_ap, after):
            t_hi = act_do(hi, bank_ap, ACT.Identity, after)
            t_lo = tt(dve, lo, bank_ap, f(hi), ALU.subtract, [*after, t_hi])
            return [t_hi, t_lo]

        def split_biased(parts, after):
            for hi, lo, ps, bias in parts:
                t_hi = act_do(hi, ps, ACT.Identity, after, bias=bias)
            for hi, lo, ps, bias in parts:
                t_lo = stt(lo, ps, bias, f(hi), ALU.add, ALU.subtract, [*after, t_hi])
            return [t_hi, t_lo]

        def split_dve(hi, lo, x, after):
            t_hi = copy(dve, hi, x, after)
            t_lo = tt(dve, lo, x, f(hi), ALU.subtract, [t_hi])
            return [t_hi, t_lo]

        def split_pool(hi, lo, x, after):
            t_hi = ts(pool, hi, x, 1.0, 0.0, ALU.mult, ALU.add, after=after)
            t_lo = tt(pool, lo, x, f(hi), ALU.subtract, [t_hi])
            return [t_hi, t_lo]

        def fence():
            return [x.last() for x in (pe, act, dve, pool)]

        x_tok = sb("x_tok", [P, NT, D])
        ident = sb("ident", [P, P])
        ones = sb("ones", [P, P])
        ln_stats = sb("ln_stats", [P, 2, TT, 6])
        ln_mv = sb("ln_mv", [P, 2, TT, 2])
        ln_rstd = sb("ln_rstd", [P, 2, TT])
        minus_half = sb("minus_half", [P, 4])
        gw_raw = sb("gw_raw", [P, KC, NE])
        b2_sb = sb("b2", [NE, D])
        iota8 = sb("iota8", [P, NE])
        shares = sb("shares", [P, NT, TOPK])
        before = sb("before", [P, P])
        seen = sb("seen", [P, NE])
        codes = sb("codes", [P, NT, TOPK], U32)
        block_no = sb("block_no", [P, NBK])
        row_no = sb("row_no", [P, 1])
        none_t = sb("none", [P, (NE * B * S + BT) // P], U32)
        xt_hi = sb("xt_hi", [P, KC, B * S], F32R, mid)
        xt_lo = sb("xt_lo", [P, KC, B * S], F32R, mid)
        r_bufs = Turns([sb(f"resid{i}", [P, TT, D], F32, mid) for i in range(3)])
        mask_a = sb("mask_a", [P, 3 * P], F32, mid)
        ctx_raw = Turns([(i, sb(f"ctx_raw{i}", [CK, 2, S], F32, mid)) for i in range(2)])
        ctx_t = Turns([[sb(f"ctx_{n}{i}", [CK, 2, S], F32R, mid) for n in ("hi", "lo")] for i in range(2)])

        x_rows = nc.dram_tensor("x_rows", (B * S, D), F32, kind="Internal").ap()
        y_rows = nc.dram_tensor("y_rows", (TOPK * B * S, D), F32, kind="Internal").ap()
        slot_codes = nc.dram_tensor("slot_codes", (NE * B * S + BT, 1), U32, kind="Internal").ap()
        dram_sems = {}

        def signal_for(name):
            if name not in dram_sems:
                dram_sems[name] = [sem(f"w_{name}"), 0]
            dram_sems[name][1] += 16
            return (dram_sems[name][0], 16, dram_sems[name][1])

        def xt(buf, b, c):
            return buf[:, c, b * S:(b + 1) * S]

        def xt_tile(b, t):
            c0 = b * S + t * P
            return [(xt_hi[:, c, c0:c0 + P], xt_lo[:, c, c0:c0 + P]) for c in range(KC)]

        x_ready = [None] * B
        xt_ready = [None] * B
        ln_turn = [0]
        ln_readers = [[], []]

        def layernorm(b, r, r_ready, xt_readers, last=False):
            i = ln_turn[0] % 2
            ln_turn[0] += 1
            for t in range(TT):
                t_st = dve.do(lambda e, t=t: e.bn_stats(ln_stats[:, i, t, :], r[:, t, :]), r_ready if t == 0 else ())
            for t in range(TT):
                t_mv = dve.do(lambda e, t=t: e.bn_aggr(ln_mv[:, i, t, :], ln_stats[:, i, t, :]),
                              [t_st, *ln_readers[i]])
            t_ve = ts(dve, ln_rstd[:, i, :], ln_mv[:, i, :, 1], EPS_LN, None, ALU.add, after=[t_mv])
            t_rs = tt(pool, ln_rstd[:, i, :], ln_rstd[:, i, :], minus_half[:, 0:TT], ALU.pow, [t_ve, t_const])
            yield
            if last:
                t_s = stt(ln_mv[:, i, :, 0], ln_mv[:, i, :, 0], -1.0, ln_rstd[:, i, :], ALU.mult, ALU.mult, [t_rs])
                for t in range(TT):
                    t_x = act_do(x_tok[:, b * TT + t, :], r[:, t, :], ACT.Identity, [t_s],
                                 scale=ln_rstd[:, i, t:t + 1], bias=ln_mv[:, i, t, 0:1])
                x_ready[b] = ln_readers[i] = [t_x]
                return
            for t in range(TT):
                t_x = ts(dve, x_tok[:, b * TT + t, :], r[:, t, :], ln_mv[:, i, t, 0:1], ln_rstd[:, i, t:t + 1],
                         ALU.subtract, ALU.mult, after=[t_rs])
            x_ready[b] = [t_x]
            r_bufs.give(r, [t_x])
            yield
            bank, free = banks.take()
            t_tr = transposes(bank, [(bank[:, c * S + t * P:c * S + (t + 1) * P],
                                      x_tok[:, b * TT + t, c * P:(c + 1) * P])
                                     for c in range(KC) for t in range(TT)], [t_x, t_const, *free])
            hi = xt_hi[:, :, b * S:(b + 1) * S]
            lo = xt_lo[:, :, b * S:(b + 1) * S]
            done = split_bank(hi, lo, bank[:, :].rearrange("p (c t) -> p c t", c=KC), [t_tr, *xt_readers])
            xt_ready[b] = done
            banks.give(bank, done)

        staging_t = Turns([(i, sb(f"staging{i}", [P, KC * 3 * D], F32, mid)) for i in range(2)])

        def weights(split, hi, lo, source, after=()):
            (i, raw), free = staging_t.take()
            n = int(np.prod(source.shape[1:]))
            raw_view = raw[0:source.shape[0], 0:n].rearrange("p (a b) -> p a b", a=source.shape[1])
            t_l = load(f"staging{i}", raw_view, source, free)
            toks = split(hi, lo, raw_view, [t_l, *after])
            staging_t.give((i, raw), toks)
            return toks

        plan = []

        def at(round_, gen):
            plan.append((round_, len(plan), gen))

        t_ident = load("ident", ident[:, :], a["ident"])
        t_mask_a = load("mask_a", mask_a[:, :], a["mask_a"])
        t_const = pool.do(lambda e: e.memset(minus_half[:, :], -0.5))
        t_const_ident = t_ident
        t_rt = [load("gw", gw_raw[:, :, :], a["gate_w"]), load("b2", b2_sb[:, :], a["F_b2"]),
                load("iota8", iota8[:, :], a["iota8"]), load("before", before[:, :], a["before"]),
                load("codes", codes[:, :, :], a["codes"]), load("block_no", block_no[:, :], a["block_no"]),
                load("row_no", row_no[:, :], a["row_no"]), pool.do(lambda e: e.memset(seen[:, :], 0.0))]
        t_none = pool.do(lambda e: e.memset(none_t[:, :], NONE))
        t_empty = sp.do(lambda e: e.dma_start(slot_codes.rearrange("(p n) one -> p (n one)", p=P), none_t[:, :]),
                        [t_none], signal_for("empty"))

        xraw = Turns([sb(f"xraw{i}", [P, KC, S], F32, early) for i in range(2)])
        wqkv = [sb(f"wqkv_{n}", [P, KC, 3 * D], F32R, early) for n in ("hi", "lo")]
        bqkv = sb("bqkv", [P, 6], F32, early)
        wconv = sb("wconv", [P, KC, 3], F32, early)
        t_bc = [load("a_bias", bqkv[:, :], a["A_b"]), load("a_conv", wconv[:, :, :], a["A_wconv"])]

        def load_x(b):
            buf, free = xraw.take()
            t_l = load(f"xT{b % 2}", buf[:, :, :], a["xT"][:, :, b * S:(b + 1) * S], free)
            t_x = load(f"x{b % 2}", x_tok[:, b * TT:(b + 1) * TT, :], a["x"][:, b * TT:(b + 1) * TT, :])
            x_ready[b] = [t_x]
            hi = xt_hi[:, :, b * S:(b + 1) * S]
            lo = xt_lo[:, :, b * S:(b + 1) * S]
            xt_ready[b] = (split_dve if b < 2 else split_pool)(hi, lo, buf[:, :, :], [t_l])
            xraw.give(buf, xt_ready[b])
            return
            yield

        at(0, load_x(0))
        t_wq = []

        def split_wqkv():
            t_wq.extend(weights(split_dve, wqkv[0][:, :, :], wqkv[1][:, :, :], a["A_wqkv"]))
            return
            yield
        at(0, split_wqkv())
        for b in range(1, B):
            at(max(0, b - 2), load_x(b))

        qa = [[sb(f"qa_{n}{i}", [P, KC, S], F32R, early) for n in ("hi", "lo")] for i in range(2)]
        ka = [[sb(f"ka_{n}{i}", [P, KC, S], F32R, early) for n in ("hi", "lo")] for i in range(2)]
        qa_t, ka_t = Turns(qa), Turns(ka)
        vpad_t = Turns([sb(f"vpad{i}", [P, KC, S + 2], F32, early) for i in range(2)])
        ucv_t = Turns([(sb(f"uT{i}", [P, KC, S], F32, early), sb(f"cT{i}", [P, KC, S], F32, early)) for i in range(2)])
        utok_t = Turns([sb(f"utok{i}", [P, TT, D], F32, early) for i in range(2)])
        ctok_t = Turns([[sb(f"ctok_{n}{i}", [P, TT, D], F32R, early) for n in ("hi", "lo")] for i in range(2)])
        sm_t = Turns([sb(f"scoreA{i}", [P, 3 * P], F32, early) for i in range(2)])
        pa_t = Turns([sb(f"probA{i}", [P, 3 * P], F32, early) for i in range(2)])
        pta_t = Turns([[sb(f"probTA_{n}{i}", [P, 3 * P], F32R, early) for n in ("hi", "lo")] for i in range(2)])
        sma_t = Turns([sb(f"smallA{i}", [P, 16], F32, early) for i in range(3)])
        junk_a = sb("junkA", [P, P], F32, early)
        t_vz = [pool.do(lambda e, v=v: e.memset(v[:, :, :], 0.0)) for v, _ in vpad_t.free]
        scale_a = float(D) ** -0.5

        def attention_a(b):
            (qh, ql), q_free = qa_t.take()
            (kh, kl), k_free = ka_t.take()
            vp, v_free = vpad_t.take()
            (uT, cT), uc_free = ucv_t.take()
            need = [*xt_ready[b], *t_wq, *t_bc]
            done = []
            for which in range(3):
                bank, free = banks.take()
                for c in range(KC):
                    col = (which * KC + c) * P
                    t_mm = product(bank[:, c * S:(c + 1) * S],
                                   [((wqkv[0][:, k, col:col + P], wqkv[1][:, k, col:col + P]),
                                     (xt(xt_hi, b, k), xt(xt_lo, b, k))) for k in range(KC)],
                                   [*need, *free])
                halves = [(bank[:, c * S:(c + 1) * S], bqkv[:, which * KC + c:which * KC + c + 1]) for c in range(KC)]
                if which < 2:
                    hi, lo = ((qh, ql), (kh, kl))[which]
                    reads = split_biased([(hi[:, c, :], lo[:, c, :], *halves[c]) for c in range(KC)],
                                         [t_mm, *t_bc, *(q_free, k_free)[which]])
                else:
                    reads = [act_do(vp[:, c, 1:S + 1], ps, ACT.Identity, [t_mm, *t_vz, *v_free], bias=bias)
                             for c, (ps, bias) in enumerate(halves)]
                banks.give(bank, reads)
                done.append(reads)
            t_v = done[2]
            t_proj = t_mm
            t_c = []
            for c in range(KC):
                w = [wconv[:, c, j:j + 1] for j in range(3)]
                t_u = ts(pool, uT[:, c, :], vp[:, c, 2:S + 2], w[2], 1.0, ALU.mult, ALU.mult, after=[*t_v, *uc_free])
                t_1 = stt(cT[:, c, :], vp[:, c, 0:S], w[0], uT[:, c, :], ALU.mult, ALU.add, [t_u])
                t_c.append(stt(cT[:, c, :], vp[:, c, 1:S + 1], w[1], cT[:, c, :], ALU.mult, ALU.add, [t_1]))
            vpad_t.give(vp, t_c)
            yield
            bank, free = banks.take()
            t_s = product(bank[:, 0:P], [((qh[:, k, 0:P], ql[:, k, 0:P]), (kh[:, k, 0:P], kl[:, k, 0:P]))
                                         for k in range(KC)], [*done[0], *done[1], *free])
            t_s = product(bank[:, P:3 * P], [((qh[:, k, P:S], ql[:, k, P:S]), (kh[:, k, :], kl[:, k, :]))
                                             for k in range(KC)])
            qa_t.give((qh, ql), [t_s])
            ka_t.give((kh, kl), [t_s])
            bank_c, free_c = banks.take()
            t_ct = transposes(bank_c, [(bank_c[:, t * D + c * P:t * D + (c + 1) * P], cT[:, c, t * P:(t + 1) * P])
                                       for t in range(TT) for c in range(KC)], [*t_c, t_const_ident, *free_c])
            bank_u, free_u = banks.take()
            t_ut = transposes(bank_u, [(bank_u[:, t * D + c * P:t * D + (c + 1) * P], uT[:, c, t * P:(t + 1) * P])
                                       for t in range(TT) for c in range(KC)], free_u)
            ucv_t.give((uT, cT), [t_ut])
            sm, sm_free = sm_t.take()
            pr, pr_free = pa_t.take()
            small, small_free = sma_t.take()
            t_m = tt(dve, sm[:, :], bank[:, 0:3 * P], mask_a[:, :], ALU.add, [t_s, t_mask_a, *sm_free])
            banks.give(bank, [t_m])
            mx, nmx, den, dia, rin, ndg = (small[:, 2 * j:2 * j + 2] for j in range(6))
            dve.do(lambda e: e.tensor_reduce(mx[:, 0:1], sm[:, 0:P], AX.X, ALU.max), [t_m, *small_free])
            t_mx = dve.do(lambda e: e.tensor_reduce(mx[:, 1:2], sm[:, P:3 * P], AX.X, ALU.max))
            t_nm = ts(dve, nmx, mx, -scale_a, None, ALU.mult, after=[t_mx])
            act_do(pr[:, 0:P], sm[:, 0:P], ACT.Exp, [t_nm, *pr_free], scale=scale_a, bias=nmx[:, 0:1],
                   accum_out=den[:, 0:1])
            t_p = act_do(pr[:, P:3 * P], sm[:, P:3 * P], ACT.Exp, scale=scale_a, bias=nmx[:, 1:2],
                         accum_out=den[:, 1:2])
            sm_t.give(sm, [t_p])
            (ch, cl), c_free = ctok_t.take()
            t_cs = split_bank(ch[:, :, :], cl[:, :, :], bank_c[:, :].rearrange("p (t d) -> p t d", t=TT),
                              [t_ct, *c_free])
            banks.give(bank_c, t_cs)
            utok, u_free = utok_t.take()
            t_uc = act_do(utok[:, :, :], bank_u[:, :].rearrange("p (t d) -> p t d", t=TT), ACT.Identity,
                          [t_ut, *u_free])
            banks.give(bank_u, [t_uc])
            diag_cols = (slice(0, P), slice(2 * P, 3 * P))
            t_j = None
            for t in range(TT):
                t_j = stt(junk_a[:, :], pr[:, diag_cols[t]], 1.0, ident[:, :], ALU.mult, ALU.mult,
                          [t_p, t_const_ident] if t_j is None else [t_j], accum_out=dia[:, t:t + 1])
            t_ri = dve.do(lambda e: e.reciprocal(rin, den), [t_p])
            t_nd = stt(ndg, dia, -1.0, rin, ALU.mult, ALU.mult, [t_ri, t_j])
            yield
            bank, free = banks.take()
            t_t = transposes(bank, [(bank[:, j * P:(j + 1) * P], pr[:, j * P:(j + 1) * P]) for j in range(3)],
                             [t_p, *free])
            pa_t.give(pr, [t_t, t_j])
            (ph, pl), p_free = pta_t.take()
            t_ps = split_bank(ph[:, :], pl[:, :], bank[:, 0:3 * P], [t_t, *p_free])
            banks.give(bank, t_ps)
            yield
            bank, free = banks.take()
            t_o = product(bank[:, 0:D], [((ph[:, 0:P], pl[:, 0:P]), (ch[:, 0, :], cl[:, 0, :]))],
                          [*t_ps, *t_cs, *free])
            t_o = product(bank[:, D:2 * D], [((ph[:, (1 + j) * P:(2 + j) * P], pl[:, (1 + j) * P:(2 + j) * P]),
                                              (ch[:, j, :], cl[:, j, :])) for j in range(TT)])
            pta_t.give((ph, pl), [t_o])
            ctok_t.give((ch, cl), [t_o])
            r, r_free = r_bufs.take()
            for t in range(TT):
                t_r = stt(r[:, t, :], bank[:, t * D:(t + 1) * D], rin[:, t:t + 1], x_tok[:, b * TT + t, :],
                          ALU.mult, ALU.add, [t_o, t_ri, *x_ready[b], *r_free])
                t_r2 = stt(r[:, t, :], utok[:, t, :], ndg[:, t:t + 1], r[:, t, :], ALU.mult, ALU.add,
                           [t_r, t_nd, t_uc])
            banks.give(bank, [t_r])
            utok_t.give(utok, [t_r2])
            sma_t.give(small, [t_r2])
            yield from layernorm(b, r, [t_r2], [t_proj])

        for b in range(B):
            at(1 + b, attention_a(b))

        wv_b = [sb(f"bwv_{n}", [P, KC, P], F32R, early) for n in ("hi", "lo")]
        wt_b = [sb(f"bwt_{n}", [CK, 2, P], F32R, early) for n in ("hi", "lo")]
        b_bias = sb("b_bias", [P, 2], F32, early)
        t_ones = pool.do(lambda e: e.memset(ones[:, :], 1.0))
        t_bb = load("b_bias", b_bias[:, :], a["B_b"])
        t_bw = []

        def weights_b():
            t_bw.extend(weights(split_pool, wv_b[0][:, :, :], wv_b[1][:, :, :], a["B_wv"]))
            t_bw.extend(weights(split_pool, wt_b[0][:, :, :], wt_b[1][:, :, :], a["B_wt"]))
            return
            yield
        at(2, weights_b())

        def load_context(b):
            (i, raw), free = ctx_raw.take()
            t_l = load(f"ctx{i}", raw[:, :, :], a["ctxT"][:, :, b * S:(b + 1) * S], free)
            (hi, lo), c_free = ctx_t.take()
            toks = split_pool(hi[:, :, :], lo[:, :, :], raw[:, :, :], [t_l, *c_free])
            ctx_raw.give((i, raw), toks)
            return (hi, lo), toks

        vt_t = Turns([[sb(f"vt_{n}{i}", [P, 2, S], F32R, early) for n in ("hi", "lo")] for i in range(4)])
        sq_t = Turns([sb(f"sq{i}", [P, 2, S], F32, early) for i in range(2)])
        rn_t = Turns([sb(f"rn{i}", [P, 4], F32, early) for i in range(4)])
        dg_t = Turns([sb(f"dgt{i}", [P, TT, P], F32, early) for i in range(2)])
        rec_t = Turns([sb(f"recB{i}", [P, TT, S], F32, early) for i in range(2)])

        def cosine_b(b):
            (cxh, cxl), t_cx = load_context(b)
            yield
            bank, free = banks.take()
            t_v = product(bank[:, 0:S], [((wv_b[0][:, k, :], wv_b[1][:, k, :]), (xt(xt_hi, b, k), xt(xt_lo, b, k)))
                                         for k in range(KC)], [*xt_ready[b], *t_bw, *free])
            t_t = product(bank[:, S:2 * S], [((wt_b[0][:, k, :], wt_b[1][:, k, :]), (cxh[:, k, :], cxl[:, k, :]))
                                             for k in range(2)], t_cx)
            ctx_t.give((cxh, cxl), [t_t])
            (vh, vl), vt_free = vt_t.take()
            sq, sq_free = sq_t.take()
            halves = [(bank[:, i * S:(i + 1) * S], b_bias[:, i:i + 1]) for i in range(2)]
            for i, (ps, bias) in enumerate(halves):
                t_q = act_do(sq[:, i, :], ps, ACT.Square, [t_t, t_bb, *sq_free], bias=bias)
            toks = [t_q, *split_biased([(vh[:, i, :], vl[:, i, :], *halves[i]) for i in range(2)], [t_t, *vt_free])]
            banks.give(bank, toks)
            yield
            bank, free = banks.take()
            for i in range(2):
                for t in range(TT):
                    j = i * TT + t
                    t_n = matmuls([(bank[:, j:j + 1], sq[:, i, t * P:(t + 1) * P], ones[:, 0:1])],
                                  [*toks, t_ones, *free])
            sq_t.give(sq, [t_n])
            rn, rn_free = rn_t.take()
            t_rn = copy(dve, rn[:, :], bank[:, 0:4], [t_n, *rn_free])
            banks.give(bank, [t_rn])
            t_rn = tt(pool, rn[:, :], rn[:, :], minus_half[:, :], ALU.pow, [t_rn, t_const])
            yield
            dgt, dg_free = dg_t.take()
            for t in range(TT):
                t_d = ts(dve, dgt[:, t, :], ident[:, :], rn[:, TT + t:TT + t + 1], None, ALU.mult,
                         after=[t_rn, t_const_ident, *dg_free])
            yield
            bank_r, free = banks.take()
            for t in range(TT):
                t_r = matmuls([(bank_r[:, t * P:(t + 1) * P], ones[:, :], dgt[:, t, :])], [t_d, *free])
            dg_t.give(dgt, [t_r])
            bank, free = banks.take()
            for t in range(TT):
                t_dot = product(bank[:, t * S:(t + 1) * S],
                                [((vh[:, 0, t * P:(t + 1) * P], vl[:, 0, t * P:(t + 1) * P]), (vh[:, 1, :], vl[:, 1, :]))],
                                free)
            vt_t.give((vh, vl), [t_dot])
            rec, rec_free = rec_t.take()
            r, r_free = r_bufs.take()
            for t in range(TT):
                t_rec = ts(dve, rec[:, t, :], bank_r[:, 0:S], rn[:, t:t + 1], 1e8, ALU.mult, ALU.min,
                           after=[t_r, *rec_free])
            banks.give(bank_r, [t_rec])
            rn_t.give(rn, [t_rec])
            t_m = tt(dve, rec[:, :, :], bank[:, :].rearrange("p (t s) -> p t s", t=TT), rec[:, :, :], ALU.mult,
                     [t_dot, t_rec])
            banks.give(bank, [t_m])
            t_add = tt(dve, r[:, :, :], rec[:, :, :], x_tok[:, b * TT:(b + 1) * TT, :], ALU.add,
                       [t_m, *x_ready[b], *r_free])
            rec_t.give(rec, [t_add])
            yield from layernorm(b, r, [t_add], [t_v])

        first_b = 6
        for b in range(B):
            at(first_b + b, cosine_b(b))

        def run():
            todo = sorted(plan)
            plan.clear()
            live, r = [], 0
            while todo or live:
                while todo and todo[0][0] <= r:
                    live.append(todo.pop(0)[2])
                live = [g for g in live if next(g, "end") != "end"]
                r += 1

        run()
        early.close()
        t_early = fence()
        NPIECE = 4 + 8 + 8 + 2
        wraw_t = Turns([(i, sb(f"wraw{i}", [P, CW], F32, late, "right")) for i in range(3)], t_early)
        wpiece_t = Turns([[sb(f"wpiece_{n}{i}", [P, CW], F32R, late, "right") for n in ("hi", "lo")] for i in range(3)], t_early)
        hid = [[sb(f"hid{i}_{n}", [P, FC, SB], F32R, late, "right") for n in ("hi", "lo")] for i in range(2)]
        hf_t = Turns([sb(f"hf{i}", [P, SB], F32, late, "right") for i in range(2)], t_early)
        sg_t = Turns([sb(f"sg{i}", [P, SB], F32, late, "right") for i in range(2)], t_early)
        scl = sb("ffn_scales", [P, 4, FC], F32, late, "right")
        s3b = sb("ffn_s3", [P, D], F32, late, "right")
        t_scl = [load("ffn_s", scl[:, :, :], a["C_s"], t_early), load("ffn_s3", s3b[:, :], a["C_s3"], t_early)]

        pieces = {}

        def piece(sbk, n):
            (i, raw), free = wraw_t.take()
            t_l = load(f"piece{i}", raw[:, :], a["C_w"][n], free)
            (hi, lo), w_free = wpiece_t.take()
            toks = split_pool(hi[:, :], lo[:, :], raw[:, :], [t_l, *w_free])
            wraw_t.give((i, raw), toks)
            pieces[(sbk, n)] = ((hi, lo), toks)

        def ffn():
            order = [(s, n) for s in range(NSB) for n in range(NPIECE)]
            ahead = [0]

            def want():
                if ahead[0] < len(order) and len(wpiece_t.free) and len(wraw_t.free):
                    piece(*order[ahead[0]])
                    ahead[0] += 1

            want(), want()
            hid_readers = [t_early, t_early]
            for s in range(NSB):
                cols = slice(s * SB, (s + 1) * SB)
                seqs = range(s * BPS, (s + 1) * BPS)
                x_in = [(xt_hi[:, k, cols], xt_lo[:, k, cols]) for k in range(KC)]
                need = [t for b in seqs for t in xt_ready[b]]
                chunk_ready = []
                for n in range(4):
                    want()
                    (wh, wl), t_w = pieces.pop((s, n))
                    for oo in range(2):
                        o = 2 * n + oo
                        pair = []
                        for mat in range(2):
                            bank, free = banks.take()
                            terms = []
                            for k in range(KC):
                                c0 = ((mat * 2 + oo) * KC + k) * P
                                terms.append(((wh[:, c0:c0 + P], wl[:, c0:c0 + P]), x_in[k]))
                            t_mm = product(bank[:, :], terms, [*need, *t_w, *free])
                            pair.append((bank, t_mm))
                        sg, sg_free = sg_t.take()
                        hf, hf_free = hf_t.take()
                        t_sg = act_do(sg[:, :], pair[0][0][:, :], ACT.Silu, [pair[0][1], *t_scl, *sg_free],
                                      scale=scl[:, 0, o:o + 1])
                        banks.give(pair[0][0], [t_sg])
                        t_h = stt(hf[:, :], pair[1][0][:, :], scl[:, 1, o:o + 1], sg[:, :], ALU.mult, ALU.mult,
                                  [pair[1][1], t_sg, *t_scl, *hf_free])
                        banks.give(pair[1][0], [t_h])
                        sg_t.give(sg, [t_h])
                        toks = split_dve(hid[0][0][:, o, :], hid[0][1][:, o, :], hf[:, :], [t_h, *hid_readers[0]])
                        hf_t.give(hf, toks)
                        chunk_ready.append(toks)
                    wpiece_t.give((wh, wl), [t_mm])
                for layer in range(2):
                    src, dst = hid[layer % 2], hid[(layer + 1) % 2]
                    new_ready = []
                    for o in range(FC):
                        want()
                        (wh, wl), t_w = pieces.pop((s, 4 + layer * FC + o))
                        bank, free = banks.take()
                        for k in range(FC):
                            for i3, (ww, hh) in enumerate(((wl, src[0]), (wh, src[1]), (wh, src[0]))):
                                first, final = k == 0 and i3 == 0, k == FC - 1 and i3 == 2
                                mm = lambda e, ww=ww, hh=hh, k=k, first=first, final=final, bank=bank: e.matmul(
                                    bank[:, :], ww[:, k * P:(k + 1) * P], hh[:, k, :], start=first, stop=final)
                                after = (*chunk_ready[k], *t_w, *free) if i3 == 0 else ()
                                if final:
                                    t_mm = pe.do(mm, after)
                                else:
                                    pe.quiet(mm, after)
                        wpiece_t.give((wh, wl), [t_mm])
                        hf, hf_free = hf_t.take()
                        t_g = act_do(hf[:, :], bank[:, :], ACT.Gelu, [t_mm, *t_scl, *hf_free],
                                     scale=scl[:, 2 + layer, o:o + 1])
                        banks.give(bank, [t_g])
                        toks = split_dve(dst[0][:, o, :], dst[1][:, o, :], hf[:, :],
                                         [t_g, *hid_readers[(layer + 1) % 2]])
                        hf_t.give(hf, toks)
                        new_ready.append(toks)
                    hid_readers[layer % 2] = [t_mm]
                    chunk_ready = new_ready
                src = hid[0]
                want(), want()
                halves = [pieces.pop((s, NPIECE - 2 + j)) for j in range(2)]
                for bi, b in enumerate(seqs):
                    bank, free = banks.take()
                    for t in range(TT):
                        c0 = bi * S + t * P
                        terms = []
                        need3 = [*free]
                        for k in range(FC):
                            (wh, wl), t_w = halves[k // 4]
                            w0 = (k % 4) * D
                            terms.append(((src[0][:, k, c0:c0 + P], src[1][:, k, c0:c0 + P]),
                                          (wh[:, w0:w0 + D], wl[:, w0:w0 + D])))
                            need3 += [*t_w, *chunk_ready[k]]
                        t_mm = product(bank[:, t * D:(t + 1) * D], terms, need3)
                    r, r_free = r_bufs.take()
                    for t in range(TT):
                        t_y = tt(dve, r[:, t, :], bank[:, t * D:(t + 1) * D], s3b[:, :], ALU.mult,
                                 [t_mm, *t_scl, *r_free])
                    banks.give(bank, [t_y])
                    t_r = tt(dve, r[:, :, :], r[:, :, :], x_tok[:, b * TT:(b + 1) * TT, :], ALU.add,
                             [t_y, *x_ready[b]])
                    yield from layernorm(b, r, [t_r], [t_mm])
                for (wh, wl), _ in halves:
                    wpiece_t.give((wh, wl), [t_mm])
                hid_readers[0] = [t_mm]

        at(0, ffn())
        run()
        late.close()

        t_late = fence()
        part = ExitStack()
        sbp = lambda name, shape, dt=F32, scope=part, side="left": sb(name, shape, dt, scope, side)
        v_heads = sbp("v_heads", [P, TT, NH, P], F32R)
        acc_sb_t = Turns([sbp(f"accT{i}", [P, 2, S]) for i in range(3)])
        ctok2_t = Turns([sbp(f"ctxtok{i}", [P, TT, D]) for i in range(2)])
        rin_t = Turns([sbp(f"crin{i}", [P, TT * HPB]) for i in range(2)])
        cT_t = Turns([[sbp(f"ctxT_{n}{i}", [P, KC, S], F32R) for n in ("hi", "lo")] for i in range(1)])
        sum_t = Turns([sbp(f"csum{i}", [P, TT * HPB, DH]) for i in range(2)])
        vf_t = Turns([sbp(f"vf{i}", [P, TT, D]) for i in range(2)])
        xb_t = Turns([sbp(f"xb{i}", [P, TT, D]) for i in range(2)])
        t_z = pool.do(lambda e: e.memset(f(v_heads[:, :, :, :]), 0.0), t_late)
        for g in range(VH):
            heads = v_heads[:, :, g::VH, g * VW + 2 * DH:g * VW + 2 * DH + 1]
            t_z = pool.do(lambda e, heads=heads: e.memset(f(heads), 1.0), [t_z])
        v_readers = [[t_z] for _ in range(NVT)]

        def place(state, b, i):
            st = state[b]
            n = min(VH, NH - i * VH)
            step = P + VW if n > 1 else P
            cols = v_heads[:, :, :, :].rearrange("p t h c -> p t (h c)")[:, :, i * VH * P:i * VH * P + n * step]
            cols = cols.rearrange("p t (h c) -> p t h c", h=n)
            hi, lo = cols[:, :, :, 0:DH], cols[:, :, :, DH:2 * DH]
            src = st["vf"][:, :, i * VH * DH:(i * VH + n) * DH].rearrange("p t (h d) -> p t h d", h=n)
            st["v_ready"][i] = split_pool(hi, lo, src, [st["t_vf"], *v_readers[i]])
            if i == NVT - 1:
                vf_t.give(st["vf"], [pool.last()])
            return
            yield

        def drain(state, b, i, delta):
            st = state[b]
            bank, t_acc = st["accs"][i]
            acc_sb, s_free = acc_sb_t.take()
            t_e = act_do(acc_sb[:, :, :], bank[:, :].rearrange("p (j s) -> p j s", j=2), ACT.Identity,
                         [t_acc, *s_free])
            banks.give(bank, [t_e])
            yield
            if i == 0:
                st["ctok"], st["ctok_free"] = ctok2_t.take()
            h0, nh = HPB * i, min(HPB, NH - HPB * i)
            bank, free = banks.take()
            parts = []
            for t in range(TT):
                for j in range(2):
                    rows = VW * min(VH, NH - (2 * i + j) * VH)
                    c0 = (t * nh + j * VH) * VW
                    parts.append((bank[:, c0:c0 + rows], acc_sb[0:rows, j, t * P:(t + 1) * P]))
            t_tr = transposes(bank, parts, [t_e, *free])
            acc_sb_t.give(acc_sb, [t_tr])
            csum, cs_free = sum_t.take()
            rin, ri_free = rin_t.take()
            n = TT * nh
            view = bank[:, 0:n * VW].rearrange("p (h w) -> p h w", w=VW)
            hi_lo = view[:, :, 0:2 * DH].rearrange("p h (two d) -> p h d two", two=2)
            t_sum = dve.do(lambda e: e.tensor_reduce(csum[:, 0:n, :], hi_lo, AX.X, ALU.add), [t_tr, *cs_free])
            t_den = ts(dve, rin[:, 0:n], view[:, :, 2 * DH], delta, None, ALU.add, after=[t_tr, *ri_free])
            banks.give(bank, [t_sum, t_den])
            t_ri = dve.do(lambda e: e.reciprocal(rin[:, 0:n], rin[:, 0:n]), [t_den])
            t_ct = tt(dve, st["ctok"][:, :, h0 * DH:(h0 + nh) * DH].rearrange("p t (h d) -> p t h d", h=nh),
                      csum[:, 0:n, :].rearrange("p (t h) d -> p t h d", t=TT),
                      rin[:, 0:n].rearrange("p (t h) -> p t h", t=TT)[:, :, :, None].to_broadcast([P, TT, nh, DH]),
                      ALU.mult, [t_ri, t_sum, *st["ctok_free"]])
            sum_t.give(csum, [t_ct])
            rin_t.give(rin, [t_ct])
            st["t_ct"] = t_ct

        def finish_heads(b, st, wo, bo, t_wo, then=None):
            ctok, t_ct, xt_readers = st["ctok"], st["t_ct"], [st["xt_last"]]
            xb, xb_free = xb_t.take()
            for t in range(TT):
                t_xb = tt(pool, xb[:, t, :], x_tok[:, b * TT + t, :], bo[:, :], ALU.add, [*x_ready[b], *t_wo, *xb_free])
            bank, free = banks.take()
            t_tr = transposes(bank, [(bank[:, c * S + t * P:c * S + (t + 1) * P], ctok[:, t, c * P:(c + 1) * P])
                                     for c in range(KC) for t in range(TT)], [t_ct, *free])
            ctok2_t.give(ctok, [t_tr])
            (ch, cl), ct_free = cT_t.take()
            t_cs = split_bank(ch[:, :, :], cl[:, :, :], bank[:, :].rearrange("p (c s) -> p c s", c=KC),
                              [t_tr, *ct_free])
            banks.give(bank, t_cs)
            yield
            bank, free = banks.take()
            for t in range(TT):
                t_y = product(bank[:, t * D:(t + 1) * D],
                              [((ch[:, c, t * P:(t + 1) * P], cl[:, c, t * P:(t + 1) * P]), (wo[0][:, c, :], wo[1][:, c, :]))
                               for c in range(KC)], [*t_cs, *t_wo, *free])
            cT_t.give((ch, cl), [t_y])
            r, r_free = r_bufs.take()
            t_r = tt(dve, r[:, :, :], bank[:, :].rearrange("p (t d) -> p t d", t=TT), xb[:, :, :], ALU.add,
                     [t_y, t_xb, *r_free])
            banks.give(bank, [t_r])
            xb_t.give(xb, [t_r])
            yield from layernorm(b, r, [t_r], xt_readers)
            if then is not None:
                yield
                yield from then(b)

        dpart = ExitStack()
        sbd = lambda name, shape, dt=F32: sb(name, shape, dt, dpart, "right")
        dw = [sbd(f"dw_{n}", [P, KC, 3 * D], F32R) for n in ("hi", "lo")]
        dwo = [sbd(f"dwo_{n}", [P, KC, D], F32R) for n in ("hi", "lo")]
        proj = [sbd(f"proj_{n}", [P, NH // 2, P], F32R) for n in ("hi", "lo")]
        dbias = sbd("dbias", [P, 2 * KC])
        dbv = sbd("dbv", [P, D])
        dbo = sbd("dbo", [P, D])
        mask_d = sbd("mask_d", [P, 3 * P])
        t_db = [load("d_b", dbias[:, :], a["D_b"], t_late), load("d_bv", dbv[:, :], a["D_bv"], t_late),
                load("d_bo", dbo[:, :], a["D_bo"], t_late), load("d_mask", mask_d[:, :], a["mask_d"], t_late)]
        t_dw = weights(split_dve, dw[0][:, :, :], dw[1][:, :, :], a["D_w"], t_late)
        t_dp = weights(split_dve, proj[0][:, :, :], proj[1][:, :, :], a["D_proj"], t_late)
        t_dwo = weights(split_pool, dwo[0][:, :, :], dwo[1][:, :, :], a["D_wo"], t_late)
        qk_t = Turns([[[sbd(f"{w}d_{n}{i}", [P, KC, S], F32R) for n in ("hi", "lo")] for w in "qk"] for i in range(2)],
                     t_late)
        feat_t = Turns([[sbd(f"feat_{n}{i}", [P, 2, S], F32R) for n in ("hi", "lo")] for i in range(3)], t_late)
        awm_t = Turns([sbd(f"awm{i}", [P, 3 * P]) for i in range(4)], t_late)
        aw_t = Turns([[sbd(f"aw_{n}{i}", [P, 3 * P], F32R) for n in ("hi", "lo")] for i in range(6)], t_late)
        state_d = {}

        def prelude_d(b):
            ((qh, ql), (kh, kl)), qk_free = qk_t.take()
            need = [*xt_ready[b], *t_dw, *t_db]
            toks = []
            for which, (hi, lo) in enumerate(((qh, ql), (kh, kl))):
                bank, free = banks.take()
                for c in range(KC):
                    col = (which * KC + c) * P
                    t_mm = product(bank[:, c * S:(c + 1) * S],
                                   [((dw[0][:, k, col:col + P], dw[1][:, k, col:col + P]),
                                     (xt(xt_hi, b, k), xt(xt_lo, b, k))) for k in range(KC)], [*need, *free])
                reads = split_biased([(hi[:, c, :], lo[:, c, :], bank[:, c * S:(c + 1) * S],
                                       dbias[:, which * KC + c:which * KC + c + 1]) for c in range(KC)],
                                     [t_mm, *t_db, *qk_free])
                banks.give(bank, reads)
                toks += reads
                yield
            bank, free = banks.take()
            for t in range(TT):
                t_mm = product(bank[:, t * D:(t + 1) * D],
                               [(sh, (dw[0][:, k, 2 * D:3 * D], dw[1][:, k, 2 * D:3 * D]))
                                for k, sh in enumerate(xt_tile(b, t))], free)
            vf, vf_free = vf_t.take()
            for t in range(TT):
                t_vf = tt(dve, vf[:, t, :], bank[:, t * D:(t + 1) * D], dbv[:, :], ALU.add, [t_mm, *vf_free, *t_late])
            banks.give(bank, [t_vf])
            state_d[b] = dict(q=(qh, ql), k=(kh, kl), qk_ready=toks, vf=vf, t_vf=t_vf, xt_last=t_mm,
                           v_ready=[None] * NVT, accs=[])

        def pair_d(b, j):
            st = state_d[b]
            c = 2 * j // (NH // KC)
            pair_bufs, f_free = feat_t.take()
            feat_hi, feat_lo = pair_bufs
            (qfh, kfh), (qfl, kfl) = ((x[:, 0, :], x[:, 1, :]) for x in pair_bufs)
            bank, free = banks.take()
            for w, (hi, lo) in enumerate((st["q"], st["k"])):
                t_f = product(bank[:, w * S:(w + 1) * S],
                              [((proj[0][:, j, :], proj[1][:, j, :]), (hi[:, c, :], lo[:, c, :]))],
                              [*st["qk_ready"], *t_dp, *free])
            if j == NH // 2 - 1:
                qk_t.give((st["q"], st["k"]), [t_f])
            both = bank[:, :].rearrange("p (w s) -> p w s", w=2)
            t_hi = act_do(feat_hi[:, :, :], both, ACT.Relu, [t_f, *f_free])
            t_lo = stt(feat_lo[:, :, :], both, 0.0, f(feat_hi[:, :, :]), ALU.max, ALU.subtract, [t_hi])
            f_ready = [t_hi, t_lo]
            banks.give(bank, f_ready)
            yield
            yield
            aws = []
            for g in range(2):
                rows = slice(g * M, (g + 1) * M)
                bank, free = banks.take()
                t_a = product(bank[:, 0:S], [((kfh[rows, 0:P], kfl[rows, 0:P]), (qfh[rows, :], qfl[rows, :]))],
                              [*f_ready, *free])
                t_a = product(bank[:, S:S + P], [((kfh[rows, P:S], kfl[rows, P:S]), (qfh[rows, P:S], qfl[rows, P:S]))])
                awm, m_free = awm_t.take()
                (ah, al), a_free = aw_t.take()
                t_m = tt(dve, awm[:, :], bank[:, 0:3 * P], mask_d[:, :], ALU.mult, [t_a, *t_db, *m_free])
                banks.give(bank, [t_m])
                t_h = act_do(ah[:, :], awm[:, :], ACT.Identity, [t_m, *a_free])
                aws.append([(ah, al), awm, t_h])
            feat_t.give(pair_bufs, [t_a])
            yield
            for g, ((ah, al), awm, t_h) in enumerate(aws):
                t_l = tt(dve, al[:, :], awm[:, :], f(ah[:, :]), ALU.subtract, [t_h])
                awm_t.give(awm, [t_h, t_l])
                aws[g] = ((ah, al), [t_h, t_l])
            yield
            for g in range(2):
                h = 2 * j + g
                (ah, al), ready = aws[g]
                weighted_values(st, h, [(0, ah[:, 0:S], al[:, 0:S], slice(0, S)),
                                        (1, ah[:, S:S + P], al[:, S:S + P], slice(P, S))], ready)
                aw_t.give((ah, al), [pe.last()])

        def weighted_values(st, h, parts, ready):
            if h % HPB == 0:
                bank, bank_free = banks.take()
                st["accs"].append((bank, None))
            else:
                (bank, _), bank_free = st["accs"][-1], []
            base = (h // VH % 2) * S
            first_of_tile = h % VH == 0
            last_of_tile = h % VH == VH - 1 or h == NH - 1
            terms = [(t, w, cols) for t, hi, lo, cols in parts for w in (lo, hi)]
            for i, (t, w, cols) in enumerate(terms):
                o = bank[:, base + cols.start:base + cols.stop]
                mm = lambda e, o=o, t=t, w=w, i=i: e.matmul(
                    o, v_heads[:, t, h, :], w, start=(first_of_tile and i == 0),
                    stop=(last_of_tile and i == len(terms) - 1), skip_group_check=True)
                after = [*ready, *st["v_ready"][h // VH], *bank_free] if i == 0 else ()
                if i == len(terms) - 1:
                    pe.do(mm, after)
                else:
                    pe.quiet(mm, after)
            if last_of_tile:
                v_readers[h // VH] = [pe.last()]
                st["accs"][-1] = (bank, pe.last())

        def finish_d(b):
            yield from finish_heads(b, state_d[b], dwo, dbo, [*t_dwo, *t_db])

        per_b = NH // 2
        first_d = 3
        for b in range(B):
            base = first_d + per_b * b
            at(base - 3, prelude_d(b))
            for j in range(per_b):
                at(base + j, pair_d(b, j))
            for i in range(NVT):
                at(base + min(VH * i + 2, NH - 1) // 2 - 1 if b else base - 1 + i // 3, place(state_d, b, i))
            for i in range(NAB):
                at(base + min(HPB * i + HPB - 1, NH - 1) // 2 + 5, drain(state_d, b, i, DELTA))
            at(base + per_b + 6, finish_d(b))
        run()
        dpart.close()
        t_d = fence()

        epart = ExitStack()
        sbe = lambda name, shape, dt=F32: sb(name, shape, dt, epart, "right")
        NS4 = 4
        eq = [sbe(f"eq_{n}", [P, KC, NS4 * P], F32R) for n in ("hi", "lo")]
        ek = [sbe(f"ek_{n}", [CK, 2, NS4 * P], F32R) for n in ("hi", "lo")]
        ev = [sbe(f"ev_{n}", [CK, 2, D], F32R) for n in ("hi", "lo")]
        eo = [sbe(f"eo_{n}", [P, KC, D], F32R) for n in ("hi", "lo")]
        ebias = sbe("ebias", [P, 3 * NS4])
        ebv, ebo = sbe("ebv", [P, D]), sbe("ebo", [P, D])
        low_rows = sbe("low_rows", [P, 1])
        t_eb = [load("e_b", ebias[:, 0:2 * NS4], a["E_b"], t_d), load("e_bv", ebv[:, :], a["E_bv"], t_d),
                load("e_bo", ebo[:, :], a["E_bo"], t_d), load("e_m", low_rows[:, :], a["low_rows"], t_d)]
        t_ew = [*weights(split_dve, eq[0][:, :, :], eq[1][:, :, :], a["E_wq"], t_d),
                *weights(split_dve, ek[0][:, :, :], ek[1][:, :, :], a["E_wk"], t_d),
                *weights(split_pool, ev[0][:, :, :], ev[1][:, :, :], a["E_wv"], t_d)]
        t_eo = weights(split_pool, eo[0][:, :, :], eo[1][:, :, :], a["E_wo"], t_d)
        t_eb.append(ts(dve, ebias[:, 2 * NS4:3 * NS4], ebias[:, 0:NS4], low_rows[:, 0:1], None, ALU.mult, after=t_eb))
        qs_t = Turns([sbe(f"qslots{i}", [P, NS4, S], F32R) for i in range(2)], t_d)
        qm_t = Turns([sbe(f"qmask{i}", [P, 2, S], F32R) for i in range(2)], t_d)
        ks_t = Turns([[sbe(f"kslots_{n}{i}", [P, NS4, S], F32R) for n in ("hi", "lo")] for i in range(2)], t_d)
        se_t = Turns([sbe(f"scoreE{i}", [P, TT, S]) for i in range(3)], t_d)
        pe_t = Turns([sbe(f"probE{i}", [P, TT, S]) for i in range(2)], t_d)
        pte_t = Turns([[sbe(f"probTE_{n}{i}", [P, TT, S], F32R) for n in ("hi", "lo")] for i in range(3)], t_d)
        sme_t = Turns([sbe(f"smallE{i}", [P, 2 * TT]) for i in range(3)], t_d)
        scale_e = float(DH) ** -0.5
        lim = CLAMP / scale_e
        state_e = {}

        def prelude_e(b):
            (cxh, cxl), t_cx = load_context(b)
            qs, q_free = qs_t.take()
            (kh, kl), k_free = ks_t.take()
            ready = []
            yield
            for half in range(2):
                bank, free = banks.take()
                for j in range(2):
                    n = 2 * half + j
                    t_mm = product(bank[:, j * S:(j + 1) * S],
                                   [((eq[0][:, k, n * P:(n + 1) * P], eq[1][:, k, n * P:(n + 1) * P]),
                                     (xt(xt_hi, b, k), xt(xt_lo, b, k))) for k in range(KC)],
                                   [*xt_ready[b], *t_ew, *free])
                qm, m_free = qm_t.take()
                for j in range(2):
                    n = 2 * half + j
                    t_m = act_do(qm[:, j, :], bank[:, j * S:(j + 1) * S], ACT.Identity, [t_mm, *t_eb, *m_free],
                                 scale=low_rows[:, 0:1], bias=ebias[:, 2 * NS4 + n:2 * NS4 + n + 1])
                for j in range(2):
                    n = 2 * half + j
                    t_q = stt(qs[:, n, :], bank[:, j * S:(j + 1) * S], ebias[:, n:n + 1], f(qm[:, j, :]),
                              ALU.add, ALU.subtract, [t_m, *q_free])
                toks = [t_m, t_q]
                banks.give(bank, toks)
                qm_t.give(qm, toks)
                ready += toks
                yield
            t_xt = t_mm
            for half in range(2):
                bank, free = banks.take()
                for j in range(2):
                    n = 2 * half + j
                    t_mm = product(bank[:, j * S:(j + 1) * S],
                                   [((ek[0][:, k, n * P:(n + 1) * P], ek[1][:, k, n * P:(n + 1) * P]),
                                     (cxh[:, k, :], cxl[:, k, :])) for k in range(2)], [*t_cx, *free])
                toks = split_biased([(kh[:, n, :], kl[:, n, :], bank[:, (n % 2) * S:(n % 2 + 1) * S],
                                      ebias[:, NS4 + n:NS4 + n + 1]) for n in (2 * half, 2 * half + 1)],
                                    [t_mm, *t_eb, *k_free])
                banks.give(bank, toks)
                ready += toks
                yield
            bank, free = banks.take()
            for t in range(TT):
                t_mm = product(bank[:, t * D:(t + 1) * D],
                               [((cxh[:, k, t * P:(t + 1) * P], cxl[:, k, t * P:(t + 1) * P]),
                                 (ev[0][:, k, :], ev[1][:, k, :])) for k in range(2)], free)
            ctx_t.give((cxh, cxl), [t_mm])
            vf, vf_free = vf_t.take()
            for t in range(TT):
                t_vf = tt(dve, vf[:, t, :], bank[:, t * D:(t + 1) * D], ebv[:, :], ALU.add, [t_mm, *t_eb, *vf_free])
            banks.give(bank, [t_vf])
            state_e[b] = dict(q=qs, k=(kh, kl), qk_ready=ready, vf=vf, t_vf=t_vf, xt_last=t_xt,
                           v_ready=[None] * NVT, accs=[])

        def head_e(b, h):
            st = state_e[b]
            rows, n = slice(32 * (h % 4), 32 * (h % 4) + 32), h // 4
            qs, (kh, kl) = st["q"], st["k"]
            bank, free = banks.take()
            for t in range(TT):
                o = bank[:, t * S:(t + 1) * S]
                q = qs[rows, n, t * P:(t + 1) * P]
                t_s = matmuls([(o, q, kl[rows, n, :]), (o, q, kh[rows, n, :])], [*st["qk_ready"], *free])
            if h == NH - 1:
                qs_t.give(qs, [t_s])
                ks_t.give((kh, kl), [t_s])
            sc, sc_free = se_t.take()
            small, sm_free = sme_t.take()
            mx, nmx = small[:, 0:TT], small[:, TT:2 * TT]
            yield
            for t in range(TT):
                t_c = dve.do(lambda e, t=t, bank=bank: e.tensor_scalar(
                    sc[:, t, :], bank[:, t * S:(t + 1) * S], lim, None, ALU.min, ALU.max, accum_out=mx[:, t:t + 1]),
                             [t_s, *sc_free, *sm_free])
            banks.give(bank, [t_c])
            t_nm = ts(dve, nmx, mx, -lim, -scale_e, ALU.max, ALU.mult, after=[t_c])
            t_cl = ts(dve, sc[:, :, :], sc[:, :, :], -lim, None, ALU.max, after=[t_c])
            yield
            pr, p_free = pe_t.take()
            for t in range(TT):
                t_p = act_do(pr[:, t, :], sc[:, t, :], ACT.Exp, [t_nm, t_cl, *p_free], scale=scale_e, bias=nmx[:, t:t + 1])
            se_t.give(sc, [t_p])
            sme_t.give(small, [t_p])
            yield
            bank, free = banks.take()
            t_t = transposes(bank, [(bank[:, kt * S + t * P:kt * S + (t + 1) * P], pr[:, t, kt * P:(kt + 1) * P])
                                    for kt in range(TT) for t in range(TT)], [t_p, *free])
            pe_t.give(pr, [t_t])
            (ph, pl), pt_free = pte_t.take()
            both = bank[:, :].rearrange("p (k s) -> p k s", k=TT)
            t_hi = act_do(ph[:, :, :], both, ACT.Identity, [t_t, *pt_free])
            yield
            ready = [t_hi, tt(dve, pl[:, :, :], both, f(ph[:, :, :]), ALU.subtract, [t_hi])]
            banks.give(bank, ready)
            yield
            weighted_values(st, h, [(kt, ph[:, kt, :], pl[:, kt, :], slice(0, S)) for kt in range(TT)], ready)
            pte_t.give((ph, pl), [pe.last()])

        xtf_t = Turns([sbe(f"xtf{i}", [P, KC, S]) for i in range(1)], t_d)
        rt_t = Turns([sbe(f"route{i}", [P, TT, 13, NE]) for i in range(2)], t_d)
        gT_t = Turns([sbe("gatesT", [NE, S])], t_d)
        ridx_t = Turns([(sbe(f"ridx{i}", [P, TT, NE], U32), sbe(f"slot{i}", [P, TT, TOPK], U32)) for i in range(2)],
                       t_d)
        t_seen = [t_rt[-1]]
        t_codes, t_rows = [], []

        def route(b):
            t_store = sp.do(lambda e: e.dma_start(
                x_rows[b * S:(b + 1) * S, :].rearrange("(t p) d -> p t d", p=P), x_tok[:, b * TT:(b + 1) * TT, :]),
                [*x_ready[b], *t_rows[-2:-1]], signal_for(f"x_rows{b % 2}"))
            t_rows.append(t_store)
            xtf, x_free = xtf_t.take()
            t_x = tt(pool, xtf[:, :, :], f(xt_hi[:, :, b * S:(b + 1) * S]), f(xt_lo[:, :, b * S:(b + 1) * S]), ALU.add,
                     [*xt_ready[b], *x_free])
            yield
            bank, free = banks.take()
            for t in range(TT):
                t_l = matmuls([(bank[:, t * NE:(t + 1) * NE], xtf[:, k, t * P:(t + 1) * P], gw_raw[:, k, :])
                               for k in range(KC)], [t_x, *t_rt, *free])
            xtf_t.give(xtf, [t_l])
            rt, rt_free = rt_t.take()
            (ridx, slot), ri_free = ridx_t.take()
            lg, ex, top = rt[:, :, 0, :], rt[:, :, 1, :], rt[:, :, 2, :]
            oh, ohr = rt[:, :, 3:5, :], rt[:, :, 9:11, :]
            small, idf, both, share = rt[:, :, 5, :], rt[:, :, 6, :], rt[:, :, 7, :], rt[:, :, 8, :]
            rank = rt[:, :, 11, :]
            t_c = copy(dve, lg, bank[:, 0:TT * NE].rearrange("p (t e) -> p t e", t=TT), [t_l, *rt_free, *ri_free])
            banks.give(bank, [t_c])
            t_m = dve.do(lambda e: e.tensor_reduce(small[:, :, 0], lg, AX.X, ALU.max, negate=True), [t_c])
            for t in range(TT):
                t_e = act_do(ex[:, t, :], lg[:, t, :], ACT.Exp, [t_m], bias=small[:, t, 0:1],
                             accum_out=small[:, t, 1:2])
            yield
            t_r = dve.do(lambda e: e.reciprocal(small[:, :, 2], small[:, :, 1]), [t_e])
            for t in range(TT):
                t_g = ts(dve, ex[:, t, :], ex[:, t, :], small[:, t, 2:3], None, ALU.mult, after=[t_r])
            for t in range(TT):
                t_t = dve.do(lambda e, t=t: e.max(top[:, t, :], ex[:, t, :]), [t_g])
            for t in range(TT):
                t_i = dve.do(lambda e, t=t: e.max_index(ridx[:, t, :], top[:, t, :], ex[:, t, :]), [t_t])
            t_f = copy(dve, idf, ridx[:, :, :], [t_i])
            for t in range(TT):
                for j in range(TOPK):
                    t_o = ts(dve, oh[:, t, j, :], iota8[:, :], idf[:, t, j:j + 1], None, ALU.is_equal,
                             after=[t_f, *t_rt])
            t_b = tt(dve, both, oh[:, :, 0, :], oh[:, :, 1, :], ALU.add, [t_o])
            t_s = tt(dve, small[:, :, 3], top[:, :, 0], top[:, :, 1], ALU.add, [t_t])
            t_s = dve.do(lambda e: e.reciprocal(small[:, :, 3], small[:, :, 3]), [t_s])
            for t in range(TT):
                t_s2 = ts(dve, shares[:, b * TT + t, :], top[:, t, 0:TOPK], small[:, t, 3:4], None, ALU.mult, after=[t_s])
            for t in range(TT):
                n = b * TT + t
                t_g = ts(dve, share[:, t, :], oh[:, t, 0, :], shares[:, n, 0:1], None, ALU.mult, after=[t_s2, t_o])
                t_g = stt(share[:, t, :], oh[:, t, 1, :], shares[:, n, 1:2], share[:, t, :], ALU.mult, ALU.add, [t_g])
            yield
            bank, free = banks.take()
            for t in range(TT):
                terms = [(bank[:, t * NE:(t + 1) * NE], before[:, :], both[:, t, :]),
                         (bank[:, t * NE:(t + 1) * NE], ones[:, :], seen[:, :])]
                terms += [(bank[:, t * NE:(t + 1) * NE], ones[:, :], both[:, u, :]) for u in range(t)]
                t_k = matmuls(terms, [t_b, *t_seen, t_ones, *free])
            t_sn = [t_k]
            for t in range(TT):
                t_sn = [tt(dve, seen[:, :], seen[:, :], both[:, t, :], ALU.add, [t_b, *t_sn, *t_seen])]
            t_seen[:] = t_sn
            for j in range(TOPK):
                t_p = tt(dve, ohr[:, :, j, :], oh[:, :, j, :], bank[:, 0:TT * NE].rearrange("p (t e) -> p t e", t=TT),
                         ALU.mult, [t_k])
            banks.give(bank, [t_p])
            t_p = dve.do(lambda e: e.tensor_reduce(rank[:, :, 0:TOPK], ohr, AX.X, ALU.add), [t_p])
            t_p = stt(slot[:, :, :], idf[:, :, 0:TOPK], float(B * S), rank[:, :, 0:TOPK], ALU.mult, ALU.add, [t_p, t_f])
            for t in range(TT):
                for j in range(TOPK):
                    t_sc = pool.do(lambda e, t=t, j=j: e.indirect_dma_start(
                        slot_codes, bass.IndirectOffsetOnAxis(ap=slot[:, t, j:j + 1], axis=0),
                        codes[:, b * TT + t, j:j + 1], None), [t_p, t_empty, *t_rt], signal_for(f"codes{b % 2}"))
            ridx_t.give((ridx, slot), [t_sc])
            t_codes.append(t_sc)
            bank, free = banks.take()
            t_t = transposes(bank, [(bank[0:NE, t * P:(t + 1) * P], share[:, t, :]) for t in range(TT)],
                             [t_g, *free])
            rt_t.give(rt, [t_t, t_p])
            gT, gT_free = gT_t.take()
            t_c = copy(dve, gT[:, :], bank[0:NE, 0:S], [t_t, *gT_free])
            banks.give(bank, [t_c])
            yield
            bank, free = banks.take()
            for t in range(TT):
                t_b = matmuls([(bank[:, t * D:(t + 1) * D], gT[:, t * P:(t + 1) * P], b2_sb[:, :])],
                              [t_c, *t_rt, *free])
            gT_t.give(gT, [t_b])
            xs = x_tok[:, b * TT:(b + 1) * TT, :]
            t_a = tt(dve, xs, bank[:, :].rearrange("p (t d) -> p t d", t=TT), xs, ALU.add,
                     [t_b, t_store, *x_ready[b], *xt_ready[b]])
            banks.give(bank, [t_a])
            x_ready[b] = [t_a]

        def finish_e(b):
            yield from finish_heads(b, state_e[b], eo, ebo, [*t_eo, *t_eb], route)

        first_e = 10
        for b in range(B):
            base = first_e + NH * b
            at(base - 10, prelude_e(b))
            for h in range(NH):
                at(base + h, head_e(b, h))
            for i in range(NVT):
                at(base + min(VH * i + 2, NH - 1) - 6, place(state_e, b, i))
            for i in range(NAB):
                at(base + min(HPB * i + HPB - 1, NH - 1) + 6, drain(state_e, b, i, 0.0))
            at(base + NH + 7, finish_e(b))
        run()
        epart.close()
        part.close()
        mid.close()
        t_e = fence()

        fpart = ExitStack()
        sbf = lambda name, shape, dt=F32: sb(name, shape, dt, fpart, "right")
        BR = BT // P
        PAIR = 2
        NQ = FC // PAIR
        AHEAD = 2
        W1C = KC * HID + FC
        w1r_t = Turns([(i, sbf(f"w1raw{i}", [P, W1C])) for i in range(4)], t_e)
        w2r_t = Turns([(i, sbf(f"w2raw{i}", [P, FC * D])) for i in range(4)], t_e)
        w1_t = Turns([[sbf(f"w1_{n}{i}", [P, KC, PAIR * P], F32R) for n in ("hi", "lo")] for i in range(4)], t_e)
        w2_t = Turns([[sbf(f"w2_{n}{i}", [P, PAIR, D], F32R) for n in ("hi", "lo")] for i in range(6)], t_e)
        xg_t = Turns([(i, sbf(f"xg{i}", [P, BR, D])) for i in range(4)], t_e)
        xg_split_t = Turns([[sbf(f"xgT_{n}{i}", [P, KC, BT], F32R) for n in ("hi", "lo")] for i in range(2)], t_e)
        gf_t = Turns([sbf(f"gf{i}", [P, PAIR * BT]) for i in range(2)], t_e)
        gh_t = Turns([[sbf(f"gh_{n}{i}", [P, PAIR, BT], F32R) for n in ("hi", "lo")] for i in range(4)], t_e)
        ysb_t = Turns([(i, sbf(f"yblock{i}", [P, BR, D])) for i in range(3)], t_e)
        counts = sbf("counts", [P, NE])
        ends = sbf("ends", [P, NE])
        past = sbf("past", [P, NE])
        expert_of = sbf("expert_of", [P, NBK])
        row_stats = sbf("row_stats", [P, 4])
        row_i = sbf("row_i", [P, 1], U32)
        wrow_i = sbf("wrow_i", [P, NBK], U32)
        block_codes = sbf("block_codes", [NBK, BT], U32)
        block_codes_f = sbf("block_codes_f", [NBK, BT])
        code_f = sbf("code_f", [P, BR * NBK])
        token_f = sbf("token_f", [P, BR * NBK])
        slot_i = sbf("slot_i", [P, BR * NBK], U32)
        token_i = sbf("token_i", [P, BR * NBK], U32)

        def gather(name, dst, rows, index, after):
            if name not in loads:
                loads[name] = [sem(f"l_{name}"), 0]
            loads[name][1] += 16
            return pool.do(lambda e: e.indirect_dma_start(
                dst, None, rows, bass.IndirectOffsetOnAxis(ap=index, axis=0)), after, (loads[name][0], 16, loads[name][1]))

        bank, free = banks.take()
        t_n = matmuls([(bank[:, 0:NE], ones[:, :], seen[:, :])], [*t_seen, t_ones, *free])
        t_n = copy(dve, counts[:, :], bank[:, 0:NE], [t_n, *t_e])
        banks.give(bank, [t_n])
        t_n = ts(dve, ends[:, :], counts[:, :], 0.0, None, ALU.is_gt, after=[t_n])
        for i in range(1, XPB):
            t_n = stt(ends[:, :], counts[:, :], float(i * BT), ends[:, :], ALU.is_gt, ALU.add, [t_n])
        for i in range(1, NE):
            t_n = tt(dve, ends[:, i:i + 1], ends[:, i:i + 1], ends[:, i - 1:i], ALU.add, [t_n])
        t_p = ts(dve, past[:, :], ends[:, :], row_no[:, 0:1], None, ALU.is_le, after=[t_n])
        t_p = dve.do(lambda e: e.tensor_reduce(row_stats[:, 0:1], past[:, :], AX.X, ALU.add), [t_p])
        t_p = tt(dve, past[:, :], past[:, :], ends[:, :], ALU.mult, [t_p])
        t_p = dve.do(lambda e: e.tensor_reduce(row_stats[:, 1:2], past[:, :], AX.X, ALU.max), [t_p])
        t_p = stt(row_stats[:, 2:3], row_stats[:, 0:1], float(XPB), row_no[:, :], ALU.mult, ALU.add, [t_p])
        t_p = tt(dve, row_stats[:, 2:3], row_stats[:, 2:3], row_stats[:, 1:2], ALU.subtract, [t_p])
        t_p = ts(dve, row_i[:, :], row_stats[:, 2:3], float(NE * XPB), None, ALU.min, after=[t_p])
        t_bc = gather("block_codes", block_codes[:, :], slot_codes.rearrange("(r s) one -> r (s one)", s=BT),
                      row_i[0:NBK, 0:1], [t_p, *t_codes])
        t_w = ts(dve, expert_of[:, :], block_no[:, :], ends[:, 0:1], None, ALU.is_ge, after=[t_n])
        for i in range(1, NE - 1):
            t_w = stt(expert_of[:, :], block_no[:, :], ends[:, i:i + 1], expert_of[:, :], ALU.is_ge, ALU.add, [t_w])
        t_w = ts(dve, wrow_i[:, :], expert_of[:, :], float(P), row_no[:, 0:1], ALU.mult, ALU.add, after=[t_w])
        raws = {}

        def gather_weights(j):
            (i, raw1), free1 = w1r_t.take()
            (i2, raw2), free2 = w2r_t.take()
            t_1 = gather(f"w1raw{i}", raw1[:, :], a["F_w1"], wrow_i[:, j:j + 1], [t_w, *free1])
            t_2 = gather(f"w2raw{i2}", raw2[:, :], a["F_w2"], wrow_i[:, j:j + 1], [t_w, *free2])
            raws[j] = (i, raw1, t_1, i2, raw2, t_2)

        gather_weights(0)
        t_c = copy(dve, block_codes_f[:, :], block_codes[:, :], [t_bc])
        bank, free = banks.take()
        t_t = transposes(bank, [(bank[:, t * NBK:(t + 1) * NBK], block_codes_f[:, t * P:(t + 1) * P])
                                for t in range(BR)], [t_c, *free])
        t_c = copy(dve, code_f[:, :], bank[:, 0:BR * NBK], [t_t])
        banks.give(bank, [t_c])
        t_slot = copy(dve, slot_i[:, :], code_f[:, :], [t_c])
        t_f = ts(dve, token_f[:, :], code_f[:, :], float(B * S), float(-B * S), ALU.is_ge, ALU.mult, after=[t_c])
        t_f = tt(dve, token_f[:, :], token_f[:, :], code_f[:, :], ALU.add, [t_f])
        t_tok = ts(dve, token_i[:, :], token_f[:, :], float(B * S - 1), None, ALU.min, after=[t_f])
        xgs, xgTs, split_ws, ybanks = {}, {}, {}, {}
        t_y_rows = []

        def gather_x(j):
            (i, xg), free = xg_t.take()
            for t in range(BR):
                t_g = gather(f"xg{i}", xg[:, t, :], x_rows, token_i[:, t * NBK + j:t * NBK + j + 1],
                             [t_tok, *t_rows, *free])
            xgs[j] = (i, xg, t_g)

        def block_x(j):
            i, xg, t_g = xgs.pop(j)
            bank, free = banks.take()
            t_tr = transposes(bank, [(bank[:, c * BT + t * P:c * BT + (t + 1) * P], xg[:, t, c * P:(c + 1) * P])
                                     for c in range(KC) for t in range(BR)], [t_g, *free])
            xg_t.give((i, xg), [t_tr])
            (xh, xl), x_free = xg_split_t.take()
            toks = split_bank(xh[:, :, :], xl[:, :, :], bank[:, :].rearrange("p (c t) -> p c t", c=KC),
                              [t_tr, *x_free])
            banks.give(bank, toks)
            xgTs[j] = ((xh, xl), toks)

        def split_w(j, q):
            i, raw1, t_1, i2, raw2, t_2 = raws[j]
            (h1, l1), free1 = w1_t.take()
            (h2, l2), free2 = w2_t.take()
            w1 = raw1[:, 0:KC * HID].rearrange("p (k n) -> p k n", k=KC)[:, :, q * PAIR * P:(q + 1) * PAIR * P]
            w2 = raw2[:, q * PAIR * D:(q + 1) * PAIR * D].rearrange("p (k n) -> p k n", k=PAIR)
            t_h1 = act_do(h1[:, :, :], w1, ACT.Identity, [t_1, *free1])
            t_h2 = act_do(h2[:, :, :], w2, ACT.Identity, [t_2, *free2])
            t_l1 = tt(dve, l1[:, :, :], w1, f(h1[:, :, :]), ALU.subtract, [t_h1, t_1])
            t_l2 = [tt(eng, l2[:, u, :], w2[:, u, :], f(h2[:, u, :]), ALU.subtract, [t_h2, t_2])
                    for u, eng in enumerate((dve, pool))]
            split_ws[(j, q)] = ((h1, l1), [t_h1, t_l1], (h2, l2), [t_h2, *t_l2])

        def block_pair(j, q):
            if q == 0:
                if j + 3 < NBK:
                    gather_weights(j + 3)
                    gather_x(j + 3)
            ahead = (j * NQ + q + AHEAD) // NQ, (q + AHEAD) % NQ
            if ahead[0] < NBK:
                split_w(*ahead)
            if q == NQ - 2 and j + 1 < NBK:
                block_x(j + 1)
            (h1, l1), w1_ready, (h2, l2), w2_ready = split_ws.pop((j, q))
            (xh, xl), x_ready_j = xgTs[j]
            i, raw1, _, i2, raw2, _ = raws[j]
            bank, free = banks.take()
            for u in range(PAIR):
                fcols = slice(u * P, (u + 1) * P)
                t_mm = product(bank[:, u * BT:(u + 1) * BT],
                               [((h1[:, k, fcols], l1[:, k, fcols]), (xh[:, k, :], xl[:, k, :])) for k in range(KC)],
                               [*x_ready_j, *w1_ready, *free])
            gf, gf_free = gf_t.take()
            for u in range(PAIR):
                bias = raw1[:, KC * HID + q * PAIR + u:KC * HID + q * PAIR + u + 1]
                t_g = act_do(gf[:, u * BT:(u + 1) * BT], bank[:, u * BT:(u + 1) * BT], ACT.Gelu, [t_mm, *gf_free],
                             bias=bias)
            banks.give(bank, [t_g])
            (gh, gl), g_free = gh_t.take()
            ready = split_dve(gh[:, :, :], gl[:, :, :], gf[:, :].rearrange("p (u s) -> p u s", u=PAIR), [t_g, *g_free])
            gf_t.give(gf, ready)
            w1_t.give((h1, l1), [t_mm])
            last = q == NQ - 1
            if last:
                xg_split_t.give((xh, xl), [t_mm])
                w1r_t.give((i, raw1), [t_g])
                w2r_t.give((i2, raw2), w2_ready)
            yield
            yield
            if q == 0:
                ybanks[j] = banks.take()
            ybank, free = ybanks[j]
            for u in range(PAIR):
                fc = q * PAIR + u
                for t in range(BR):
                    o = ybank[:, t * D:(t + 1) * D]
                    st = slice(t * P, (t + 1) * P)
                    for n, (hh, ww) in enumerate(((gl, h2), (gh, l2), (gh, h2))):
                        mm = lambda e, o=o, st=st, hh=hh, ww=ww, n=n, t=t, u=u, fc=fc: e.matmul(
                            o, hh[:, u, st], ww[:, u, :], start=(fc == 0 and n == 0 and t == 0),
                            stop=(fc == FC - 1 and n == 2), skip_group_check=True)
                        after = [*ready, *w2_ready, *free] if n == 0 else ()
                        if n == 2 and t == BR - 1 and u == PAIR - 1:
                            t_y = pe.do(mm, after)
                        else:
                            pe.quiet(mm, after)
            gh_t.give((gh, gl), [t_y])
            w2_t.give((h2, l2), [t_y])
            if not last:
                return
            (n, ysb), y_free = ysb_t.take()
            t_s = act_do(ysb[:, :, :], ybank[:, :].rearrange("p (t d) -> p t d", t=BR), ACT.Identity, [t_y, *y_free])
            banks.give(ybank, [t_s])
            yield
            for t in range(BR):
                t_o = pool.do(lambda e, t=t: e.indirect_dma_start(
                    y_rows, bass.IndirectOffsetOnAxis(ap=slot_i[:, t * NBK + j:t * NBK + j + 1], axis=0),
                    ysb[:, t, :], None, bounds_check=TOPK * B * S - 1, oob_is_err=False),
                    [t_s, t_slot], signal_for(f"y_rows{n}"))
            ysb_t.give((n, ysb), [t_o])
            t_y_rows[:] = [*t_y_rows[-2:], t_o]

        gather_x(0)
        for j in (1, 2):
            gather_weights(j)
            gather_x(j)
        for q in range(AHEAD):
            split_w(0, q)
        block_x(0)
        for j in range(NBK):
            for q in range(NQ):
                at(NQ * j + q, block_pair(j, q))
        run()

        fpart.close()
        t_f = fence()
        cpart = ExitStack()
        ycs = [sb(f"yc{b}", [P, TOPK, TT, D], F32, cpart, "right") for b in range(B)]
        yc_ready = []
        for b in range(B):
            for k in range(TOPK):
                t_l = load(f"yc{b}", ycs[b][:, k, :, :],
                           y_rows.rearrange("(k b t p) d -> k b p t d", k=TOPK, b=B, t=TT)[k, b], [*t_y_rows, *t_f])
            yc_ready.append(t_l)

        def combine(b):
            yc, t_l = ycs[b], yc_ready[b]
            for t in range(TT):
                for k in range(TOPK):
                    n = b * TT + t
                    t_a = stt(x_tok[:, n, :], yc[:, k, t, :], shares[:, n, k:k + 1], x_tok[:, n, :], ALU.mult, ALU.add,
                              [t_l, *x_ready[b]])
                    x_ready[b] = [t_a]
            yield from layernorm(b, x_tok[:, b * TT:(b + 1) * TT, :], [t_a], [], last=True)
            stored[0] += 16
            sp.do(lambda e: e.dma_start(out[b * TT:(b + 1) * TT].rearrange("t p d -> p t d"),
                                        x_tok[:, b * TT:(b + 1) * TT, :]), x_ready[b], (out_sem, 16, stored[0]))

        stored = [0]
        for b in range(B):
            at(b, combine(b))
        run()

        block = ctx.enter_context(nc.Block())

        @block.tensor
        def _(e):
            pe.play(e)

        @block.scalar
        def _(e):
            act.play(e)

        @block.vector
        def _(e):
            dve.play(e)

        @block.gpsimd
        def _(e):
            pool.play(e)

        @block.sync
        def _(e):
            sp.play(e)
            e.wait_ge(out_sem, stored[0])
            for s, value in dram_sems.values():
                e.wait_ge(s, value)
        cpart.close()


def kernel(**inputs):
    import concourse.bacc as _bacc
    from concourse.bass_utils import run_bass_kernel_spmd as _run

    g = {k: np.asarray(v) for k, v in inputs.items()}

    def rows(w, n=P):
        return w.reshape(w.shape[0] // n, n, *w.shape[1:]).swapaxes(0, 1)

    def cols(v):
        return v.reshape(-1, P).T

    def wide(v):
        return np.broadcast_to(v, (P, v.shape[0]))

    def slots(w):
        w = w.reshape(*w.shape[:-1], NH, 1, DH)
        return np.broadcast_to(w, (*w.shape[:-2], 2, DH)).reshape(*w.shape[:-3], NH * 2 * DH)

    tri = np.tril(np.ones((P, P), np.float32))
    L0, L1 = "L0_", "L1_"
    w12 = np.stack([g[L0 + "ffn_w1_w"].T.reshape(KC, P, 4, 2, P), g[L0 + "ffn_w2_w"].T.reshape(KC, P, 4, 2, P)])
    w12 = w12.transpose(3, 2, 0, 4, 1, 5).reshape(4, P, CW)
    square = [g[L0 + f"ffn_{n}_w"].T.reshape(FC, P, FC, P).transpose(2, 1, 0, 3).reshape(FC, P, CW) for n in ("h1", "h2")]
    w3 = g[L0 + "ffn_w3_w"].T.reshape(2, 4, P, D).transpose(0, 2, 1, 3).reshape(2, P, CW)
    proj = np.zeros((P, NH // 2, 2, M), np.float32)
    for h in range(NH):
        r = h % (P // DH) * DH
        proj[r:r + DH, h // 2, h % 2, :] = g[L1 + "attn_proj"][h]
    laid = {
        "ident": np.eye(P, dtype=np.float32),
        "mask_a": np.concatenate([np.where(tri > 0, 0, MASKED), np.zeros((P, P)), np.where(tri > 0, 0, MASKED)], 1)
        .astype(np.float32),
        "mask_d": np.concatenate([tri.T, np.ones((P, P), np.float32), tri.T], 1),
        "low_rows": (np.arange(P) % 32 >= 16).astype(np.float32)[:, None],
        "iota8": np.broadcast_to(np.arange(NE, dtype=np.float32), (P, NE)),
        "x": rows(g["x"].reshape(B * S, D)),
        "xT": rows(g["x"].reshape(B * S, D).T),
        "ctxT": rows(g["ctx_768"].reshape(B * S, DC).T, CK),
        "A_wqkv": rows(g[L0 + "attn_W_qkv"]),
        "A_b": cols(g[L0 + "attn_b_qkv"]),
        "A_wconv": rows(g[L0 + "attn_W_vconv"]),
        "B_wv": rows(g[L0 + "xattn_Wv"].T),
        "B_wt": rows(g[L0 + "xattn_Wt"].T, CK),
        "B_b": np.stack([g[L0 + "xattn_bv"], g[L0 + "xattn_bt"]], 1),
        "C_w": np.concatenate([w12, *square, w3]),
        "C_s": np.stack([cols(g[L0 + f"ffn_{n}_s"]) for n in ("w1", "w2", "h1", "h2")], 1),
        "C_s3": wide(g[L0 + "ffn_w3_s"]),
        "D_w": rows(g[L1 + "attn_Wqkv"].T),
        "D_b": cols(g[L1 + "attn_bqkv"][:2 * D]),
        "D_bv": wide(g[L1 + "attn_bqkv"][2 * D:]),
        "D_wo": rows(g[L1 + "attn_Wout"].T),
        "D_bo": wide(g[L1 + "attn_bout"]),
        "D_proj": proj.reshape(P, NH // 2, P),
        "E_wq": rows(slots(g[L1 + "xattn_Wq"])),
        "E_wk": rows(slots(g[L1 + "xattn_Wk"]), CK),
        "E_b": np.concatenate([cols(slots(g[L1 + "xattn_bq"])), cols(slots(g[L1 + "xattn_bk"]))], 1),
        "E_wv": rows(g[L1 + "xattn_Wv"], CK),
        "E_bv": wide(g[L1 + "xattn_bv"]),
        "E_wo": rows(g[L1 + "xattn_Wo"]),
        "E_bo": wide(g[L1 + "xattn_bo"]),
        "gate_w": rows(g[L1 + "ffn_gate_w"]),
        "F_w1": np.concatenate([g[L1 + "ffn_w1"].reshape(NE, KC, P, HID).transpose(0, 2, 1, 3).reshape(NE * P, KC * HID),
                                g[L1 + "ffn_b1"].reshape(NE, FC, P).transpose(0, 2, 1).reshape(NE * P, FC)], 1),
        "F_w2": g[L1 + "ffn_w2"].reshape(NE, FC, P, D).transpose(0, 2, 1, 3).reshape(NE * P, FC * D),
        "before": np.triu(np.ones((P, P), np.float32), 1),
        "codes": np.arange(TOPK * B * S, dtype=np.uint32).reshape(TOPK, NT, P).transpose(2, 1, 0),
        "block_no": np.broadcast_to(np.arange(NBK, dtype=np.float32), (P, NBK)),
        "row_no": np.arange(P, dtype=np.float32)[:, None],
        "F_b2": g[L1 + "ffn_b2"],
    }
    nc = _bacc.Bacc("TRN2", target_bir_lowering=False, num_devices=1)
    arrays = {f"in_{k}": np.ascontiguousarray(v) for k, v in laid.items()}
    aps = {k: nc.dram_tensor(f"in_{k}", arrays[f"in_{k}"].shape, mybir.dt.from_np(arrays[f"in_{k}"].dtype),
                             kind="ExternalInput").ap() for k in laid}
    out = nc.dram_tensor("out_x", (NT, P, D), F32, kind="ExternalOutput").ap()
    build(nc, aps, out)
    r = _run(nc, [arrays], core_ids=[0])
    return r.results[0]["out_x"].reshape(B, S, D)
```

```python
from contextlib import ExitStack

import numpy as np

import concourse.bass as bass
from concourse import mybir

F32 = mybir.dt.float32
F32R = mybir.dt.float32r
U32 = mybir.dt.uint32
ALU = mybir.AluOpType
ACT = mybir.ActivationFunctionType
AX = mybir.AxisListType

P = 128
B, S, D = 8, 256, 256
DC = 192
TT = S // P
NT = B * TT
KC = D // P
CK = DC // 2
HID = 1024
FC = HID // P
NH, DH, M = 16, 16, 64
NE = 8
SB = 512
NSB = B * S // SB
BPS = SB // S
EPS_LN = 1e-5
DELTA = 1e-6
CLAMP = 10000.0
MASKED = -3.0e38
VW = 34
VH = 3
NVT = -(-NH // VH)
HPB = 2 * VH
NAB = -(-NVT // 2)
CW = 1024
TOPK = 2
BT = 256
XPB = B * S // BT
NBK = (TOPK * B * S - NE) // BT + NE
NONE = 1 << 20


class Engine:

    def __init__(self, sem):
        self.sem, self.count, self.queue = sem, 0, []

    def do(self, instruction, after=(), signal=None):
        if signal is None:
            self.count += 1
            signal = (self.sem, 1, self.count)
        self.queue.append((list(after), instruction, signal))
        return (signal[0], signal[2])

    def quiet(self, instruction, after=()):
        self.queue.append((list(after), instruction, None))

    def last(self):
        return (self.sem, self.count)

    def play(self, eng):
        seen = {}
        for after, instruction, signal in self.queue:
            for sem, value in after:
                if value > seen.get(id(sem), 0):
                    eng.wait_ge(sem, value)
                    seen[id(sem)] = value
            made = instruction(eng)
            if signal is not None:
                made.then_inc(signal[0], signal[1])


class Turns:

    def __init__(self, buffers, after=()):
        self.free = [(b, list(after)) for b in buffers]

    def take(self):
        return self.free.pop(0)

    def give(self, buffer, readers):
        self.free.append((buffer, list(readers)))


def build(nc, a, out):
    ctx = ExitStack()
    mid = ExitStack()
    early = ExitStack()
    late = ExitStack()
    with ctx:
        def sem(name):
            return ctx.enter_context(nc.semaphore(name))

        def sb(name, shape, dt=F32, scope=ctx, side="left"):
            return scope.enter_context(nc.sbuf_tensor(name, shape, dt, side=side))

        pe, act, dve, pool = (Engine(sem(f"s_{n}")) for n in ("pe", "act", "dve", "pool"))
        sp = Engine(None)
        out_sem = sem("s_out")
        banks = Turns([ctx.enter_context(nc.psum_tensor(f"bank{i}", [P, 512], F32)) for i in range(8)])

        loads = {}

        def load(name, dst, src, after=()):
            if name not in loads:
                loads[name] = [sem(f"l_{name}"), 0]
            loads[name][1] += 16
            return sp.do(lambda e: e.dma_start(dst, src), after, (loads[name][0], 16, loads[name][1]))

        def matmuls(terms, after=()):
            n = len(terms)
            for i, (o, st, mv, *own) in enumerate(terms):
                def mm(e, o=o, st=st, mv=mv, i=i):
                    return e.matmul(o, st, mv, start=(i == 0), stop=(i == n - 1))
                need = [*(after if i == 0 else ()), *(own[0] if own else ())]
                if i < n - 1:
                    pe.quiet(mm, need)
                else:
                    tok = pe.do(mm, need)
            return tok

        def product(o, pairs, after=()):
            terms = []
            for (sh, sl), (mh, ml), *own in pairs:
                terms += [(o, sl, mh, *own), (o, sh, ml), (o, sh, mh)]
            return matmuls(terms, after)

        def transposes(bank, parts, after=()):
            for i, (dst, src) in enumerate(parts):
                n = src.shape[0]
                fn = lambda e, dst=dst, src=src, n=n: e.transpose(dst, src, ident[0:n, 0:n])
                if i < len(parts) - 1:
                    pe.quiet(fn, after if i == 0 else ())
                else:
                    tok = pe.do(fn, after if i == 0 else ())
            return tok

        def act_do(o, i, func, after=(), **kw):
            return act.do(lambda e: e.activation(o, i, func, **kw), after)

        def tt(eng, o, x, y, op, after=()):
            return eng.do(lambda e: e.tensor_tensor(o, x, y, op), after)

        def ts(eng, o, x, s1, s2, op0, op1=None, after=()):
            if op1 is None:
                return eng.do(lambda e: e.tensor_scalar(o, x, s1, s2, op0), after)
            return eng.do(lambda e: e.tensor_scalar(o, x, s1, s2, op0, op1), after)

        def stt(o, x, s, y, op0, op1, after=(), **kw):
            return dve.do(lambda e: e.scalar_tensor_tensor(out=o, in0=x, scalar=s, in1=y, op0=op0, op1=op1, **kw),
                          after)

        def copy(eng, o, i, after=()):
            return eng.do(lambda e: e.tensor_copy(o, i), after)

        def f(ap):
            return ap.bitcast(F32)

        def split_bank(hi, lo, bank_ap, after):
            t_hi = act_do(hi, bank_ap, ACT.Identity, after)
            t_lo = tt(dve, lo, bank_ap, f(hi), ALU.subtract, [*after, t_hi])
            return [t_hi, t_lo]

        def split_biased(parts, after):
            for hi, lo, ps, bias in parts:
                t_hi = act_do(hi, ps, ACT.Identity, after, bias=bias)
            for hi, lo, ps, bias in parts:
                t_lo = stt(lo, ps, bias, f(hi), ALU.add, ALU.subtract, [*after, t_hi])
            return [t_hi, t_lo]

        def split_dve(hi, lo, x, after):
            t_hi = copy(dve, hi, x, after)
            t_lo = tt(dve, lo, x, f(hi), ALU.subtract, [t_hi])
            return [t_hi, t_lo]

        def split_pool(hi, lo, x, after):
            t_hi = ts(pool, hi, x, 1.0, 0.0, ALU.mult, ALU.add, after=after)
            t_lo = tt(pool, lo, x, f(hi), ALU.subtract, [t_hi])
            return [t_hi, t_lo]

        def fence():
            return [x.last() for x in (pe, act, dve, pool)]

        x_tok = sb("x_tok", [P, NT, D])
        ident = sb("ident", [P, P])
        ones = sb("ones", [P, P])
        ln_stats = sb("ln_stats", [P, 2, TT, 6])
        ln_mv = sb("ln_mv", [P, 2, TT, 2])
        ln_rstd = sb("ln_rstd", [P, 2, TT])
        minus_half = sb("minus_half", [P, 4])
        gw_raw = sb("gw_raw", [P, KC, NE])
        iota8 = sb("iota8", [P, NE])
        shares = sb("shares", [P, NT, TOPK])
        before = sb("before", [P, P], F32R)
        ones_r = sb("ones_r", [P, P], F32R)
        seen = sb("seen", [P, NE], F32R)
        codes = sb("codes", [P, NT, TOPK], U32)
        block_no = sb("block_no", [P, NBK])
        row_no = sb("row_no", [P, 1])
        none_t = sb("none", [P, (NE * B * S + BT) // P], U32)
        xt_hi = sb("xt_hi", [P, KC, B * S], F32R, mid)
        xt_lo = sb("xt_lo", [P, KC, B * S], F32R, mid)
        r_bufs = Turns([sb(f"resid{i}", [P, TT, D], F32, mid) for i in range(3)])
        mask_a = sb("mask_a", [P, 3 * P], F32, mid)
        ctx_raw = Turns([(i, sb(f"ctx_raw{i}", [CK, 2, S], F32, mid)) for i in range(2)])
        ctx_t = Turns([[sb(f"ctx_{n}{i}", [CK, 2, S], F32R, mid) for n in ("hi", "lo")] for i in range(2)])

        x_rows = nc.dram_tensor("x_rows", (B * S, D), F32, kind="Internal").ap()
        y_rows = nc.dram_tensor("y_rows", (TOPK * B * S, D), F32, kind="Internal").ap()
        slot_codes = nc.dram_tensor("slot_codes", (NE * B * S + BT, 1), U32, kind="Internal").ap()
        dram_sems = {}

        def signal_for(name):
            if name not in dram_sems:
                dram_sems[name] = [sem(f"w_{name}"), 0]
            dram_sems[name][1] += 16
            return (dram_sems[name][0], 16, dram_sems[name][1])

        def xt(buf, b, c):
            return buf[:, c, b * S:(b + 1) * S]

        def xt_tile(b, t):
            c0 = b * S + t * P
            return [(xt_hi[:, c, c0:c0 + P], xt_lo[:, c, c0:c0 + P]) for c in range(KC)]

        x_ready = [None] * B
        xt_ready = [None] * B
        ln_turn = [0]
        ln_readers = [[], []]

        def layernorm(b, r, r_ready, xt_readers, last=False):
            i = ln_turn[0] % 2
            ln_turn[0] += 1
            for t in range(TT):
                t_st = dve.do(lambda e, t=t: e.bn_stats(ln_stats[:, i, t, :], r[:, t, :]), r_ready if t == 0 else ())
            for t in range(TT):
                t_mv = dve.do(lambda e, t=t: e.bn_aggr(ln_mv[:, i, t, :], ln_stats[:, i, t, :]),
                              [t_st, *ln_readers[i]])
            t_ve = ts(dve, ln_rstd[:, i, :], ln_mv[:, i, :, 1], EPS_LN, None, ALU.add, after=[t_mv])
            t_rs = tt(pool, ln_rstd[:, i, :], ln_rstd[:, i, :], minus_half[:, 0:TT], ALU.pow, [t_ve, t_const])
            yield
            if last:
                yield
            t_s = stt(ln_mv[:, i, :, 0], ln_mv[:, i, :, 0], -1.0, ln_rstd[:, i, :], ALU.mult, ALU.mult, [t_rs])
            for t in range(TT):
                t_x = act_do(x_tok[:, b * TT + t, :], r[:, t, :], ACT.Identity, [t_s],
                             scale=ln_rstd[:, i, t:t + 1], bias=ln_mv[:, i, t, 0:1])
            x_ready[b] = ln_readers[i] = [t_x]
            if last:
                return
            r_bufs.give(r, [t_x])
            yield
            bank, free = banks.take()
            t_tr = transposes(bank, [(bank[:, c * S + t * P:c * S + (t + 1) * P],
                                      x_tok[:, b * TT + t, c * P:(c + 1) * P])
                                     for c in range(KC) for t in range(TT)], [t_x, t_const, *free])
            hi = xt_hi[:, :, b * S:(b + 1) * S]
            lo = xt_lo[:, :, b * S:(b + 1) * S]
            done = split_bank(hi, lo, bank[:, :].rearrange("p (c t) -> p c t", c=KC), [t_tr, *xt_readers])
            xt_ready[b] = done
            banks.give(bank, done)

        staging = [sb(f"staging{i}", [P, KC * 3 * D], F32, mid) for i in range(2)]
        staging_t = Turns(list(enumerate(staging)))

        def weights(split, hi, lo, source, after=()):
            (i, raw), free = staging_t.take()
            n = int(np.prod(source.shape[1:]))
            raw_view = raw[0:source.shape[0], 0:n].rearrange("p (a b) -> p a b", a=source.shape[1])
            t_l = load(f"staging{i}", raw_view, source, free)
            toks = split(hi, lo, raw_view, [t_l, *after])
            staging_t.give((i, raw), toks)
            return toks

        plan = []

        def at(round_, gen, behind=0, carry=False):
            plan.append((round_, len(plan), behind, carry, gen))

        t_ident = load("ident", ident[:, :], a["ident"])
        t_const = pool.do(lambda e: e.memset(minus_half[:, :], -0.5))
        xraw = Turns([sb(f"xraw{i}", [P, KC, S], F32, early) for i in range(2)])
        wqkv = [sb(f"wqkv_{n}", [P, KC, 3 * D], F32R, early) for n in ("hi", "lo")]
        bqkv = sb("bqkv", [P, 6], F32, early)
        wconv = sb("wconv", [P, KC, 3], F32, early)
        t_bc, t_mask_a = [], []

        def load_x(b):
            buf, free = xraw.take()
            t_l = load(f"xT{b % 2}", buf[:, :, :], a["xT"][:, :, b * S:(b + 1) * S], free)
            t_x = load(f"x{b % 2}", x_tok[:, b * TT:(b + 1) * TT, :], a["x"][:, b * TT:(b + 1) * TT, :])
            x_ready[b] = [t_x]
            hi = xt_hi[:, :, b * S:(b + 1) * S]
            lo = xt_lo[:, :, b * S:(b + 1) * S]
            xt_ready[b] = (split_dve if b < 2 else split_pool)(hi, lo, buf[:, :, :], [t_l])
            xraw.give(buf, xt_ready[b])
            return
            yield

        t_rt, t_empty = [], []

        def load_before():
            (i, raw), free = staging_t.take()
            t_l = load(f"staging{i}", raw[:, 0:P], a["before"], free)
            t_c = copy(dve, before[:, :], raw[:, 0:P], [t_l])
            staging_t.give((i, raw), [t_c])
            return [t_c]

        def routing_constants():
            t_rt.extend([load("gw", gw_raw[:, :, :], a["gate_w"]),
                         load("iota8", iota8[:, :], a["iota8"]), 
                         load("codes", codes[:, :, :], a["codes"]), load("block_no", block_no[:, :], a["block_no"]),
                         load("row_no", row_no[:, :], a["row_no"]),
                         *load_before(), pool.do(lambda e: e.memset(f(ones_r[:, :]), 1.0)),
                         pool.do(lambda e: e.memset(f(seen[:, :]), 0.0))])
            t_none = pool.do(lambda e: e.memset(none_t[:, :], NONE))
            t_empty.append(sp.do(lambda e: e.dma_start(slot_codes.rearrange("(p n) one -> p (n one)", p=P),
                                                       none_t[:, :]), [t_none], signal_for("empty")))
            return
            yield

        at(0, load_x(0))
        t_wq = []

        at(5, routing_constants())

        def split_wqkv():
            t_wq.extend(weights(split_dve, wqkv[0][:, :, :], wqkv[1][:, :, :], a["A_wqkv"]))
            t_bc.extend([load("a_bias", bqkv[:, :], a["A_b"]), load("a_conv", wconv[:, :, :], a["A_wconv"])])
            t_mask_a.append(load("mask_a", mask_a[:, :], a["mask_a"]))
            return
            yield
        at(0, split_wqkv())
        for b in range(1, B):
            at(max(0, b - 2), load_x(b))

        NPIECE = 2 * KC + 2 * FC + 2
        first_pieces = ExitStack()
        wraw_t = Turns([(i, sb(f"wraw{i}", [P, CW], F32, first_pieces, "right")) for i in range(3)])
        wpiece_t = Turns([[sb(f"wpiece_{n}0", [P, CW], F32R, first_pieces, "right") for n in ("hi", "lo")]])
        piece_order = [(s, n) for s in range(NSB) for n in range(NPIECE)]
        n_loaded, loaded, pieces = [0], [], {}

        def want():
            while wraw_t.free and n_loaded[0] < len(piece_order):
                (i, raw), free = wraw_t.take()
                s, n = piece_order[n_loaded[0]]
                n_loaded[0] += 1
                loaded.append((s, n, i, raw, load(f"piece{i}", raw[:, :], a["C_w"][n], free)))
            if loaded and wpiece_t.free:
                s, n, i, raw, t_l = loaded.pop(0)
                (hi, lo), w_free = wpiece_t.take()
                toks = split_pool(hi[:, :], lo[:, :], raw[:, :], [t_l, *w_free])
                wraw_t.give((i, raw), toks)
                pieces[(s, n)] = ((hi, lo), toks)

        def first_piece():
            want()
            return
            yield
        at(4, first_piece())

        qa = [[sb(f"qa_{n}{i}", [P, KC, S], F32R, early) for n in ("hi", "lo")] for i in range(2)]
        ka = [[sb(f"ka_{n}{i}", [P, KC, S], F32R, early) for n in ("hi", "lo")] for i in range(2)]
        qa_t, ka_t = Turns(qa), Turns(ka)
        vpad_t = Turns([sb(f"vpad{i}", [P, KC, S + 2], F32, early) for i in range(2)])
        ucv_t = Turns([(sb(f"uT{i}", [P, KC, S], F32, early), sb(f"cT{i}", [P, KC, S], F32, early)) for i in range(2)])
        utok_t = Turns([sb(f"utok{i}", [P, TT, D], F32, early) for i in range(2)])
        ctok_t = Turns([[sb(f"ctok_{n}{i}", [P, TT, D], F32R, early) for n in ("hi", "lo")] for i in range(2)])
        sm_t = Turns([sb(f"scoreA{i}", [P, 3 * P], F32, early) for i in range(2)])
        pa_t = Turns([sb(f"probA{i}", [P, 3 * P], F32, early) for i in range(2)])
        pta_t = Turns([[sb(f"probTA_{n}{i}", [P, 3 * P], F32R, early) for n in ("hi", "lo")] for i in range(2)])
        sma_t = Turns([sb(f"smallA{i}", [P, 16], F32, early) for i in range(3)])
        junk_a = sb("junkA", [P, P], F32, early)
        t_vz = [pool.do(lambda e, v=v: e.memset(v[:, :, :], 0.0)) for v, _ in vpad_t.free]
        scale_a = float(D) ** -0.5

        def attention_a(b):
            (qh, ql), q_free = qa_t.take()
            (kh, kl), k_free = ka_t.take()
            vp, v_free = vpad_t.take()
            (uT, cT), uc_free = ucv_t.take()
            need = [*xt_ready[b], *t_wq, *t_bc]
            done = []
            for which in range(3):
                bank, free = banks.take()
                for c in range(KC):
                    col = (which * KC + c) * P
                    t_mm = product(bank[:, c * S:(c + 1) * S],
                                   [((wqkv[0][:, k, col:col + P], wqkv[1][:, k, col:col + P]),
                                     (xt(xt_hi, b, k), xt(xt_lo, b, k))) for k in range(KC)],
                                   [*need, *free])
                halves = [(bank[:, c * S:(c + 1) * S], bqkv[:, which * KC + c:which * KC + c + 1]) for c in range(KC)]
                if which < 2:
                    hi, lo = ((qh, ql), (kh, kl))[which]
                    reads = split_biased([(hi[:, c, :], lo[:, c, :], *halves[c]) for c in range(KC)],
                                         [t_mm, *t_bc, *(q_free, k_free)[which]])
                else:
                    reads = [act_do(vp[:, c, 1:S + 1], ps, ACT.Identity, [t_mm, *t_vz, *v_free], bias=bias)
                             for c, (ps, bias) in enumerate(halves)]
                banks.give(bank, reads)
                done.append(reads)
            t_v = done[2]
            t_proj = t_mm
            t_c = []
            for c in range(KC):
                w = [wconv[:, c, j:j + 1] for j in range(3)]
                t_u = ts(pool, uT[:, c, :], vp[:, c, 2:S + 2], w[2], 1.0, ALU.mult, ALU.mult, after=[*t_v, *uc_free])
                t_1 = stt(cT[:, c, :], vp[:, c, 0:S], w[0], uT[:, c, :], ALU.mult, ALU.add, [t_u])
                t_c.append(stt(cT[:, c, :], vp[:, c, 1:S + 1], w[1], cT[:, c, :], ALU.mult, ALU.add, [t_1]))
            vpad_t.give(vp, t_c)
            yield
            bank, free = banks.take()
            t_s = product(bank[:, 0:P], [((qh[:, k, 0:P], ql[:, k, 0:P]), (kh[:, k, 0:P], kl[:, k, 0:P]))
                                         for k in range(KC)], [*done[0], *done[1], *free])
            t_s = product(bank[:, P:3 * P], [((qh[:, k, P:S], ql[:, k, P:S]), (kh[:, k, :], kl[:, k, :]))
                                             for k in range(KC)])
            qa_t.give((qh, ql), [t_s])
            ka_t.give((kh, kl), [t_s])
            bank_c, free_c = banks.take()
            t_ct = transposes(bank_c, [(bank_c[:, t * D + c * P:t * D + (c + 1) * P], cT[:, c, t * P:(t + 1) * P])
                                       for t in range(TT) for c in range(KC)], [*t_c, t_ident, *free_c])
            bank_u, free_u = banks.take()
            t_ut = transposes(bank_u, [(bank_u[:, t * D + c * P:t * D + (c + 1) * P], uT[:, c, t * P:(t + 1) * P])
                                       for t in range(TT) for c in range(KC)], free_u)
            ucv_t.give((uT, cT), [t_ut])
            sm, sm_free = sm_t.take()
            pr, pr_free = pa_t.take()
            small, small_free = sma_t.take()
            t_m = tt(dve, sm[:, :], bank[:, 0:3 * P], mask_a[:, :], ALU.add, [t_s, *t_mask_a, *sm_free])
            banks.give(bank, [t_m])
            mx, nmx, den, dia, rin, ndg = (small[:, 2 * j:2 * j + 2] for j in range(6))
            dve.do(lambda e: e.tensor_reduce(mx[:, 0:1], sm[:, 0:P], AX.X, ALU.max), [t_m, *small_free])
            t_mx = dve.do(lambda e: e.tensor_reduce(mx[:, 1:2], sm[:, P:3 * P], AX.X, ALU.max))
            t_nm = ts(dve, nmx, mx, -scale_a, None, ALU.mult, after=[t_mx])
            act_do(pr[:, 0:P], sm[:, 0:P], ACT.Exp, [t_nm, *pr_free], scale=scale_a, bias=nmx[:, 0:1],
                   accum_out=den[:, 0:1])
            t_p = act_do(pr[:, P:3 * P], sm[:, P:3 * P], ACT.Exp, scale=scale_a, bias=nmx[:, 1:2],
                         accum_out=den[:, 1:2])
            sm_t.give(sm, [t_p])
            (ch, cl), c_free = ctok_t.take()
            t_cs = split_bank(ch[:, :, :], cl[:, :, :], bank_c[:, :].rearrange("p (t d) -> p t d", t=TT),
                              [t_ct, *c_free])
            banks.give(bank_c, t_cs)
            utok, u_free = utok_t.take()
            t_uc = act_do(utok[:, :, :], bank_u[:, :].rearrange("p (t d) -> p t d", t=TT), ACT.Identity,
                          [t_ut, *u_free])
            banks.give(bank_u, [t_uc])
            diag_cols = (slice(0, P), slice(2 * P, 3 * P))
            t_j = None
            for t in range(TT):
                t_j = stt(junk_a[:, :], pr[:, diag_cols[t]], 1.0, ident[:, :], ALU.mult, ALU.mult,
                          [t_p, t_ident] if t_j is None else [t_j], accum_out=dia[:, t:t + 1])
            t_ri = dve.do(lambda e: e.reciprocal(rin, den), [t_p])
            t_nd = stt(ndg, dia, -1.0, rin, ALU.mult, ALU.mult, [t_ri, t_j])
            yield
            bank, free = banks.take()
            t_t = transposes(bank, [(bank[:, j * P:(j + 1) * P], pr[:, j * P:(j + 1) * P]) for j in range(3)],
                             [t_p, *free])
            pa_t.give(pr, [t_t, t_j])
            (ph, pl), p_free = pta_t.take()
            t_ps = split_bank(ph[:, :], pl[:, :], bank[:, 0:3 * P], [t_t, *p_free])
            banks.give(bank, t_ps)
            yield
            bank, free = banks.take()
            t_o = product(bank[:, 0:D], [((ph[:, 0:P], pl[:, 0:P]), (ch[:, 0, :], cl[:, 0, :]))],
                          [*t_ps, *t_cs, *free])
            t_o = product(bank[:, D:2 * D], [((ph[:, (1 + j) * P:(2 + j) * P], pl[:, (1 + j) * P:(2 + j) * P]),
                                              (ch[:, j, :], cl[:, j, :])) for j in range(TT)])
            pta_t.give((ph, pl), [t_o])
            ctok_t.give((ch, cl), [t_o])
            r, r_free = r_bufs.take()
            for t in range(TT):
                t_r = stt(r[:, t, :], bank[:, t * D:(t + 1) * D], rin[:, t:t + 1], x_tok[:, b * TT + t, :],
                          ALU.mult, ALU.add, [t_o, t_ri, *x_ready[b], *r_free])
                t_r2 = stt(r[:, t, :], utok[:, t, :], ndg[:, t:t + 1], r[:, t, :], ALU.mult, ALU.add,
                           [t_r, t_nd, t_uc])
            banks.give(bank, [t_r])
            utok_t.give(utok, [t_r2])
            sma_t.give(small, [t_r2])
            yield from layernorm(b, r, [t_r2], [t_proj])

        for b in range(B):
            at(1 + b, attention_a(b), 1)

        wv_b = [sb(f"bwv_{n}", [P, KC, P], F32R, early) for n in ("hi", "lo")]
        wt_b = [sb(f"bwt_{n}", [CK, 2, P], F32R, early) for n in ("hi", "lo")]
        b_bias = sb("b_bias", [P, 2], F32, early)
        t_ones = pool.do(lambda e: e.memset(ones[:, :], 1.0))
        t_bb = load("b_bias", b_bias[:, :], a["B_b"])
        t_bw = []

        def weights_b():
            t_bw.extend(weights(split_pool, wv_b[0][:, :, :], wv_b[1][:, :, :], a["B_wv"]))
            t_bw.extend(weights(split_pool, wt_b[0][:, :, :], wt_b[1][:, :, :], a["B_wt"]))
            return
            yield
        at(2, weights_b())

        def load_context(b):
            (i, raw), free = ctx_raw.take()
            t_l = load(f"ctx{i}", raw[:, :, :], a["ctxT"][:, :, b * S:(b + 1) * S], free)
            (hi, lo), c_free = ctx_t.take()
            toks = split_pool(hi[:, :, :], lo[:, :, :], raw[:, :, :], [t_l, *c_free])
            ctx_raw.give((i, raw), toks)
            return (hi, lo), toks

        vt_t = Turns([[sb(f"vt_{n}{i}", [P, 2, S], F32R, early) for n in ("hi", "lo")] for i in range(4)])
        sq_t = Turns([sb(f"sq{i}", [P, 2, S], F32, early) for i in range(2)])
        rn_t = Turns([sb(f"rn{i}", [P, 4], F32, early) for i in range(4)])
        dg_t = Turns([sb(f"dgt{i}", [P, TT, P], F32, early) for i in range(2)])
        rec_t = Turns([sb(f"recB{i}", [P, TT, S], F32, early) for i in range(2)])

        def cosine_b(b):
            (cxh, cxl), t_cx = load_context(b)
            yield
            bank, free = banks.take()
            t_v = product(bank[:, 0:S], [((wv_b[0][:, k, :], wv_b[1][:, k, :]), (xt(xt_hi, b, k), xt(xt_lo, b, k)))
                                         for k in range(KC)], [*xt_ready[b], *t_bw, *free])
            t_t = product(bank[:, S:2 * S], [((wt_b[0][:, k, :], wt_b[1][:, k, :]), (cxh[:, k, :], cxl[:, k, :]))
                                             for k in range(2)], t_cx)
            ctx_t.give((cxh, cxl), [t_t])
            (vh, vl), vt_free = vt_t.take()
            sq, sq_free = sq_t.take()
            halves = [(bank[:, i * S:(i + 1) * S], b_bias[:, i:i + 1]) for i in range(2)]
            for i, (ps, bias) in enumerate(halves):
                t_q = act_do(sq[:, i, :], ps, ACT.Square, [t_t, t_bb, *sq_free], bias=bias)
            toks = [t_q, *split_biased([(vh[:, i, :], vl[:, i, :], *halves[i]) for i in range(2)], [t_t, *vt_free])]
            banks.give(bank, toks)
            yield
            bank, free = banks.take()
            for i in range(2):
                for t in range(TT):
                    j = i * TT + t
                    t_n = matmuls([(bank[:, j:j + 1], sq[:, i, t * P:(t + 1) * P], ones[:, 0:1])],
                                  [*toks, t_ones, *free])
            sq_t.give(sq, [t_n])
            rn, rn_free = rn_t.take()
            t_rn = copy(dve, rn[:, :], bank[:, 0:4], [t_n, *rn_free])
            banks.give(bank, [t_rn])
            t_rn = tt(pool, rn[:, :], rn[:, :], minus_half[:, :], ALU.pow, [t_rn, t_const])
            yield
            dgt, dg_free = dg_t.take()
            for t in range(TT):
                t_d = ts(dve, dgt[:, t, :], ident[:, :], rn[:, TT + t:TT + t + 1], None, ALU.mult,
                         after=[t_rn, t_ident, *dg_free])
            yield
            bank_r, free = banks.take()
            for t in range(TT):
                t_r = matmuls([(bank_r[:, t * P:(t + 1) * P], ones[:, :], dgt[:, t, :])], [t_d, *free])
            dg_t.give(dgt, [t_r])
            bank, free = banks.take()
            for t in range(TT):
                t_dot = product(bank[:, t * S:(t + 1) * S],
                                [((vh[:, 0, t * P:(t + 1) * P], vl[:, 0, t * P:(t + 1) * P]), (vh[:, 1, :], vl[:, 1, :]))],
                                free)
            vt_t.give((vh, vl), [t_dot])
            rec, rec_free = rec_t.take()
            r, r_free = r_bufs.take()
            for t in range(TT):
                t_rec = ts(dve, rec[:, t, :], bank_r[:, 0:S], rn[:, t:t + 1], 1e8, ALU.mult, ALU.min,
                           after=[t_r, *rec_free])
            banks.give(bank_r, [t_rec])
            rn_t.give(rn, [t_rec])
            t_m = tt(dve, rec[:, :, :], bank[:, :].rearrange("p (t s) -> p t s", t=TT), rec[:, :, :], ALU.mult,
                     [t_dot, t_rec])
            banks.give(bank, [t_m])
            t_add = tt(dve, r[:, :, :], rec[:, :, :], x_tok[:, b * TT:(b + 1) * TT, :], ALU.add,
                       [t_m, *x_ready[b], *r_free])
            rec_t.give(rec, [t_add])
            yield from layernorm(b, r, [t_add], [t_v])

        first_b = 6
        for b in range(B):
            at(first_b + b, cosine_b(b))

        def run():
            todo = sorted(plan)
            plan.clear()
            live, r = [], 0
            while not all(entry[3] for entry in [*todo, *live]):
                while todo and todo[0][0] <= r:
                    live.append(todo.pop(0))
                live.sort(key=lambda entry: entry[2])
                live = [entry for entry in live if next(entry[4], "end") != "end"]
                r += 1
            for entry in [*live, *todo]:
                at(0, entry[4])

        run()
        early.close()
        t_early = fence()
        dw_scope = ExitStack()
        dw = [sb(f"dw_{n}", [P, KC, 3 * D], F32R, dw_scope) for n in ("hi", "lo")]
        t_dw = []
        for n in ("1", "2"):
            wpiece_t.give([sb(f"wpiece_{x}{n}", [P, CW], F32R, late, "right") for x in ("hi", "lo")], t_early)
        hid = [[sb(f"hid{i}_{n}", [P, FC, SB], F32R, late, "right") for n in ("hi", "lo")] for i in range(2)]
        hf_t = Turns([sb(f"hf{i}", [P, SB], F32, late, "right") for i in range(2)], t_early)
        sg_t = Turns([sb(f"sg{i}", [P, SB], F32, late, "right") for i in range(2)], t_early)
        scl = sb("ffn_scales", [P, 4, FC], F32, late, "right")
        s3b = sb("ffn_s3", [P, D], F32, late, "right")
        t_scl = [load("ffn_s", scl[:, :, :], a["C_s"], t_early), load("ffn_s3", s3b[:, :], a["C_s3"], t_early)]

        def ffn():
            want(), want()
            hid_readers = [t_early, t_early]
            for s in range(NSB):
                cols = slice(s * SB, (s + 1) * SB)
                seqs = range(s * BPS, (s + 1) * BPS)
                x_in = [(xt_hi[:, k, cols], xt_lo[:, k, cols]) for k in range(KC)]
                need = [t for b in seqs for t in xt_ready[b]]
                chunk_ready = []
                for n in range(4):
                    want()
                    (wh, wl), t_w = pieces.pop((s, n))
                    step_norms()
                    for oo in range(2):
                        o = 2 * n + oo
                        pair = []
                        for mat in range(2):
                            bank, free = banks.take()
                            terms = []
                            for k in range(KC):
                                c0 = ((mat * 2 + oo) * KC + k) * P
                                terms.append(((wh[:, c0:c0 + P], wl[:, c0:c0 + P]), x_in[k]))
                            t_mm = product(bank[:, :], terms, [*need, *t_w, *free])
                            pair.append((bank, t_mm))
                        sg, sg_free = sg_t.take()
                        hf, hf_free = hf_t.take()
                        t_sg = act_do(sg[:, :], pair[0][0][:, :], ACT.Silu, [pair[0][1], *t_scl, *sg_free],
                                      scale=scl[:, 0, o:o + 1])
                        banks.give(pair[0][0], [t_sg])
                        t_h = stt(hf[:, :], pair[1][0][:, :], scl[:, 1, o:o + 1], sg[:, :], ALU.mult, ALU.mult,
                                  [pair[1][1], t_sg, *t_scl, *hf_free])
                        banks.give(pair[1][0], [t_h])
                        sg_t.give(sg, [t_h])
                        toks = split_dve(hid[0][0][:, o, :], hid[0][1][:, o, :], hf[:, :], [t_h, *hid_readers[0]])
                        hf_t.give(hf, toks)
                        chunk_ready.append(toks)
                    wpiece_t.give((wh, wl), [t_mm])
                for layer in range(2):
                    src, dst = hid[layer % 2], hid[(layer + 1) % 2]
                    new_ready = []
                    for o in range(FC):
                        want()
                        (wh, wl), t_w = pieces.pop((s, 4 + layer * FC + o))
                        bank, free = banks.take()
                        t_mm = product(bank[:, :], [((wh[:, k * P:(k + 1) * P], wl[:, k * P:(k + 1) * P]),
                                                     (src[0][:, k, :], src[1][:, k, :]), chunk_ready[k])
                                                    for k in range(FC)], [*t_w, *free])
                        wpiece_t.give((wh, wl), [t_mm])
                        hf, hf_free = hf_t.take()
                        t_g = act_do(hf[:, :], bank[:, :], ACT.Gelu, [t_mm, *t_scl, *hf_free],
                                     scale=scl[:, 2 + layer, o:o + 1])
                        banks.give(bank, [t_g])
                        toks = split_dve(dst[0][:, o, :], dst[1][:, o, :], hf[:, :],
                                         [t_g, *hid_readers[(layer + 1) % 2]])
                        hf_t.give(hf, toks)
                        new_ready.append(toks)
                    hid_readers[layer % 2] = [t_mm]
                    chunk_ready = new_ready
                if s == 0:
                    t_dw.extend(weights(split_dve, dw[0][:, :, :], dw[1][:, :, :], a["D_w"], t_early))
                src = hid[0]
                want(), want()
                halves = [pieces.pop((s, NPIECE - 2 + j)) for j in range(2)]
                for bi, b in enumerate(seqs):
                    bank, free = banks.take()
                    for t in range(TT):
                        c0 = bi * S + t * P
                        terms = []
                        for k in range(FC):
                            (wh, wl), t_w = halves[k // 4]
                            w0 = (k % 4) * D
                            terms.append(((src[0][:, k, c0:c0 + P], src[1][:, k, c0:c0 + P]),
                                          (wh[:, w0:w0 + D], wl[:, w0:w0 + D]), [*t_w, *chunk_ready[k]]))
                        t_mm = product(bank[:, t * D:(t + 1) * D], terms, free)
                    r, r_free = r_bufs.take()
                    for t in range(TT):
                        t_y = tt(dve, r[:, t, :], bank[:, t * D:(t + 1) * D], s3b[:, :], ALU.mult,
                                 [t_mm, *t_scl, *r_free])
                    banks.give(bank, [t_y])
                    t_r = tt(dve, r[:, :, :], r[:, :, :], x_tok[:, b * TT:(b + 1) * TT, :], ALU.add,
                             [t_y, *x_ready[b]])
                    norm = layernorm(b, r, [t_r], [t_mm])
                    next(norm)
                    norms.append(norm)
                for (wh, wl), _ in halves:
                    wpiece_t.give((wh, wl), [t_mm])
                hid_readers[0] = [t_mm]

        norms = []

        def step_norms():
            norms[:] = [g for g in norms if next(g, "end") != "end"]

        ffn()
        late.close()
        first_pieces.close()

        t_late = fence()
        part = ExitStack()
        sbp = lambda name, shape, dt=F32: sb(name, shape, dt, part, "right")
        v_heads = sbp("v_heads", [P, TT, NH, P], F32R)
        acc_sb_t = Turns([sbp(f"accT{i}", [P, 2, S]) for i in range(3)])
        ctok2_t = Turns([sbp(f"ctxtok{i}", [P, TT, D]) for i in range(2)])
        rin_t = Turns([sbp(f"crin{i}", [P, TT * HPB]) for i in range(2)])
        cT_t = Turns([[sbp(f"ctxT_{n}{i}", [P, KC, S], F32R) for n in ("hi", "lo")] for i in range(1)])
        sum_t = Turns([sbp(f"csum{i}", [P, TT * HPB, DH]) for i in range(2)])
        vf_t = Turns([sbp(f"vf{i}", [P, TT, D]) for i in range(2)])
        xb_t = Turns([sbp(f"xb{i}", [P, TT, D]) for i in range(1)])
        t_z = pool.do(lambda e: e.memset(f(v_heads[:, :, :, :]), 0.0), t_late)
        for g in range(VH):
            heads = v_heads[:, :, g::VH, g * VW + 2 * DH:g * VW + 2 * DH + 1]
            t_z = pool.do(lambda e, heads=heads: e.memset(f(heads), 1.0), [t_z])
        v_readers = [[t_z] for _ in range(NVT)]

        def place(state, b, i):
            st = state[b]
            n = min(VH, NH - i * VH)
            step = P + VW if n > 1 else P
            cols = v_heads[:, :, :, :].rearrange("p t h c -> p t (h c)")[:, :, i * VH * P:i * VH * P + n * step]
            cols = cols.rearrange("p t (h c) -> p t h c", h=n)
            hi, lo = cols[:, :, :, 0:DH], cols[:, :, :, DH:2 * DH]
            src = st["vf"][:, :, i * VH * DH:(i * VH + n) * DH].rearrange("p t (h d) -> p t h d", h=n)
            st["v_ready"][i] = split_pool(hi, lo, src, [st["t_vf"], *v_readers[i]])
            if i == NVT - 1:
                vf_t.give(st["vf"], [pool.last()])
            return
            yield

        def drain(state, b, i, delta):
            st = state[b]
            bank, t_acc = st["accs"][i]
            acc_sb, s_free = acc_sb_t.take()
            t_e = act_do(acc_sb[:, :, :], bank[:, :].rearrange("p (j s) -> p j s", j=2), ACT.Identity,
                         [t_acc, *s_free])
            banks.give(bank, [t_e])
            yield
            if i == 0:
                st["ctok"], st["ctok_free"] = ctok2_t.take()
            h0, nh = HPB * i, min(HPB, NH - HPB * i)
            bank, free = banks.take()
            parts = []
            for t in range(TT):
                for j in range(2):
                    rows = VW * min(VH, NH - (2 * i + j) * VH)
                    c0 = (t * nh + j * VH) * VW
                    parts.append((bank[:, c0:c0 + rows], acc_sb[0:rows, j, t * P:(t + 1) * P]))
            t_tr = transposes(bank, parts, [t_e, *free])
            acc_sb_t.give(acc_sb, [t_tr])
            csum, cs_free = sum_t.take()
            rin, ri_free = rin_t.take()
            n = TT * nh
            view = bank[:, 0:n * VW].rearrange("p (h w) -> p h w", w=VW)
            hi_lo = view[:, :, 0:2 * DH].rearrange("p h (two d) -> p h d two", two=2)
            t_sum = dve.do(lambda e: e.tensor_reduce(csum[:, 0:n, :], hi_lo, AX.X, ALU.add), [t_tr, *cs_free])
            t_den = ts(dve, rin[:, 0:n], view[:, :, 2 * DH], delta, None, ALU.add, after=[t_tr, *ri_free])
            banks.give(bank, [t_sum, t_den])
            t_ri = dve.do(lambda e: e.reciprocal(rin[:, 0:n], rin[:, 0:n]), [t_den])
            t_ct = tt(dve, st["ctok"][:, :, h0 * DH:(h0 + nh) * DH].rearrange("p t (h d) -> p t h d", h=nh),
                      csum[:, 0:n, :].rearrange("p (t h) d -> p t h d", t=TT),
                      rin[:, 0:n].rearrange("p (t h) -> p t h", t=TT)[:, :, :, None].to_broadcast([P, TT, nh, DH]),
                      ALU.mult, [t_ri, t_sum, *st["ctok_free"]])
            sum_t.give(csum, [t_ct])
            rin_t.give(rin, [t_ct])
            st["t_ct"] = t_ct

        def finish_heads(b, st, wo, bo, t_wo, then=None):
            ctok, t_ct, xt_readers = st["ctok"], st["t_ct"], [st["xt_last"]]
            xb, xb_free = xb_t.take()
            for t in range(TT):
                t_xb = tt(pool, xb[:, t, :], x_tok[:, b * TT + t, :], bo[:, :], ALU.add, [*x_ready[b], *t_wo, *xb_free])
            bank, free = banks.take()
            t_tr = transposes(bank, [(bank[:, c * S + t * P:c * S + (t + 1) * P], ctok[:, t, c * P:(c + 1) * P])
                                     for c in range(KC) for t in range(TT)], [t_ct, *free])
            ctok2_t.give(ctok, [t_tr])
            (ch, cl), ct_free = cT_t.take()
            t_cs = split_bank(ch[:, :, :], cl[:, :, :], bank[:, :].rearrange("p (c s) -> p c s", c=KC),
                              [t_tr, *ct_free])
            banks.give(bank, t_cs)
            yield
            bank, free = banks.take()
            for t in range(TT):
                t_y = product(bank[:, t * D:(t + 1) * D],
                              [((ch[:, c, t * P:(t + 1) * P], cl[:, c, t * P:(t + 1) * P]), (wo[0][:, c, :], wo[1][:, c, :]))
                               for c in range(KC)], [*t_cs, *t_wo, *free])
            cT_t.give((ch, cl), [t_y])
            r, r_free = r_bufs.take()
            t_r = tt(dve, r[:, :, :], bank[:, :].rearrange("p (t d) -> p t d", t=TT), xb[:, :, :], ALU.add,
                     [t_y, t_xb, *r_free])
            banks.give(bank, [t_r])
            xb_t.give(xb, [t_r])
            yield from layernorm(b, r, [t_r], xt_readers)
            if then is not None:
                yield
                yield from then(b)

        dpart = ExitStack()
        sbd = lambda name, shape, dt=F32: sb(name, shape, dt, dpart)
        dwo = [sbp(f"dwo_{n}", [P, KC, D], F32R) for n in ("hi", "lo")]
        proj = [sbd(f"proj_{n}", [P, NH // 2, P], F32R) for n in ("hi", "lo")]
        dbias = sbd("dbias", [P, 2 * KC])
        dbv = sbd("dbv", [P, D])
        dbo = sbp("dbo", [P, D])
        mask_d = sbd("mask_d", [P, 3 * P])
        t_db = [load("d_b", dbias[:, :], a["D_b"], t_late), load("d_bv", dbv[:, :], a["D_bv"], t_late),
                load("d_bo", dbo[:, :], a["D_bo"], t_late), load("d_mask", mask_d[:, :], a["mask_d"], t_late)]
        t_dp = weights(split_dve, proj[0][:, :, :], proj[1][:, :, :], a["D_proj"], t_late)
        t_dwo = weights(split_pool, dwo[0][:, :, :], dwo[1][:, :, :], a["D_wo"], t_late)
        qk_t = Turns([[[sbd(f"{w}d_{n}{i}", [P, KC, S], F32R) for n in ("hi", "lo")] for w in "qk"] for i in range(2)],
                     t_late)
        feat_t = Turns([[sbd(f"feat_{n}{i}", [P, 2, S], F32R) for n in ("hi", "lo")] for i in range(3)], t_late)
        awm_t = Turns([sbd(f"awm{i}", [P, 3 * P]) for i in range(4)], t_late)
        aw_t = Turns([[sbd(f"aw_{n}{i}", [P, 3 * P], F32R) for n in ("hi", "lo")] for i in range(6)], t_late)
        state_d = {}

        def prelude_d(b):
            ((qh, ql), (kh, kl)), qk_free = qk_t.take()
            need = [*xt_ready[b], *t_dw, *t_db]
            toks = []
            for which, (hi, lo) in enumerate(((qh, ql), (kh, kl))):
                bank, free = banks.take()
                for c in range(KC):
                    col = (which * KC + c) * P
                    t_mm = product(bank[:, c * S:(c + 1) * S],
                                   [((dw[0][:, k, col:col + P], dw[1][:, k, col:col + P]),
                                     (xt(xt_hi, b, k), xt(xt_lo, b, k))) for k in range(KC)], [*need, *free])
                reads = split_biased([(hi[:, c, :], lo[:, c, :], bank[:, c * S:(c + 1) * S],
                                       dbias[:, which * KC + c:which * KC + c + 1]) for c in range(KC)],
                                     [t_mm, *t_db, *qk_free])
                banks.give(bank, reads)
                toks += reads
                yield
            bank, free = banks.take()
            for t in range(TT):
                t_mm = product(bank[:, t * D:(t + 1) * D],
                               [(sh, (dw[0][:, k, 2 * D:3 * D], dw[1][:, k, 2 * D:3 * D]))
                                for k, sh in enumerate(xt_tile(b, t))], free)
            vf, vf_free = vf_t.take()
            for t in range(TT):
                t_vf = tt(dve, vf[:, t, :], bank[:, t * D:(t + 1) * D], dbv[:, :], ALU.add, [t_mm, *vf_free, *t_late])
            banks.give(bank, [t_vf])
            state_d[b] = dict(q=(qh, ql), k=(kh, kl), qk_ready=toks, vf=vf, t_vf=t_vf, xt_last=t_mm,
                           v_ready=[None] * NVT, accs=[])

        def pair_d(b, j):
            st = state_d[b]
            c = 2 * j // (NH // KC)
            pair_bufs, f_free = feat_t.take()
            feat_hi, feat_lo = pair_bufs
            (qfh, kfh), (qfl, kfl) = ((x[:, 0, :], x[:, 1, :]) for x in pair_bufs)
            bank, free = banks.take()
            for w, (hi, lo) in enumerate((st["q"], st["k"])):
                t_f = product(bank[:, w * S:(w + 1) * S],
                              [((proj[0][:, j, :], proj[1][:, j, :]), (hi[:, c, :], lo[:, c, :]))],
                              [*st["qk_ready"], *t_dp, *free])
            if j == NH // 2 - 1:
                qk_t.give((st["q"], st["k"]), [t_f])
            both = bank[:, :].rearrange("p (w s) -> p w s", w=2)
            t_hi = act_do(feat_hi[:, :, :], both, ACT.Relu, [t_f, *f_free])
            t_lo = stt(feat_lo[:, :, :], both, 0.0, f(feat_hi[:, :, :]), ALU.max, ALU.subtract, [t_hi])
            f_ready = [t_hi, t_lo]
            banks.give(bank, f_ready)
            yield
            yield
            aws = []
            for g in range(2):
                rows = slice(g * M, (g + 1) * M)
                bank, free = banks.take()
                t_a = product(bank[:, 0:S], [((kfh[rows, 0:P], kfl[rows, 0:P]), (qfh[rows, :], qfl[rows, :]))],
                              [*f_ready, *free])
                t_a = product(bank[:, S:S + P], [((kfh[rows, P:S], kfl[rows, P:S]), (qfh[rows, P:S], qfl[rows, P:S]))])
                awm, m_free = awm_t.take()
                (ah, al), a_free = aw_t.take()
                t_m = tt(dve, awm[:, :], bank[:, 0:3 * P], mask_d[:, :], ALU.mult, [t_a, *t_db, *m_free])
                banks.give(bank, [t_m])
                t_h = act_do(ah[:, :], awm[:, :], ACT.Identity, [t_m, *a_free])
                aws.append([(ah, al), awm, t_h])
            feat_t.give(pair_bufs, [t_a])
            yield
            for g, ((ah, al), awm, t_h) in enumerate(aws):
                t_l = tt(pool, al[:, :], awm[:, :], f(ah[:, :]), ALU.subtract, [t_h])
                awm_t.give(awm, [t_h, t_l])
                aws[g] = ((ah, al), [t_h, t_l])
            yield
            for g in range(2):
                h = 2 * j + g
                (ah, al), ready = aws[g]
                weighted_values(st, h, [(0, ah[:, 0:S], al[:, 0:S], slice(0, S)),
                                        (1, ah[:, S:S + P], al[:, S:S + P], slice(P, S))], ready)
                aw_t.give((ah, al), [pe.last()])

        def weighted_values(st, h, parts, ready):
            if h % HPB == 0:
                bank, bank_free = banks.take()
                st["accs"].append((bank, None))
            else:
                (bank, _), bank_free = st["accs"][-1], []
            base = (h // VH % 2) * S
            first_of_tile = h % VH == 0
            last_of_tile = h % VH == VH - 1 or h == NH - 1
            terms = [(t, w, cols) for t, hi, lo, cols in parts for w in (lo, hi)]
            for i, (t, w, cols) in enumerate(terms):
                o = bank[:, base + cols.start:base + cols.stop]
                mm = lambda e, o=o, t=t, w=w, i=i: e.matmul(
                    o, v_heads[:, t, h, :], w, start=(first_of_tile and i == 0),
                    stop=(last_of_tile and i == len(terms) - 1), skip_group_check=True)
                after = [*ready, *st["v_ready"][h // VH], *bank_free] if i == 0 else ()
                if i == len(terms) - 1:
                    pe.do(mm, after)
                else:
                    pe.quiet(mm, after)
            if last_of_tile:
                v_readers[h // VH] = [pe.last()]
                st["accs"][-1] = (bank, pe.last())

        def finish_d(b):
            yield from finish_heads(b, state_d[b], dwo, dbo, [*t_dwo, *t_db])

        per_b = NH // 2
        first_d = 6
        for norm in norms:
            at(0, norm)
        for b in range(B):
            base = first_d + per_b * b
            at(base - 6, prelude_d(b))
            for j in range(per_b):
                at(base + j, pair_d(b, j), -(per_b * b + j))
            for i in range(NVT):
                at(base + min(VH * i + 2, NH - 1) // 2 - 1 if b else base - 1 + i // 3, place(state_d, b, i))
            for i in range(NAB):
                at(base + min(HPB * i + HPB - 1, NH - 1) // 2 + 5, drain(state_d, b, i, DELTA))
            at(base + per_b + 6, finish_d(b), carry=(b == B - 1))
        run()
        dpart.close()
        dw_scope.close()
        t_d = fence()

        epart = ExitStack()
        sbe = lambda name, shape, dt=F32: sb(name, shape, dt, epart)
        NS4 = 4
        eq = [sbe(f"eq_{n}", [P, KC, NS4 * P], F32R) for n in ("hi", "lo")]
        ek = [sbe(f"ek_{n}", [CK, 2, NS4 * P], F32R) for n in ("hi", "lo")]
        ev = [sbe(f"ev_{n}", [CK, 2, D], F32R) for n in ("hi", "lo")]
        eo = [sbe(f"eo_{n}", [P, KC, D], F32R) for n in ("hi", "lo")]
        ebias = sbe("ebias", [P, 2 * NS4])
        ebv, ebo = sbe("ebv", [P, D]), sbe("ebo", [P, D])
        low_rows = sbe("low_rows", [P, 1])
        t_eb = [load("e_b", ebias[:, :], a["E_b"], t_d), load("e_bv", ebv[:, :], a["E_bv"], t_d),
                load("e_bo", ebo[:, :], a["E_bo"], t_d), load("e_m", low_rows[:, :], a["low_rows"], t_d)]
        t_ew = [*weights(split_dve, eq[0][:, :, :], eq[1][:, :, :], a["E_wq"], t_d),
                *weights(split_dve, ek[0][:, :, :], ek[1][:, :, :], a["E_wk"], t_d),
                *weights(split_pool, ev[0][:, :, :], ev[1][:, :, :], a["E_wv"], t_d)]
        t_eo = weights(split_pool, eo[0][:, :, :], eo[1][:, :, :], a["E_wo"], t_d)
        qs_t = Turns([sbe(f"qslots{i}", [P, NS4, S], F32R) for i in range(2)], t_d)
        qm_t = Turns([sbe(f"qmask{i}", [P, 2, S], F32R) for i in range(2)], t_d)
        ks_t = Turns([[sbe(f"kslots_{n}{i}", [P, NS4, S], F32R) for n in ("hi", "lo")] for i in range(2)], t_d)
        se_t = Turns([sbe(f"scoreE{i}", [P, TT, S]) for i in range(2)], t_d)
        pe_t = Turns([sbe(f"probE{i}", [P, TT, S]) for i in range(3)], t_d)
        pte_t = Turns([[sbe(f"probTE_{n}{i}", [P, TT, S], F32R) for n in ("hi", "lo")] for i in range(3)], t_d)
        sme_t = Turns([sbe(f"smallE{i}", [P, 2 * TT]) for i in range(3)], t_d)
        scale_e = float(DH) ** -0.5
        lim = CLAMP / scale_e
        state_e = {}

        def prelude_e(b):
            (cxh, cxl), t_cx = load_context(b)
            qs, q_free = qs_t.take()
            (kh, kl), k_free = ks_t.take()
            ready = []
            yield
            for half in range(2):
                bank, free = banks.take()
                for j in range(2):
                    n = 2 * half + j
                    t_mm = product(bank[:, j * S:(j + 1) * S],
                                   [((eq[0][:, k, n * P:(n + 1) * P], eq[1][:, k, n * P:(n + 1) * P]),
                                     (xt(xt_hi, b, k), xt(xt_lo, b, k))) for k in range(KC)],
                                   [*xt_ready[b], *t_ew, *free])
                (i, full), f_free = staging_t.take()
                full = full[:, 0:2 * S].rearrange("p (j s) -> p j s", j=2)
                for j in range(2):
                    n = 2 * half + j
                    t_f = act_do(full[:, j, :], bank[:, j * S:(j + 1) * S], ACT.Identity, [t_mm, *t_eb, *f_free],
                                 bias=ebias[:, n:n + 1])
                banks.give(bank, [t_f])
                qm, m_free = qm_t.take()
                t_m = ts(pool, qm[:, :, :], full, low_rows[:, 0:1], 1.0, ALU.mult, ALU.mult, after=[t_f, *t_eb, *m_free])
                toks = [tt(pool, qs[:, 2 * half:2 * half + 2, :], full, f(qm[:, :, :]), ALU.subtract, [t_m, *q_free])]
                qm_t.give(qm, toks)
                staging_t.give((i, staging[i]), toks)
                ready += toks
                yield
            t_xt = t_mm
            for half in range(2):
                bank, free = banks.take()
                for j in range(2):
                    n = 2 * half + j
                    t_mm = product(bank[:, j * S:(j + 1) * S],
                                   [((ek[0][:, k, n * P:(n + 1) * P], ek[1][:, k, n * P:(n + 1) * P]),
                                     (cxh[:, k, :], cxl[:, k, :])) for k in range(2)], [*t_cx, *free])
                (i, full), f_free = staging_t.take()
                full = full[:, 0:2 * S].rearrange("p (j s) -> p j s", j=2)
                for j in range(2):
                    n = NS4 + 2 * half + j
                    t_f = act_do(full[:, j, :], bank[:, j * S:(j + 1) * S], ACT.Identity, [t_mm, *t_eb, *f_free],
                                 bias=ebias[:, n:n + 1])
                banks.give(bank, [t_f])
                ns = slice(2 * half, 2 * half + 2)
                toks = split_pool(kh[:, ns, :], kl[:, ns, :], full, [t_f, *k_free])
                staging_t.give((i, staging[i]), toks)
                ready += toks
                yield
            bank, free = banks.take()
            for t in range(TT):
                t_mm = product(bank[:, t * D:(t + 1) * D],
                               [((cxh[:, k, t * P:(t + 1) * P], cxl[:, k, t * P:(t + 1) * P]),
                                 (ev[0][:, k, :], ev[1][:, k, :])) for k in range(2)], free)
            ctx_t.give((cxh, cxl), [t_mm])
            vf, vf_free = vf_t.take()
            for t in range(TT):
                t_vf = tt(dve, vf[:, t, :], bank[:, t * D:(t + 1) * D], ebv[:, :], ALU.add, [t_mm, *t_eb, *vf_free])
            banks.give(bank, [t_vf])
            state_e[b] = dict(q=qs, k=(kh, kl), qk_ready=ready, vf=vf, t_vf=t_vf, xt_last=t_xt,
                           v_ready=[None] * NVT, accs=[])

        def head_e(b, h):
            st = state_e[b]
            rows, n = slice(32 * (h % 4), 32 * (h % 4) + 32), h // 4
            qs, (kh, kl) = st["q"], st["k"]
            bank, free = banks.take()
            for t in range(TT):
                o = bank[:, t * S:(t + 1) * S]
                q = qs[rows, n, t * P:(t + 1) * P]
                t_s = matmuls([(o, q, kl[rows, n, :]), (o, q, kh[rows, n, :])], [*st["qk_ready"], *free])
            if h == NH - 1:
                qs_t.give(qs, [t_s])
                ks_t.give((kh, kl), [t_s])
            sc, sc_free = se_t.take()
            small, sm_free = sme_t.take()
            mx, nmx = small[:, 0:TT], small[:, TT:2 * TT]
            yield
            for t in range(TT):
                t_c = dve.do(lambda e, t=t, bank=bank: e.tensor_scalar(
                    sc[:, t, :], bank[:, t * S:(t + 1) * S], lim, None, ALU.min, ALU.max, accum_out=mx[:, t:t + 1]),
                             [t_s, *sc_free, *sm_free])
            banks.give(bank, [t_c])
            t_nm = ts(dve, nmx, mx, -lim, -scale_e, ALU.max, ALU.mult, after=[t_c])
            t_cl = ts(dve, sc[:, :, :], sc[:, :, :], -lim, None, ALU.max, after=[t_c])
            yield
            pr, p_free = pe_t.take()
            for t in range(TT):
                t_p = act_do(pr[:, t, :], sc[:, t, :], ACT.Exp, [t_nm, t_cl, *p_free], scale=scale_e, bias=nmx[:, t:t + 1])
            se_t.give(sc, [t_p])
            sme_t.give(small, [t_p])
            yield
            yield
            bank, free = banks.take()
            t_t = transposes(bank, [(bank[:, kt * S + t * P:kt * S + (t + 1) * P], pr[:, t, kt * P:(kt + 1) * P])
                                    for kt in range(TT) for t in range(TT)], [t_p, *free])
            pe_t.give(pr, [t_t])
            (ph, pl), pt_free = pte_t.take()
            both = bank[:, :].rearrange("p (k s) -> p k s", k=TT)
            t_hi = act_do(ph[:, :, :], both, ACT.Identity, [t_t, *pt_free])
            yield
            ready = [t_hi, tt(dve, pl[:, :, :], both, f(ph[:, :, :]), ALU.subtract, [t_hi])]
            banks.give(bank, ready)
            yield
            weighted_values(st, h, [(kt, ph[:, kt, :], pl[:, kt, :], slice(0, S)) for kt in range(TT)], ready)
            pte_t.give((ph, pl), [pe.last()])

        xtf_t = Turns([sbe(f"xtf{i}", [P, KC, S]) for i in range(1)], t_d)
        rt_t = Turns([sbe(f"route{i}", [P, TT, 13, NE]) for i in range(2)], t_d)
        ridx_t = Turns([(sbe(f"ridx{i}", [P, TT, NE], U32), sbe(f"slot{i}", [P, TT, TOPK], U32)) for i in range(2)],
                       t_d)
        t_seen = [t_rt[-1]]
        both_t = [sbe(f"both{i}", [P, TT, NE], F32R) for i in range(2)]
        t_codes, t_rows = [], []

        def route(b):
            eng = dve if b == B - 1 else pool
            t_store = sp.do(lambda e: e.dma_start(
                x_rows[b * S:(b + 1) * S, :].rearrange("(t p) d -> p t d", p=P), x_tok[:, b * TT:(b + 1) * TT, :]),
                [*x_ready[b], *t_rows[-2:-1]], signal_for(f"x_rows{b % 2}"))
            t_rows.append(t_store)
            xtf, x_free = xtf_t.take()
            t_x = tt(pool, xtf[:, :, :], f(xt_hi[:, :, b * S:(b + 1) * S]), f(xt_lo[:, :, b * S:(b + 1) * S]), ALU.add,
                     [*xt_ready[b], *x_free])
            yield
            bank, free = banks.take()
            for t in range(TT):
                t_l = matmuls([(bank[:, t * NE:(t + 1) * NE], xtf[:, k, t * P:(t + 1) * P], gw_raw[:, k, :])
                               for k in range(KC)], [t_x, *t_rt, *free])
            xtf_t.give(xtf, [t_l])
            rt, rt_free = rt_t.take()
            (ridx, slot), ri_free = ridx_t.take()
            lg, ex, top = rt[:, :, 0, :], rt[:, :, 1, :], rt[:, :, 2, :]
            oh, ohr = rt[:, :, 3:5, :], rt[:, :, 9:11, :]
            small, idf = rt[:, :, 5, :], rt[:, :, 6, :]
            rank, both_r = rt[:, :, 11, :], both_t[b % 2]
            t_c = copy(dve, lg, bank[:, 0:TT * NE].rearrange("p (t e) -> p t e", t=TT), [t_l, *rt_free, *ri_free])
            banks.give(bank, [t_c])
            t_m = dve.do(lambda e: e.tensor_reduce(small[:, :, 0], lg, AX.X, ALU.max, negate=True), [t_c])
            for t in range(TT):
                t_e = act_do(ex[:, t, :], lg[:, t, :], ACT.Exp, [t_m], bias=small[:, t, 0:1],
                             accum_out=small[:, t, 1:2])
            yield
            t_r = dve.do(lambda e: e.reciprocal(small[:, :, 2], small[:, :, 1]), [t_e])
            for t in range(TT):
                t_g = ts(dve, ex[:, t, :], ex[:, t, :], small[:, t, 2:3], None, ALU.mult, after=[t_r])
            for t in range(TT):
                t_t = dve.do(lambda e, t=t: e.max(top[:, t, :], ex[:, t, :]), [t_g])
            for t in range(TT):
                t_i = dve.do(lambda e, t=t: e.max_index(ridx[:, t, :], top[:, t, :], ex[:, t, :]), [t_t])
            t_f = copy(dve, idf, ridx[:, :, :], [t_i])
            for t in range(TT):
                for j in range(TOPK):
                    t_o = ts(eng, oh[:, t, j, :], iota8[:, :], idf[:, t, j:j + 1], None, ALU.is_equal,
                             after=[t_f, *t_rt])
            t_b = tt(eng, both_r[:, :, :], oh[:, :, 0, :], oh[:, :, 1, :], ALU.add, [t_o])
            t_s = tt(dve, small[:, :, 3], top[:, :, 0], top[:, :, 1], ALU.add, [t_t])
            t_s = dve.do(lambda e: e.reciprocal(small[:, :, 3], small[:, :, 3]), [t_s])
            for t in range(TT):
                t_s2 = ts(eng, shares[:, b * TT + t, :], top[:, t, 0:TOPK], small[:, t, 3:4], 1.0, ALU.mult, ALU.mult,
                          after=[t_s])
            yield
            yield
            bank, free = banks.take()
            for t in range(TT):
                terms = [(bank[:, t * NE:(t + 1) * NE], before[:, :], both_r[:, t, :]),
                         (bank[:, t * NE:(t + 1) * NE], ones_r[:, :], seen[:, :])]
                terms += [(bank[:, t * NE:(t + 1) * NE], ones_r[:, :], both_r[:, u, :]) for u in range(t)]
                t_k = matmuls(terms, [t_b, *t_seen, *free])
            t_sn = [t_k]
            for t in range(TT):
                t_sn = [tt(eng, seen[:, :], f(seen[:, :]), f(both_r[:, t, :]), ALU.add, [t_b, *t_sn, *t_seen])]
            t_seen[:] = t_sn
            for j in range(TOPK):
                t_p = tt(dve, ohr[:, :, j, :], oh[:, :, j, :], bank[:, 0:TT * NE].rearrange("p (t e) -> p t e", t=TT),
                         ALU.mult, [t_k])
            banks.give(bank, [t_p])
            t_p = dve.do(lambda e: e.tensor_reduce(rank[:, :, 0:TOPK], ohr, AX.X, ALU.add), [t_p])
            t_p = stt(slot[:, :, :], idf[:, :, 0:TOPK], float(B * S), rank[:, :, 0:TOPK], ALU.mult, ALU.add, [t_p, t_f])
            for t in range(TT):
                for j in range(TOPK):
                    t_sc = pool.do(lambda e, t=t, j=j: e.indirect_dma_start(
                        slot_codes, bass.IndirectOffsetOnAxis(ap=slot[:, t, j:j + 1], axis=0),
                        codes[:, b * TT + t, j:j + 1], None), [t_p, *t_empty, *t_rt], signal_for(f"codes{b % 2}"))
            ridx_t.give((ridx, slot), [t_sc])
            rt_t.give(rt, [t_p, *t_seen, t_s2])
            t_codes.append(t_sc)

        def finish_e(b):
            yield from finish_heads(b, state_e[b], eo, ebo, [*t_eo, *t_eb], route)

        first_e = 10
        for b in range(B):
            base = first_e + NH * b
            at(base - 10, prelude_e(b), 1)
            for h in range(NH):
                at(base + h, head_e(b, h))
            for i in range(NVT):
                at(base + min(VH * i + 2, NH - 1) - 5, place(state_e, b, i), 1)
            for i in range(NAB):
                at(base + min(HPB * i + HPB - 1, NH - 1) + 7, drain(state_e, b, i, 0.0), 1)
            at(base + NH + 8, finish_e(b), 1)
        run()
        epart.close()
        part.close()
        mid.close()
        t_e = fence()

        fpart = ExitStack()
        sbf = lambda name, shape, dt=F32: sb(name, shape, dt, fpart, "right")
        BR = BT // P
        PAIR = 2
        NQ = FC // PAIR
        AHEAD = 2
        W1C, W2C = KC * HID + FC, FC * D + D
        w1r_t = Turns([(i, sbf(f"w1raw{i}", [P, W1C])) for i in range(4)], t_e)
        w2r_t = Turns([(i, sbf(f"w2raw{i}", [P, W2C])) for i in range(4)], t_e)
        w1_t = Turns([[sbf(f"w1_{n}{i}", [P, KC, PAIR * P], F32R) for n in ("hi", "lo")] for i in range(4)], t_e)
        w2_t = Turns([[sbf(f"w2_{n}{i}", [P, PAIR, D], F32R) for n in ("hi", "lo")] for i in range(6)], t_e)
        xg_t = Turns([(i, sbf(f"xg{i}", [P, BR, D])) for i in range(4)], t_e)
        xg_split_t = Turns([[sbf(f"xgT_{n}{i}", [P, KC, BT], F32R) for n in ("hi", "lo")] for i in range(2)], t_e)
        gf_t = Turns([sbf(f"gf{i}", [P, PAIR * BT]) for i in range(2)], t_e)
        gh_t = Turns([[sbf(f"gh_{n}{i}", [P, PAIR, BT], F32R) for n in ("hi", "lo")] for i in range(4)], t_e)
        ysb_t = Turns([(i, sbf(f"yblock{i}", [P, BR, D])) for i in range(3)], t_e)
        counts = sbf("counts", [P, NE])
        ends = sbf("ends", [P, NE])
        past = sbf("past", [P, NE])
        expert_of = sbf("expert_of", [P, NBK])
        row_stats = sbf("row_stats", [P, 4])
        row_i = sbf("row_i", [P, 1], U32)
        wrow_i = sbf("wrow_i", [P, NBK], U32)
        block_codes = sbf("block_codes", [NBK, BT], U32)
        block_codes_f = sbf("block_codes_f", [NBK, BT])
        code_f = sbf("code_f", [P, BR * NBK])
        token_f = sbf("token_f", [P, BR * NBK])
        slot_i = sbf("slot_i", [P, BR * NBK], U32)
        token_i = sbf("token_i", [P, BR * NBK], U32)

        def gather(name, dst, rows, index, after):
            if name not in loads:
                loads[name] = [sem(f"l_{name}"), 0]
            loads[name][1] += 16
            return pool.do(lambda e: e.indirect_dma_start(
                dst, None, rows, bass.IndirectOffsetOnAxis(ap=index, axis=0)), after, (loads[name][0], 16, loads[name][1]))

        bank, free = banks.take()
        t_n = matmuls([(bank[:, 0:NE], ones_r[:, :], seen[:, :])], [*t_seen, *free])
        t_n = copy(dve, counts[:, :], bank[:, 0:NE], [t_n, *t_e])
        banks.give(bank, [t_n])
        t_n = ts(dve, ends[:, :], counts[:, :], 0.0, None, ALU.is_gt, after=[t_n])
        for i in range(1, XPB):
            t_n = stt(ends[:, :], counts[:, :], float(i * BT), ends[:, :], ALU.is_gt, ALU.add, [t_n])
        for i in range(1, NE):
            t_n = tt(dve, ends[:, i:i + 1], ends[:, i:i + 1], ends[:, i - 1:i], ALU.add, [t_n])
        t_p = ts(dve, past[:, :], ends[:, :], row_no[:, 0:1], None, ALU.is_le, after=[t_n])
        t_p = dve.do(lambda e: e.tensor_reduce(row_stats[:, 0:1], past[:, :], AX.X, ALU.add), [t_p])
        t_p = tt(dve, past[:, :], past[:, :], ends[:, :], ALU.mult, [t_p])
        t_p = dve.do(lambda e: e.tensor_reduce(row_stats[:, 1:2], past[:, :], AX.X, ALU.max), [t_p])
        t_p = stt(row_stats[:, 2:3], row_stats[:, 0:1], float(XPB), row_no[:, :], ALU.mult, ALU.add, [t_p])
        t_p = tt(dve, row_stats[:, 2:3], row_stats[:, 2:3], row_stats[:, 1:2], ALU.subtract, [t_p])
        t_p = ts(dve, row_i[:, :], row_stats[:, 2:3], float(NE * XPB), None, ALU.min, after=[t_p])
        t_bc = gather("block_codes", block_codes[:, :], slot_codes.rearrange("(r s) one -> r (s one)", s=BT),
                      row_i[0:NBK, 0:1], [t_p, *t_codes])
        t_w = ts(dve, expert_of[:, :], block_no[:, :], ends[:, 0:1], None, ALU.is_ge, after=[t_n])
        for i in range(1, NE - 1):
            t_w = stt(expert_of[:, :], block_no[:, :], ends[:, i:i + 1], expert_of[:, :], ALU.is_ge, ALU.add, [t_w])
        t_w = ts(dve, wrow_i[:, :], expert_of[:, :], float(P), row_no[:, 0:1], ALU.mult, ALU.add, after=[t_w])
        raws = {}

        def gather_weights(j):
            (i, raw1), free1 = w1r_t.take()
            (i2, raw2), free2 = w2r_t.take()
            t_1 = gather(f"w1raw{i}", raw1[:, :], a["F_w1"], wrow_i[:, j:j + 1], [t_w, *free1])
            t_2 = gather(f"w2raw{i2}", raw2[:, :], a["F_w2"], wrow_i[:, j:j + 1], [t_w, *free2])
            raws[j] = (i, raw1, t_1, i2, raw2, t_2)

        gather_weights(0)
        t_c = copy(dve, block_codes_f[:, :], block_codes[:, :], [t_bc])
        bank, free = banks.take()
        t_t = transposes(bank, [(bank[:, t * NBK:(t + 1) * NBK], block_codes_f[:, t * P:(t + 1) * P])
                                for t in range(BR)], [t_c, *free])
        t_c = copy(dve, code_f[:, :], bank[:, 0:BR * NBK], [t_t])
        banks.give(bank, [t_c])
        t_slot = copy(dve, slot_i[:, :], code_f[:, :], [t_c])
        t_f = ts(dve, token_f[:, :], code_f[:, :], float(B * S), float(-B * S), ALU.is_ge, ALU.mult, after=[t_c])
        t_f = tt(dve, token_f[:, :], token_f[:, :], code_f[:, :], ALU.add, [t_f])
        t_tok = ts(dve, token_i[:, :], token_f[:, :], float(B * S - 1), None, ALU.min, after=[t_f])
        xgs, xgTs, split_ws, ybanks = {}, {}, {}, {}
        t_y_rows = []

        def gather_x(j):
            (i, xg), free = xg_t.take()
            for t in range(BR):
                t_g = gather(f"xg{i}", xg[:, t, :], x_rows, token_i[:, t * NBK + j:t * NBK + j + 1],
                             [t_tok, *t_rows, *free])
            xgs[j] = (i, xg, t_g)

        def block_x(j):
            i, xg, t_g = xgs.pop(j)
            bank, free = banks.take()
            t_tr = transposes(bank, [(bank[:, c * BT + t * P:c * BT + (t + 1) * P], xg[:, t, c * P:(c + 1) * P])
                                     for c in range(KC) for t in range(BR)], [t_g, *free])
            xg_t.give((i, xg), [t_tr])
            (xh, xl), x_free = xg_split_t.take()
            toks = split_bank(xh[:, :, :], xl[:, :, :], bank[:, :].rearrange("p (c t) -> p c t", c=KC),
                              [t_tr, *x_free])
            banks.give(bank, toks)
            xgTs[j] = ((xh, xl), toks)

        def split_w(j, q):
            i, raw1, t_1, i2, raw2, t_2 = raws[j]
            (h1, l1), free1 = w1_t.take()
            (h2, l2), free2 = w2_t.take()
            w1 = raw1[:, 0:KC * HID].rearrange("p (k n) -> p k n", k=KC)[:, :, q * PAIR * P:(q + 1) * PAIR * P]
            w2 = raw2[:, q * PAIR * D:(q + 1) * PAIR * D].rearrange("p (k n) -> p k n", k=PAIR)
            t_h1 = act_do(h1[:, :, :], w1, ACT.Identity, [t_1, *free1])
            t_h2 = act_do(h2[:, :, :], w2, ACT.Identity, [t_2, *free2])
            t_l1 = tt(dve, l1[:, :, :], w1, f(h1[:, :, :]), ALU.subtract, [t_h1, t_1])
            t_l2 = [tt(eng, l2[:, u, :], w2[:, u, :], f(h2[:, u, :]), ALU.subtract, [t_h2, t_2])
                    for u, eng in enumerate((dve, pool))]
            split_ws[(j, q)] = ((h1, l1), [t_h1, t_l1], (h2, l2), [t_h2, *t_l2])

        def block_pair(j, q):
            if q == 2 and j + 3 < NBK:
                gather_weights(j + 3)
                gather_x(j + 3)
            ahead = (j * NQ + q + AHEAD) // NQ, (q + AHEAD) % NQ
            if ahead[0] < NBK:
                split_w(*ahead)
            if q == NQ - 2 and j + 1 < NBK:
                block_x(j + 1)
            (h1, l1), w1_ready, (h2, l2), w2_ready = split_ws.pop((j, q))
            (xh, xl), x_ready_j = xgTs[j]
            i, raw1, _, i2, raw2, _ = raws[j]
            bank, free = banks.take()
            for u in range(PAIR):
                fcols = slice(u * P, (u + 1) * P)
                t_mm = product(bank[:, u * BT:(u + 1) * BT],
                               [((h1[:, k, fcols], l1[:, k, fcols]), (xh[:, k, :], xl[:, k, :])) for k in range(KC)],
                               [*x_ready_j, *w1_ready, *free])
            gf, gf_free = gf_t.take()
            for u in range(PAIR):
                bias = raw1[:, KC * HID + q * PAIR + u:KC * HID + q * PAIR + u + 1]
                t_g = act_do(gf[:, u * BT:(u + 1) * BT], bank[:, u * BT:(u + 1) * BT], ACT.Gelu, [t_mm, *gf_free],
                             bias=bias)
            banks.give(bank, [t_g])
            (gh, gl), g_free = gh_t.take()
            ready = split_dve(gh[:, :, :], gl[:, :, :], gf[:, :].rearrange("p (u s) -> p u s", u=PAIR), [t_g, *g_free])
            gf_t.give(gf, ready)
            w1_t.give((h1, l1), [t_mm])
            last = q == NQ - 1
            if last:
                xg_split_t.give((xh, xl), [t_mm])
                w1r_t.give((i, raw1), [t_g])
            yield
            yield
            if q == 0:
                ybanks[j] = banks.take()
            ybank, free = ybanks[j]
            for u in range(PAIR):
                fc = q * PAIR + u
                for t in range(BR):
                    o = ybank[:, t * D:(t + 1) * D]
                    st = slice(t * P, (t + 1) * P)
                    for n, (hh, ww) in enumerate(((gl, h2), (gh, l2), (gh, h2))):
                        mm = lambda e, o=o, st=st, hh=hh, ww=ww, n=n, t=t, u=u, fc=fc: e.matmul(
                            o, hh[:, u, st], ww[:, u, :], start=(fc == 0 and n == 0 and t == 0),
                            stop=(fc == FC - 1 and n == 2), skip_group_check=True)
                        after = [*ready, *w2_ready, *free] if n == 0 else ()
                        if n == 2 and t == BR - 1 and u == PAIR - 1:
                            t_y = pe.do(mm, after)
                        else:
                            pe.quiet(mm, after)
            gh_t.give((gh, gl), [t_y])
            w2_t.give((h2, l2), [t_y])
            if not last:
                return
            (n, ysb), y_free = ysb_t.take()
            t_s = tt(dve, ysb[:, :, :], ybank[:, :].rearrange("p (t d) -> p t d", t=BR),
                     raw2[:, None, FC * D:W2C].to_broadcast([P, BR, D]), ALU.add, [t_y, *y_free])
            banks.give(ybank, [t_s])
            w2r_t.give((i2, raw2), [*w2_ready, t_s])
            yield
            for t in range(BR):
                t_o = pool.do(lambda e, t=t: e.indirect_dma_start(
                    y_rows, bass.IndirectOffsetOnAxis(ap=slot_i[:, t * NBK + j:t * NBK + j + 1], axis=0),
                    ysb[:, t, :], None, bounds_check=TOPK * B * S - 1, oob_is_err=False),
                    [t_s, t_slot], signal_for(f"y_rows{n}"))
            ysb_t.give((n, ysb), [t_o])
            t_y_rows[:] = [*t_y_rows[-2:], t_o]

        gather_x(0)
        for j in (1, 2):
            gather_weights(j)
            gather_x(j)
        for q in range(AHEAD):
            split_w(0, q)
        block_x(0)
        for j in range(NBK):
            for q in range(NQ):
                at(NQ * j + q, block_pair(j, q))
        run()

        fpart.close()
        t_f = fence()
        cpart = ExitStack()
        ycs = [sb(f"yc{b}", [P, TOPK, TT, D], F32, cpart, "right") for b in range(B)]
        yc_ready = []
        for b in range(B):
            for k in range(TOPK):
                t_l = load(f"yc{b}", ycs[b][:, k, :, :],
                           y_rows.rearrange("(k b t p) d -> k b p t d", k=TOPK, b=B, t=TT)[k, b], [*t_y_rows, *t_f])
            yc_ready.append(t_l)

        def combine(b):
            yc, t_l = ycs[b], yc_ready[b]
            t_sum = [x_ready[b]] * TT
            for k in range(TOPK):
                for t in range(TT):
                    n = b * TT + t
                    t_a = stt(x_tok[:, n, :], yc[:, k, t, :], shares[:, n, k:k + 1], x_tok[:, n, :], ALU.mult, ALU.add,
                              [t_l, *t_sum[t]])
                    t_sum[t] = [t_a]
            yield from layernorm(b, x_tok[:, b * TT:(b + 1) * TT, :], [t_a], [], last=True)
            stored[0] += 16
            sp.do(lambda e: e.dma_start(out[b * TT:(b + 1) * TT].rearrange("t p d -> p t d"),
                                        x_tok[:, b * TT:(b + 1) * TT, :]), x_ready[b], (out_sem, 16, stored[0]))

        stored = [0]
        for b in range(B):
            at(b, combine(b))
        run()

        block = ctx.enter_context(nc.Block())

        @block.tensor
        def _(e):
            pe.play(e)

        @block.scalar
        def _(e):
            act.play(e)

        @block.vector
        def _(e):
            dve.play(e)

        @block.gpsimd
        def _(e):
            pool.play(e)

        @block.sync
        def _(e):
            sp.play(e)
            e.wait_ge(out_sem, stored[0])
            for s, value in dram_sems.values():
                e.wait_ge(s, value)
        cpart.close()


def kernel(**inputs):
    import concourse.bacc as _bacc
    from concourse.bass_utils import run_bass_kernel_spmd as _run

    g = {k: np.asarray(v) for k, v in inputs.items()}

    def rows(w, n=P):
        return w.reshape(w.shape[0] // n, n, *w.shape[1:]).swapaxes(0, 1)

    def cols(v):
        return v.reshape(-1, P).T

    def wide(v):
        return np.broadcast_to(v, (P, v.shape[0]))

    def slots(w):
        w = w.reshape(*w.shape[:-1], NH, 1, DH)
        return np.broadcast_to(w, (*w.shape[:-2], 2, DH)).reshape(*w.shape[:-3], NH * 2 * DH)

    tri = np.tril(np.ones((P, P), np.float32))
    L0, L1 = "L0_", "L1_"
    w12 = np.stack([g[L0 + "ffn_w1_w"].T.reshape(KC, P, 4, 2, P), g[L0 + "ffn_w2_w"].T.reshape(KC, P, 4, 2, P)])
    w12 = w12.transpose(3, 2, 0, 4, 1, 5).reshape(4, P, CW)
    square = [g[L0 + f"ffn_{n}_w"].T.reshape(FC, P, FC, P).transpose(2, 1, 0, 3).reshape(FC, P, CW) for n in ("h1", "h2")]
    w3 = g[L0 + "ffn_w3_w"].T.reshape(2, 4, P, D).transpose(0, 2, 1, 3).reshape(2, P, CW)
    proj = np.zeros((P, NH // 2, 2, M), np.float32)
    for h in range(NH):
        r = h % (P // DH) * DH
        proj[r:r + DH, h // 2, h % 2, :] = g[L1 + "attn_proj"][h]
    laid = {
        "ident": np.eye(P, dtype=np.float32),
        "mask_a": np.concatenate([np.where(tri > 0, 0, MASKED), np.zeros((P, P)), np.where(tri > 0, 0, MASKED)], 1)
        .astype(np.float32),
        "mask_d": np.concatenate([tri.T, np.ones((P, P), np.float32), tri.T], 1),
        "low_rows": (np.arange(P) % 32 >= 16).astype(np.float32)[:, None],
        "iota8": np.broadcast_to(np.arange(NE, dtype=np.float32), (P, NE)),
        "x": rows(g["x"].reshape(B * S, D)),
        "xT": rows(g["x"].reshape(B * S, D).T),
        "ctxT": rows(g["ctx_768"].reshape(B * S, DC).T, CK),
        "A_wqkv": rows(g[L0 + "attn_W_qkv"]),
        "A_b": cols(g[L0 + "attn_b_qkv"]),
        "A_wconv": rows(g[L0 + "attn_W_vconv"]),
        "B_wv": rows(g[L0 + "xattn_Wv"].T),
        "B_wt": rows(g[L0 + "xattn_Wt"].T, CK),
        "B_b": np.stack([g[L0 + "xattn_bv"], g[L0 + "xattn_bt"]], 1),
        "C_w": np.concatenate([w12, *square, w3]),
        "C_s": np.stack([cols(g[L0 + f"ffn_{n}_s"]) for n in ("w1", "w2", "h1", "h2")], 1),
        "C_s3": wide(g[L0 + "ffn_w3_s"]),
        "D_w": rows(g[L1 + "attn_Wqkv"].T),
        "D_b": cols(g[L1 + "attn_bqkv"][:2 * D]),
        "D_bv": wide(g[L1 + "attn_bqkv"][2 * D:]),
        "D_wo": rows(g[L1 + "attn_Wout"].T),
        "D_bo": wide(g[L1 + "attn_bout"]),
        "D_proj": proj.reshape(P, NH // 2, P),
        "E_wq": rows(slots(g[L1 + "xattn_Wq"])),
        "E_wk": rows(slots(g[L1 + "xattn_Wk"]), CK),
        "E_b": np.concatenate([cols(slots(g[L1 + "xattn_bq"])), cols(slots(g[L1 + "xattn_bk"]))], 1),
        "E_wv": rows(g[L1 + "xattn_Wv"], CK),
        "E_bv": wide(g[L1 + "xattn_bv"]),
        "E_wo": rows(g[L1 + "xattn_Wo"]),
        "E_bo": wide(g[L1 + "xattn_bo"]),
        "gate_w": rows(g[L1 + "ffn_gate_w"]),
        "F_w1": np.concatenate([g[L1 + "ffn_w1"].reshape(NE, KC, P, HID).transpose(0, 2, 1, 3).reshape(NE * P, KC * HID),
                                g[L1 + "ffn_b1"].reshape(NE, FC, P).transpose(0, 2, 1).reshape(NE * P, FC)], 1),
        "F_w2": np.concatenate([g[L1 + "ffn_w2"].reshape(NE, FC, P, D).transpose(0, 2, 1, 3).reshape(NE * P, FC * D),
                                np.broadcast_to(g[L1 + "ffn_b2"][:, None, :], (NE, P, D)).reshape(NE * P, D)], 1),
        "before": np.triu(np.ones((P, P), np.float32), 1),
        "codes": np.arange(TOPK * B * S, dtype=np.uint32).reshape(TOPK, NT, P).transpose(2, 1, 0),
        "block_no": np.broadcast_to(np.arange(NBK, dtype=np.float32), (P, NBK)),
        "row_no": np.arange(P, dtype=np.float32)[:, None],
    }
    nc = _bacc.Bacc("TRN2", target_bir_lowering=False, num_devices=1)
    arrays = {f"in_{k}": np.ascontiguousarray(v) for k, v in laid.items()}
    aps = {k: nc.dram_tensor(f"in_{k}", arrays[f"in_{k}"].shape, mybir.dt.from_np(arrays[f"in_{k}"].dtype),
                             kind="ExternalInput").ap() for k in laid}
    out = nc.dram_tensor("out_x", (NT, P, D), F32, kind="ExternalOutput").ap()
    build(nc, aps, out)
    r = _run(nc, [arrays], core_ids=[0])
    return r.results[0]["out_x"].reshape(B, S, D)
```
